# Optimizing a Trainium2 kernel written in Bass

```python
import numpy as np
import jax
import jax.numpy as jnp

def _softmax(x, axis=-1):
    return jax.nn.softmax(x, axis=axis)
def _gelu(x):
    return jax.nn.gelu(x, approximate=True)
def _silu(x):
    return jax.nn.silu(x)
def _sigmoid(x):
    return jax.nn.sigmoid(x)
def _layernorm(x, axis=-1, eps=1e-5):
    m = jnp.mean(x, axis=axis, keepdims=True)
    v = jnp.var(x, axis=axis, keepdims=True)
    return (x - m) / jnp.sqrt(v + eps)
def _scatter_add(tgt, idx, src, axis=0):
    return tgt.at[idx].add(src)
def _segment_sum(src, seg, n):
    return jax.ops.segment_sum(src, seg, n)

kernel_name = 'mk_conv_seq_d2_conv_nchw192_208360'

def setup_inputs(seed: int = 0):
    np.random.seed(seed)
    _w = jnp.asarray
    def _rec_inputs():
        import jax
        import jax.numpy as jnp
        _gk = jax.random.key(seed)
        x = -0.0001538 + 1 * jax.random.normal(jax.random.fold_in(_gk, 1), (8, 192, 64, 64), jnp.float32)
        return x
    x = _rec_inputs()
    def _L0_conv_setup():
        import jax, jax.numpy as jnp
        import numpy as np
        CHUNK = 8

        def conv1x1(x, w):
            return jnp.einsum('bchw,oc->bohw', x, w)

        def layernorm2d(x, w, b, eps=1e-05):
            mu = x.mean(axis=1, keepdims=True)
            var = ((x - mu) ** 2).mean(axis=1, keepdims=True)
            return (x - mu) / jnp.sqrt(var + eps) * w[None, :, None, None] + b[None, :, None, None]

        def grn(x, gamma, beta, eps=1e-06):
            Gx = jnp.sqrt(jnp.sum(x * x, axis=(2, 3), keepdims=True))
            Nx = Gx / (Gx.mean(axis=1, keepdims=True) + eps)
            return gamma[None, :, None, None] * (x * Nx) + beta[None, :, None, None] + x

        def normalize_w(Gl, Gm, Gr, eps=1e-07):
            s = jnp.abs(Gl) + jnp.abs(Gm) + jnp.abs(Gr) + eps
            return (Gl / s, Gm / s, Gr / s)

        def gate_scan(X, L, Gl, Gm, Gr, chunk):
            B, C, H, W = X.shape
            nc = W // chunk

            def prep(a):
                return a.reshape(B, C, H, nc, chunk).transpose(4, 0, 1, 2, 3)
            xs, ls, gls, gms, grs = map(prep, (X, L, Gl, Gm, Gr))
            h0 = jnp.zeros((B, C, H, nc), X.dtype)

            def step(h, inp):
                x, l, gl, gm, gr = inp
                z = jnp.zeros_like(h[:, :, :1])
                h_up = jnp.concatenate([z, h[:, :, :-1]], axis=2)
                h_dn = jnp.concatenate([h[:, :, 1:], z], axis=2)
                hn = l * x + gl * h_up + gm * h + gr * h_dn
                return (hn, hn)
            _, hs = jax.lax.scan(step, h0, (xs, ls, gls, gms, grs))
            return hs.transpose(1, 2, 3, 4, 0).reshape(B, C, H, W)

        def ss2d_forward(x, W_in, W_dw, b_dw, W_xd, W_w, W_l, W_u, W_d, w_m, grn_gamma, grn_beta, ln_w, ln_b, W_out):
            B, _, H, W = x.shape
            Din = W_in.shape[0]
            x = conv1x1(x, W_in)
            x = jax.lax.conv_general_dilated(x, W_dw, (1, 1), 'SAME', feature_group_count=Din, dimension_numbers=('NCHW', 'OIHW', 'NCHW'))
            x = x + b_dw[None, :, None, None]
            x_proxy = conv1x1(x, W_xd)
            ws = conv1x1(x_proxy, W_w)
            Ls = conv1x1(x_proxy, W_l)
            Us = conv1x1(x_proxy, W_u)
            Ds = conv1x1(x_proxy, W_d)
            x_t = x.transpose(0, 1, 3, 2)
            x_hwwh = jnp.stack([x, x_t], axis=1)
            xs = jnp.concatenate([x_hwwh, jnp.flip(x_hwwh, axis=-1)], axis=1)
            xs = xs.reshape(B, 4 * Din, H, W)
            nd = 4 * Din
            Gl, Gm, Gr = (ws[:, :nd], ws[:, nd:2 * nd], ws[:, 2 * nd:])
            Gl, Gm, Gr = normalize_w(Gl, Gm, Gr)
            out = gate_scan(xs, Ls, Gl, Gm, Gr, CHUNK)
            out = out * Us + xs * Ds
            out_y = out.reshape(B, 4, Din, H, W)
            y = jnp.einsum('bdchw,d->bchw', out_y, w_m)
            y = layernorm2d(y, ln_w, ln_b)
            y = grn(y, grn_gamma, grn_beta)
            return conv1x1(y, W_out)
        key = jax.random.key(seed)
        ks = jax.random.split(key, 16)
        B, d_model, H, W = (8, 192, 64, 64)
        d_inner, d_state, nd = (384, 16, 4)

        def w(k, shape, fan_in):
            return jax.random.normal(k, shape, jnp.float32) / np.sqrt(fan_in)
        return {'x': jax.random.normal(ks[0], (B, d_model, H, W), jnp.float32), 'W_in': w(ks[1], (d_inner, d_model), d_model), 'W_dw': w(ks[2], (d_inner, 1, 3, 3), 9), 'b_dw': jnp.zeros((d_inner,), jnp.float32), 'W_xd': w(ks[3], (d_state, d_inner), d_inner), 'W_w': w(ks[4], (12 * d_inner, d_state), d_state), 'W_l': w(ks[5], (nd * d_inner, d_state), d_state), 'W_u': w(ks[6], (nd * d_inner, d_state), d_state), 'W_d': w(ks[7], (nd * d_inner, d_state), d_state), 'w_m': w(ks[8], (nd,), nd), 'grn_gamma': 0.1 * jax.random.normal(ks[9], (d_inner,), jnp.float32), 'grn_beta': 0.1 * jax.random.normal(ks[10], (d_inner,), jnp.float32), 'ln_w': jnp.ones((d_inner,), jnp.float32), 'ln_b': jnp.zeros((d_inner,), jnp.float32), 'W_out': w(ks[11], (d_model, d_inner), d_inner)}
    _L0_conv_all = _L0_conv_setup()
    _L0_conv_in = {k: v for k, v in _L0_conv_all.items() if k in ('W_in', 'W_dw', 'b_dw', 'W_xd', 'W_w', 'W_l', 'W_u', 'W_d', 'w_m', 'grn_gamma', 'grn_beta', 'ln_w', 'ln_b', 'W_out', )}
    del _L0_conv_all

    def _L1_conv_setup():
        import jax, jax.numpy as jnp
        import numpy as np
        D_MODEL = 192
        D_INNER = 2 * D_MODEL
        D_STATE = 16
        D_CONV = 4
        DT_RANK = (D_MODEL + 15) // 16
        LN_EPS = 1e-05

        def _mamba_params(key):
            ks = jax.random.split(key, 8)
            s = 0.02
            in_w = jax.random.normal(ks[0], (2 * D_INNER, D_MODEL), jnp.float32) * s
            conv_w = jax.random.normal(ks[1], (D_INNER, D_CONV), jnp.float32) * 0.2
            conv_b = jnp.zeros((D_INNER,), jnp.float32)
            x_w = jax.random.normal(ks[2], (DT_RANK + 2 * D_STATE, D_INNER), jnp.float32) * s
            dt_w = jax.random.normal(ks[3], (D_INNER, DT_RANK), jnp.float32) * DT_RANK ** (-0.5)
            dt_b = jnp.log(jnp.expm1(jax.random.uniform(ks[4], (D_INNER,), jnp.float32, 0.001, 0.1)))
            A_log = jnp.log(jnp.tile(jnp.arange(1, D_STATE + 1, dtype=jnp.float32), (D_INNER, 1)))
            D = jnp.ones((D_INNER,), jnp.float32)
            out_w = jax.random.normal(ks[5], (D_MODEL, D_INNER), jnp.float32) * s
            return (in_w, conv_w, conv_b, x_w, dt_w, dt_b, A_log, D, out_w)

        def _layernorm(x, g, b):
            mu = jnp.mean(x, axis=-1, keepdims=True)
            var = jnp.mean(jnp.square(x - mu), axis=-1, keepdims=True)
            return (x - mu) * jax.lax.rsqrt(var + LN_EPS) * g + b

        def _mamba(x, in_w, conv_w, conv_b, x_w, dt_w, dt_b, A_log, D, out_w):
            b, L, _ = x.shape
            xz = x @ in_w.T
            xc, z = jnp.split(xz, 2, axis=-1)
            xp = jnp.pad(xc, ((0, 0), (D_CONV - 1, 0), (0, 0)))
            xc = sum((xp[:, k:k + L, :] * conv_w[:, k] for k in range(D_CONV))) + conv_b
            xc = jax.nn.silu(xc)
            dbl = xc @ x_w.T
            dt = dbl[..., :DT_RANK]
            B = dbl[..., DT_RANK:DT_RANK + D_STATE]
            C = dbl[..., DT_RANK + D_STATE:]
            dt = jax.nn.softplus(dt @ dt_w.T + dt_b)
            A = -jnp.exp(A_log)

            def step(h, inp):
                dt_t, B_t, C_t, x_t = inp
                dA = jnp.exp(dt_t[..., None] * A)
                h = dA * h + (dt_t * x_t)[..., None] * B_t[:, None, :]
                y = jnp.einsum('bdn,bn->bd', h, C_t)
                return (h, y)
            h0 = jnp.zeros((b, D_INNER, D_STATE), x.dtype)
            seq = (dt.transpose(1, 0, 2), B.transpose(1, 0, 2), C.transpose(1, 0, 2), xc.transpose(1, 0, 2))
            _, ys = jax.lax.scan(step, h0, seq)
            y = ys.transpose(1, 0, 2) + D * xc
            y = y * jax.nn.silu(z)
            return y @ out_w.T
        key = jax.random.key(seed)
        kx, k1, k2 = jax.random.split(key, 3)
        b, c, w, h = (4, 192, 64, 64)
        inp = {'x': jax.random.normal(kx, (b, c, w, h), jnp.float32), 'ln_g': jnp.ones((c,), jnp.float32), 'ln_b': jnp.zeros((c,), jnp.float32)}
        names = ['in_w', 'conv_w', 'conv_b', 'x_w', 'dt_w', 'dt_b', 'A_log', 'D', 'out_w']
        for pref, k in (('m1_', k1), ('m2_', k2)):
            for n, v in zip(names, _mamba_params(k)):
                inp[pref + n] = v
        return inp
    _L1_conv_all = _L1_conv_setup()
    _L1_conv_in = {k: v for k, v in _L1_conv_all.items() if k in ('ln_g', 'ln_b', 'm1_in_w', 'm1_conv_w', 'm1_conv_b', 'm1_x_w', 'm1_dt_w', 'm1_dt_b', 'm1_A_log', 'm1_D', 'm1_out_w', 'm2_in_w', 'm2_conv_w', 'm2_conv_b', 'm2_x_w', 'm2_dt_w', 'm2_dt_b', 'm2_A_log', 'm2_D', 'm2_out_w', )}
    del _L1_conv_all

    return {
        "x": x,
        "L0_conv_W_in": _L0_conv_in["W_in"],
        "L0_conv_W_dw": _L0_conv_in["W_dw"],
        "L0_conv_b_dw": _L0_conv_in["b_dw"],
        "L0_conv_W_xd": _L0_conv_in["W_xd"],
        "L0_conv_W_w": _L0_conv_in["W_w"],
        "L0_conv_W_l": _L0_conv_in["W_l"],
        "L0_conv_W_u": _L0_conv_in["W_u"],
        "L0_conv_W_d": _L0_conv_in["W_d"],
        "L0_conv_w_m": _L0_conv_in["w_m"],
        "L0_conv_grn_gamma": _L0_conv_in["grn_gamma"],
        "L0_conv_grn_beta": _L0_conv_in["grn_beta"],
        "L0_conv_ln_w": _L0_conv_in["ln_w"],
        "L0_conv_ln_b": _L0_conv_in["ln_b"],
        "L0_conv_W_out": _L0_conv_in["W_out"],
        "L1_conv_ln_g": _L1_conv_in["ln_g"],
        "L1_conv_ln_b": _L1_conv_in["ln_b"],
        "L1_conv_m1_in_w": _L1_conv_in["m1_in_w"],
        "L1_conv_m1_conv_w": _L1_conv_in["m1_conv_w"],
        "L1_conv_m1_conv_b": _L1_conv_in["m1_conv_b"],
        "L1_conv_m1_x_w": _L1_conv_in["m1_x_w"],
        "L1_conv_m1_dt_w": _L1_conv_in["m1_dt_w"],
        "L1_conv_m1_dt_b": _L1_conv_in["m1_dt_b"],
        "L1_conv_m1_A_log": _L1_conv_in["m1_A_log"],
        "L1_conv_m1_D": _L1_conv_in["m1_D"],
        "L1_conv_m1_out_w": _L1_conv_in["m1_out_w"],
        "L1_conv_m2_in_w": _L1_conv_in["m2_in_w"],
        "L1_conv_m2_conv_w": _L1_conv_in["m2_conv_w"],
        "L1_conv_m2_conv_b": _L1_conv_in["m2_conv_b"],
        "L1_conv_m2_x_w": _L1_conv_in["m2_x_w"],
        "L1_conv_m2_dt_w": _L1_conv_in["m2_dt_w"],
        "L1_conv_m2_dt_b": _L1_conv_in["m2_dt_b"],
        "L1_conv_m2_A_log": _L1_conv_in["m2_A_log"],
        "L1_conv_m2_D": _L1_conv_in["m2_D"],
        "L1_conv_m2_out_w": _L1_conv_in["m2_out_w"],
    }

def reference(x, L0_conv_W_in, L0_conv_W_dw, L0_conv_b_dw, L0_conv_W_xd, L0_conv_W_w, L0_conv_W_l, L0_conv_W_u, L0_conv_W_d, L0_conv_w_m, L0_conv_grn_gamma, L0_conv_grn_beta, L0_conv_ln_w, L0_conv_ln_b, L0_conv_W_out, L1_conv_ln_g, L1_conv_ln_b, L1_conv_m1_in_w, L1_conv_m1_conv_w, L1_conv_m1_conv_b, L1_conv_m1_x_w, L1_conv_m1_dt_w, L1_conv_m1_dt_b, L1_conv_m1_A_log, L1_conv_m1_D, L1_conv_m1_out_w, L1_conv_m2_in_w, L1_conv_m2_conv_w, L1_conv_m2_conv_b, L1_conv_m2_x_w, L1_conv_m2_dt_w, L1_conv_m2_dt_b, L1_conv_m2_A_log, L1_conv_m2_D, L1_conv_m2_out_w):
    import jax
    import jax.numpy as jnp
    def _L0_conv_ref(x, W_in, W_dw, b_dw, W_xd, W_w, W_l, W_u, W_d, w_m, grn_gamma, grn_beta, ln_w, ln_b, W_out):
        import jax, jax.numpy as jnp
        import numpy as np
        CHUNK = 8

        def conv1x1(x, w):
            return jnp.einsum('bchw,oc->bohw', x, w)

        def layernorm2d(x, w, b, eps=1e-05):
            mu = x.mean(axis=1, keepdims=True)
            var = ((x - mu) ** 2).mean(axis=1, keepdims=True)
            return (x - mu) / jnp.sqrt(var + eps) * w[None, :, None, None] + b[None, :, None, None]

        def grn(x, gamma, beta, eps=1e-06):
            Gx = jnp.sqrt(jnp.sum(x * x, axis=(2, 3), keepdims=True))
            Nx = Gx / (Gx.mean(axis=1, keepdims=True) + eps)
            return gamma[None, :, None, None] * (x * Nx) + beta[None, :, None, None] + x

        def normalize_w(Gl, Gm, Gr, eps=1e-07):
            s = jnp.abs(Gl) + jnp.abs(Gm) + jnp.abs(Gr) + eps
            return (Gl / s, Gm / s, Gr / s)

        def gate_scan(X, L, Gl, Gm, Gr, chunk):
            B, C, H, W = X.shape
            nc = W // chunk

            def prep(a):
                return a.reshape(B, C, H, nc, chunk).transpose(4, 0, 1, 2, 3)
            xs, ls, gls, gms, grs = map(prep, (X, L, Gl, Gm, Gr))
            h0 = jnp.zeros((B, C, H, nc), X.dtype)

            def step(h, inp):
                x, l, gl, gm, gr = inp
                z = jnp.zeros_like(h[:, :, :1])
                h_up = jnp.concatenate([z, h[:, :, :-1]], axis=2)
                h_dn = jnp.concatenate([h[:, :, 1:], z], axis=2)
                hn = l * x + gl * h_up + gm * h + gr * h_dn
                return (hn, hn)
            _, hs = jax.lax.scan(step, h0, (xs, ls, gls, gms, grs))
            return hs.transpose(1, 2, 3, 4, 0).reshape(B, C, H, W)

        def ss2d_forward(x, W_in, W_dw, b_dw, W_xd, W_w, W_l, W_u, W_d, w_m, grn_gamma, grn_beta, ln_w, ln_b, W_out):
            B, _, H, W = x.shape
            Din = W_in.shape[0]
            x = conv1x1(x, W_in)
            x = jax.lax.conv_general_dilated(x, W_dw, (1, 1), 'SAME', feature_group_count=Din, dimension_numbers=('NCHW', 'OIHW', 'NCHW'))
            x = x + b_dw[None, :, None, None]
            x_proxy = conv1x1(x, W_xd)
            ws = conv1x1(x_proxy, W_w)
            Ls = conv1x1(x_proxy, W_l)
            Us = conv1x1(x_proxy, W_u)
            Ds = conv1x1(x_proxy, W_d)
            x_t = x.transpose(0, 1, 3, 2)
            x_hwwh = jnp.stack([x, x_t], axis=1)
            xs = jnp.concatenate([x_hwwh, jnp.flip(x_hwwh, axis=-1)], axis=1)
            xs = xs.reshape(B, 4 * Din, H, W)
            nd = 4 * Din
            Gl, Gm, Gr = (ws[:, :nd], ws[:, nd:2 * nd], ws[:, 2 * nd:])
            Gl, Gm, Gr = normalize_w(Gl, Gm, Gr)
            out = gate_scan(xs, Ls, Gl, Gm, Gr, CHUNK)
            out = out * Us + xs * Ds
            out_y = out.reshape(B, 4, Din, H, W)
            y = jnp.einsum('bdchw,d->bchw', out_y, w_m)
            y = layernorm2d(y, ln_w, ln_b)
            y = grn(y, grn_gamma, grn_beta)
            return conv1x1(y, W_out)
        return ss2d_forward(x, W_in, W_dw, b_dw, W_xd, W_w, W_l, W_u, W_d, w_m, grn_gamma, grn_beta, ln_w, ln_b, W_out)

    def _L1_conv_ref(x, ln_g, ln_b, m1_in_w, m1_conv_w, m1_conv_b, m1_x_w, m1_dt_w, m1_dt_b, m1_A_log, m1_D, m1_out_w, m2_in_w, m2_conv_w, m2_conv_b, m2_x_w, m2_dt_w, m2_dt_b, m2_A_log, m2_D, m2_out_w):
        import jax, jax.numpy as jnp
        import numpy as np
        D_MODEL = 192
        D_INNER = 2 * D_MODEL
        D_STATE = 16
        D_CONV = 4
        DT_RANK = (D_MODEL + 15) // 16
        LN_EPS = 1e-05

        def _mamba_params(key):
            ks = jax.random.split(key, 8)
            s = 0.02
            in_w = jax.random.normal(ks[0], (2 * D_INNER, D_MODEL), jnp.float32) * s
            conv_w = jax.random.normal(ks[1], (D_INNER, D_CONV), jnp.float32) * 0.2
            conv_b = jnp.zeros((D_INNER,), jnp.float32)
            x_w = jax.random.normal(ks[2], (DT_RANK + 2 * D_STATE, D_INNER), jnp.float32) * s
            dt_w = jax.random.normal(ks[3], (D_INNER, DT_RANK), jnp.float32) * DT_RANK ** (-0.5)
            dt_b = jnp.log(jnp.expm1(jax.random.uniform(ks[4], (D_INNER,), jnp.float32, 0.001, 0.1)))
            A_log = jnp.log(jnp.tile(jnp.arange(1, D_STATE + 1, dtype=jnp.float32), (D_INNER, 1)))
            D = jnp.ones((D_INNER,), jnp.float32)
            out_w = jax.random.normal(ks[5], (D_MODEL, D_INNER), jnp.float32) * s
            return (in_w, conv_w, conv_b, x_w, dt_w, dt_b, A_log, D, out_w)

        def _layernorm(x, g, b):
            mu = jnp.mean(x, axis=-1, keepdims=True)
            var = jnp.mean(jnp.square(x - mu), axis=-1, keepdims=True)
            return (x - mu) * jax.lax.rsqrt(var + LN_EPS) * g + b

        def _mamba(x, in_w, conv_w, conv_b, x_w, dt_w, dt_b, A_log, D, out_w):
            b, L, _ = x.shape
            xz = x @ in_w.T
            xc, z = jnp.split(xz, 2, axis=-1)
            xp = jnp.pad(xc, ((0, 0), (D_CONV - 1, 0), (0, 0)))
            xc = sum((xp[:, k:k + L, :] * conv_w[:, k] for k in range(D_CONV))) + conv_b
            xc = jax.nn.silu(xc)
            dbl = xc @ x_w.T
            dt = dbl[..., :DT_RANK]
            B = dbl[..., DT_RANK:DT_RANK + D_STATE]
            C = dbl[..., DT_RANK + D_STATE:]
            dt = jax.nn.softplus(dt @ dt_w.T + dt_b)
            A = -jnp.exp(A_log)

            def step(h, inp):
                dt_t, B_t, C_t, x_t = inp
                dA = jnp.exp(dt_t[..., None] * A)
                h = dA * h + (dt_t * x_t)[..., None] * B_t[:, None, :]
                y = jnp.einsum('bdn,bn->bd', h, C_t)
                return (h, y)
            h0 = jnp.zeros((b, D_INNER, D_STATE), x.dtype)
            seq = (dt.transpose(1, 0, 2), B.transpose(1, 0, 2), C.transpose(1, 0, 2), xc.transpose(1, 0, 2))
            _, ys = jax.lax.scan(step, h0, seq)
            y = ys.transpose(1, 0, 2) + D * xc
            y = y * jax.nn.silu(z)
            return y @ out_w.T
        b, c, w, h = x.shape
        xs = _layernorm(x.reshape(b, -1, c), ln_g, ln_b)
        xf = jnp.flip(xs, axis=-1)
        y1 = _mamba(xs, m1_in_w, m1_conv_w, m1_conv_b, m1_x_w, m1_dt_w, m1_dt_b, m1_A_log, m1_D, m1_out_w)
        y2 = _mamba(xf, m2_in_w, m2_conv_w, m2_conv_b, m2_x_w, m2_dt_w, m2_dt_b, m2_A_log, m2_D, m2_out_w)
        out = xs + y1 + y2
        return out.reshape(b, c, w, h)

    def _gn(v, G=32, eps=1e-5):
        B_, C_, H_, W_ = v.shape
        g = v.reshape(B_, G, C_ // G, H_, W_)
        m = jnp.mean(g, axis=(2, 3, 4), keepdims=True)
        s = jnp.var(g, axis=(2, 3, 4), keepdims=True)
        return ((g - m) / jnp.sqrt(s + eps)).reshape(v.shape)

    def _ln_c(v, eps=1e-6):
        m = jnp.mean(v, axis=1, keepdims=True)
        s = jnp.var(v, axis=1, keepdims=True)
        return (v - m) / jnp.sqrt(s + eps)

    def _ln_t(v, eps=1e-5):
        m = jnp.mean(v, axis=-1, keepdims=True)
        s = jnp.var(v, axis=-1, keepdims=True)
        return (v - m) / jnp.sqrt(s + eps)

    def _to_tokens(v):
        B_, C_, H_, W_ = v.shape
        return v.reshape(B_, C_, H_ * W_).transpose(0, 2, 1)
    def _from_tokens(t, like):
        B_, C_, H_, W_ = like.shape
        return t.transpose(0, 2, 1).reshape(B_, C_, H_, W_)

    x = _L0_conv_ref(x, L0_conv_W_in, L0_conv_W_dw, L0_conv_b_dw, L0_conv_W_xd, L0_conv_W_w, L0_conv_W_l, L0_conv_W_u, L0_conv_W_d, L0_conv_w_m, L0_conv_grn_gamma, L0_conv_grn_beta, L0_conv_ln_w, L0_conv_ln_b, L0_conv_W_out)
    x = _L1_conv_ref(x, L1_conv_ln_g, L1_conv_ln_b, L1_conv_m1_in_w, L1_conv_m1_conv_w, L1_conv_m1_conv_b, L1_conv_m1_x_w, L1_conv_m1_dt_w, L1_conv_m1_dt_b, L1_conv_m1_A_log, L1_conv_m1_D, L1_conv_m1_out_w, L1_conv_m2_in_w, L1_conv_m2_conv_w, L1_conv_m2_conv_b, L1_conv_m2_x_w, L1_conv_m2_dt_w, L1_conv_m2_dt_b, L1_conv_m2_A_log, L1_conv_m2_D, L1_conv_m2_out_w)
    return x


_drawn_inputs = setup_inputs


def setup_inputs(seed=0):
    import zlib

    import numpy as np

    out = dict(_drawn_inputs(seed))
    spreads = {'L0_conv_b_dw': (0.0, 0.1),
     'L0_conv_ln_w': (1.0, 0.2),
     'L0_conv_ln_b': (0.0, 0.1),
     'L1_conv_ln_g': (1.0, 0.2),
     'L1_conv_ln_b': (0.0, 0.1),
     'L1_conv_m1_conv_b': (0.0, 0.1),
     'L1_conv_m1_D': (1.0, 0.2),
     'L1_conv_m2_conv_b': (0.0, 0.1),
     'L1_conv_m2_D': (1.0, 0.2)}
    factors = {}
    for name, (base, spread) in spreads.items():
        noise = np.random.default_rng([zlib.crc32(name.encode()), seed]).standard_normal(out[name].shape)
        drawn = base * np.exp(spread * noise) if base else spread * noise
        out[name] = jnp.asarray(drawn.astype(out[name].dtype))
    for name, factor in factors.items():
        out[name] = (out[name] * factor).astype(out[name].dtype)
    return out
```

```python
from contextlib import ExitStack

import concourse.bass as bass
from concourse import mybir
from concourse.alu_op_type import AluOpType as ALU

ACT = mybir.ActivationFunctionType
F32 = mybir.dt.float32
BF16 = mybir.dt.bfloat16
AX_X = mybir.AxisListType.X

P = 128
BANK = 512
CH = 192
DIN = 384
CG = DIN // P
SIDE = 64
PIX = SIDE * SIDE
CHUNK = 8
NDIR = 4
PROXY = 16
NGATE = 6
START = 1
LN0_EPS, GRN_EPS, GATE_EPS, LN1_EPS = 1e-5, 1e-6, 1e-7, 1e-5


def layer0(nc, B, io, mid):
    UNITS = CHUNK * NDIR
    ROWS = BANK // SIDE
    NB = PIX // BANK
    PADW = SIDE + 2

    with ExitStack() as ctx:
        def sb(name, shape, dt=F32):
            return ctx.enter_context(nc.sbuf_tensor(name, shape, dt))

        sems = []

        def sem(name):
            sems.append(ctx.enter_context(nc.semaphore(name)))
            return sems[-1]

        w_in_a = sb("w_in_a", [P, DIN])
        w_in_b = sb("w_in_b", [CH - P, DIN])
        w_dw = sb("w_dw", [P, CG, 9])
        b_dw = sb("b_dw", [P, CG])
        w_proxy = sb("w_proxy", [P, CG, P])
        w_gate = sb("w_gate", [P, CG, NDIR, NGATE, P], BF16)
        w_mix = sb("w_mix", [P, NDIR])
        part_mask = sb("part_mask", [P, 3])
        w_out = sb("w_out", [P, CG, CH])
        vecs = sb("vecs", [P, 4, CG])
        ident = sb("ident", [P, P])
        ones = sb("ones", [P, P])
        epsv = sb("epsv", [P, 2])
        X = sb("X", [P, CG, PIX])
        S = sb("S", [P, CHUNK, BANK], BF16)
        Y = sb("Y", [P, CG, CHUNK, BANK])
        pad = Y[:, :, :, :].rearrange("p a b c -> p (a b c)")[:, 0:2 * PADW * PADW].rearrange(
            "p (n h w) -> p n h w", n=2, h=PADW)
        w_tmp = X[:, :, :].rearrange("p a b -> p (a b)")
        gabs = sb("gabs", [P, 2, 3, BANK])
        lud = sb("lud", [P, 8, BANK])
        s1 = sb("s1", [P, 2, BANK])
        s2 = sb("s2", [P, 2, BANK])
        r0 = sb("r0", [P, 2, BANK])
        prod = sb("prod", [P, 3, BANK])
        total = sb("total", [P, BANK])
        x_a = lud[:, 0:2, :]
        x_b = lud[0:CH - P, 2:4, :]
        w_out_s = prod[:, :, :].rearrange("p a b -> p (a b)")[:, 0:CG * CH].rearrange("p (g m) -> p g m", g=CG)
        LX = sb("LX", [P, 2, BANK])
        DX = sb("DX", [P, 2, BANK])
        UH = sb("UH", [P, 2, BANK])
        HP = BANK + 2 * CHUNK
        H = sb("H", [P, NDIR, 2, HP])
        gacc = sb("gacc", [P, CG, CHUNK])
        gx = sb("gx", [P, 2, CG])
        small = sb("small", [P, 8])
        svec = sb("svec", [P, 3, CG])
        b_out = sb("b_out", [P, 2])

        ps = ctx.enter_context(nc.psum_tensor("ps0", [P, 8, BANK], F32))

        s_w = sem("s_w")
        s_passed = sem("s_passed")
        s_const = sem("s_const")
        s_wsplit = sem("s_wsplit")
        s_x = [sem("s_x0"), sem("s_x1")]
        s_win = sem("s_win")
        s_pad = sem("s_pad")
        s_border = sem("s_border")
        s_conv = sem("s_conv")
        s_prox = sem("s_prox")
        s_hi = sem("s_hi")
        s_res = sem("s_res")
        s_mid = sem("s_mid")
        s_lo = sem("s_lo")
        s_gate = sem("s_gate")
        s_lud = sem("s_lud")
        s_y = sem("s_y")
        s_acc = sem("s_acc")
        s_abs = sem("s_abs")
        s_ludsb = sem("s_ludsb")
        s_ln = sem("s_ln")
        s_r0 = sem("s_r0")
        s_yout = sem("s_yout")
        s_s1 = sem("s_s1")
        s_lx = sem("s_lx")
        s_dx = sem("s_dx")
        s_uh = sem("s_uh")
        s_h0 = sem("s_h0")
        s_s2 = sem("s_s2")
        s_err = sem("s_err")
        s_rec = sem("s_rec")
        s_prod = sem("s_prod")
        s_n1 = sem("s_n1")
        s_n2 = sem("s_n2")
        s_q = sem("s_q")
        s_h = sem("s_h")
        s_mu = sem("s_mu")
        s_cen = sem("s_cen")
        s_sq = sem("s_sq")
        s_var = sem("s_var")
        s_vln = sem("s_vln")
        s_vr0 = sem("s_vr0")
        s_vv = sem("s_vv")
        s_newt = sem("s_newt")
        s_z = sem("s_z")
        s_gsq = sem("s_gsq")
        s_grn = sem("s_grn")
        s_gxr = sem("s_gxr")
        s_gsum = sem("s_gsum")
        s_oproj = sem("s_oproj")
        s_osb = sem("s_osb")
        s_out = [sem("s_out0"), sem("s_out1")]

        def xview(c, t, d):
            img = X[:, c, :]
            if d % 2 == 0:
                v = img.rearrange("p (h k t) -> p h k t", k=CHUNK, t=CHUNK)
            else:
                v = img.rearrange("p (k t h) -> p h k t", k=CHUNK, t=CHUNK)
            return v[:, :, :, t if d < 2 else CHUNK - 1 - t]

        def hk(ap, d):
            v = ap.rearrange("p (h k) -> p h k", k=CHUNK)
            return v if d < 2 else v[:, :, ::-1]

        def opx(q):
            return gabs[:, q, 0, :], gabs[0:CH - P, q, 1, :]

        def prod_sq(t):
            return lud[:, 4 * (t % 2):4 * (t % 2) + 3, :]

        mid_tmp = LX[:, :, :].rearrange("p a b -> p (a b)").bitcast(BF16)[:, 0:BANK]

        NLOADS = 11

        def waits_passed(eng):
            eng.sem_inc(s_passed, 1)

        with nc.Block() as block:
            @block.sync
            def _(sp):
                loads = [
                    (w_in_a[:, :], io["w_in"][0:P, :]), (w_in_b[:, :], io["w_in"][P:CH, :]),
                    (w_dw[:, :, :], io["w_dw"].rearrange("(g p) k -> p g k", p=P)),
                    (b_dw[:, :], io["b_dw"]), (w_proxy[:, :, :], io["w_proxy"].rearrange("(g p) m -> p g m", p=P)),
                    (w_tmp[:, 0:CG * NDIR * NGATE * P], io["w_gate"]),
                    (w_mix[:, :], io["w_mix"]),
                    (part_mask[:, :], io["part_mask"]),
                    (w_out[:, :, :], io["w_out"].rearrange("(g p) m -> p g m", p=P)),
                    (vecs[:, :, :], io["vecs"]),
                    (ident[:, :], io["ident"]),
                ]
                for dst, src in loads:
                    sp.dma_start(dst, src).then_inc(s_w, 16)
                with sp.Fori(0, B) as b:
                    for j in range(NB * CG):
                        if j == 0:
                            sp.wait_ge(s_var, START + b * CHUNK)
                            waits_passed(sp)
                        if j >= 2:
                            sp.wait_ge(s_win, START + b * (NB * CG) + (j - 1))
                        else:
                            sp.wait_ge(s_win, START + b * (NB * CG))
                        px = (j % NB) * BANK
                        sp.dma_start(x_a[:, j % 2, :], io["x"][b, 0:P, px:px + BANK]).then_inc(s_x[j % 2], 16)
                        sp.dma_start(x_b[:, j % 2, :], io["x"][b, P:CH, px:px + BANK]).then_inc(s_x[j % 2], 16)
                    for j in range(NB):
                        sp.wait_ge(s_osb, START + b * (2 * NB) + 2 * j + 2)
                        o_a, o_b = opx(j % 2)
                        sp.dma_start(mid[b, 0:P, j * BANK:(j + 1) * BANK], o_a).then_inc(s_out[j % 2], 16)
                        sp.dma_start(mid[b, P:CH, j * BANK:(j + 1) * BANK], o_b).then_inc(s_out[j % 2], 16)
                for s in s_out:
                    sp.wait_ge(s, START + B * NB * 16)

            @block.gpsimd
            def _(pool):
                for s in sems:
                    pool.sem_inc(s, START)
                pool.memset(ones[:, :], 1.0).then_inc(s_const, 1)
                pool.memset(epsv[:, 0:1], GATE_EPS).then_inc(s_const, 1)
                pool.memset(epsv[:, 1:2], LN0_EPS).then_inc(s_const, 1)
                pool.memset(H[:, :, :, :], 0.0).then_inc(s_const, 1)
                pool.wait_ge(s_const, START + 4)
                pool.wait_ge(s_wsplit, START + 8 * CG)
                with pool.Fori(0, B) as b:
                    pool.wait_ge(s_oproj, START + b * NB)
                    waits_passed(pool)
                    for n in range(2):
                        pool.memset(pad[:, n, 0:PADW:PADW - 1, :], 0.0).then_inc(s_border, 1)
                        pool.memset(pad[:, n, 1:PADW - 1, 0:PADW:PADW - 1], 0.0).then_inc(s_border, 1)
                    with pool.Fori(0, CG) as c:
                        bc = b * CG + c
                        u = bc * UNITS
                        pool.wait_ge(s_h, START + u)
                        pool.wait_ge(s_prod, START + u)
                        pool.wait_ge(s_uh, START + u)
                        waits_passed(pool)
                        pool.memset(H[:, :, 0, CHUNK:CHUNK + BANK], 0.0).then_inc(s_h0, 1)

                        def u_h(k):
                            t, d, q = k // NDIR, k % NDIR, k % 2
                            pool.wait_ge(s_h, START + u + k + 1)
                            if k >= 2:
                                pool.wait_ge(s_acc, START + u + k - 1)
                            else:
                                pool.wait_ge(s_acc, START + u)
                            pool.tensor_tensor(UH[:, q, :], lud[:, 4 + k % 4, :],
                                               H[:, d, (t + 1) % 2, CHUNK:CHUNK + BANK],
                                               ALU.mult).then_inc(s_uh, 1)

                        for k in range(UNITS):
                            t, d, q = k // NDIR, k % NDIR, k % 2
                            pool.wait_ge(s_abs, START + u + k + 1)
                            pool.wait_ge(s_s2, START + (u + k - 1 if k >= 2 else u))
                            pool.tensor_tensor(s1[:, q, :], gabs[:, q, 0, :], gabs[:, q, 1, :],
                                               ALU.add).then_inc(s_s1, 1)
                            pool.wait_ge(s_ludsb, START + 3 * (u + k) + 3)
                            pool.wait_ge(s_h, START + (u + k - 1 if k >= 2 else u))
                            waits_passed(pool)
                            pool.tensor_tensor(hk(LX[:, q, :], d), hk(lud[:, q, :], d), xview(c, t, d),
                                               ALU.mult).then_inc(s_lx, 1)
                            pool.wait_ge(s_acc, START + (u + k - 1 if k >= 2 else u))
                            waits_passed(pool)
                            pool.tensor_tensor(hk(DX[:, q, :], d), hk(lud[:, 2 + q, :], d), xview(c, t, d),
                                               ALU.mult).then_inc(s_dx, 1)
                            if k:
                                u_h(k - 1)
                        u_h(UNITS - 1)
                    for t in range(CHUNK):
                        n = b * (CHUNK * 4) + 4 * t
                        q = t % 2
                        v, r = s1[:, q, :], r0[:, q, :]
                        pool.wait_ge(s_vv, START + b * CHUNK + t + 1)
                        pool.wait_ge(s_vr0, START + b * CHUNK + t + 1)
                        pool.tensor_tensor(v, v, r, ALU.mult).then_inc(s_newt, 1)
                        pool.wait_ge(s_newt, START + n + 1)
                        pool.tensor_tensor(v, v, r, ALU.mult).then_inc(s_newt, 1)
                        pool.wait_ge(s_newt, START + n + 2)
                        waits_passed(pool)
                        pool.tensor_scalar(v, v, -0.5, 1.5, ALU.mult, ALU.add).then_inc(s_newt, 1)
                        pool.wait_ge(s_newt, START + n + 3)
                        pool.tensor_tensor(r, v, r, ALU.mult).then_inc(s_newt, 1)

            @block.tensor
            def _(pe):
                pe.wait_ge(s_w, START + 16 * NLOADS)
                pe.wait_ge(s_const, START + 4)
                with pe.Fori(0, B) as b:
                    for j in range(NB * CG):
                        g, q = j // NB, j % 2
                        pe.wait_ge(s_x[q], START + b * (NB * CG * 16) + 32 * (j // 2 + 1))
                        pe.wait_ge(s_pad, START + (b * (NB * CG) + (j - 1 if j >= 2 else 0)))
                        if j == 0:
                            pe.wait_ge(s_osb, START + b * (2 * NB))
                        pe.matmul(ps[:, q, :], w_in_a[:, g * P:(g + 1) * P], x_a[:, q, :], start=True, stop=False)
                        pe.matmul(ps[:, q, :], w_in_b[:, g * P:(g + 1) * P], x_b[:, q, :],
                                  start=False, stop=True).then_inc(s_win, 1)
                    pe.wait_ge(s_conv, START + (b + 1) * (9 * CG))
                    for t in range(CHUNK):
                        if t >= 2:
                            pe.wait_ge(s_hi, START + b * CHUNK + t - 1)
                            pe.wait_ge(s_res, START + b * CHUNK + t - 1)
                        for g in range(CG):
                            mm = pe.matmul(ps[:, 2 + t % 2, :], w_proxy[:, g, :], xview(g, t, 0),
                                           start=g == 0, stop=g == CG - 1)
                        mm.then_inc(s_prox, 1)
                    pe.wait_ge(s_wsplit, START + 24)
                    pe.wait_ge(s_lo, START + (b + 1) * CHUNK)
                    pe.wait_ge(s_mid, START + (b + 1) * (2 * CHUNK))
                    waits_passed(pe)
                    with pe.Fori(0, CG) as c:
                        bc = b * CG + c
                        u = bc * UNITS

                        def add_y(k, part, done):
                            t, d, q = k // NDIR, k % NDIR, k % 2
                            if part is DX and d == 0:
                                pe.wait_ge(s_yout, START + bc * CHUNK + t)
                            pe.wait_ge(done, START + u + k + 1)
                            return pe.matmul(ps[:, 7, :], ident[:, :], part[:, q, :], start=part is DX and d == 0,
                                             stop=part is UH and d == NDIR - 1)

                        def one_gate(k, n):
                            pe.wait_ge(s_ludsb, START + 3 * (u + k) + n)
                            pe.matmul(ps[:, 6, :], w_gate[:, c, k % NDIR, 3 + n, :], S[:, k // NDIR, :],
                                      start=True, stop=True).then_inc(s_lud, 1)

                        for k in range(UNITS):
                            t, d, q = k // NDIR, k % NDIR, k % 2
                            one_gate(k, 0)
                            pe.wait_ge(s_prod, START + (u + k - 1 if k >= 2 else u))
                            pe.wait_ge(s_abs, START + (u + k - 1 if k >= 2 else u))
                            for n in range(3):
                                mm = pe.matmul(ps[:, 3 * q + n, :], w_gate[:, c, d, n, :], S[:, t, :],
                                               start=True, stop=True)
                            mm.then_inc(s_gate, 1)
                            one_gate(k, 1)
                            if k >= 3:
                                add_y(k - 3, DX, s_dx)
                                add_y(k - 3, UH, s_uh).then_inc(s_acc, 1)
                            one_gate(k, 2)
                        for k in range(UNITS - 3, UNITS):
                            add_y(k, DX, s_dx)
                            add_y(k, UH, s_uh).then_inc(s_acc, 1)
                    pe.wait_ge(s_prod, START + (b + 1) * (CG * UNITS))
                    pe.wait_ge(s_yout, START + (b + 1) * (CG * CHUNK))

                    def var_sum(t):
                        pe.wait_ge(s_sq, START + b * CHUNK + t + 1)
                        if t >= 2:
                            pe.wait_ge(s_vv, START + b * CHUNK + t - 1)
                            pe.wait_ge(s_vln, START + b * CHUNK + t - 1)
                        for g in range(CG):
                            mm = pe.matmul(ps[:, 2 + t % 2, :], ones[:, :], prod_sq(t)[:, g, :],
                                           start=g == 0, stop=g == CG - 1)
                        mm.then_inc(s_var, 1)

                    for t in range(CHUNK):
                        if t >= 2:
                            pe.wait_ge(s_cen, START + b * (CHUNK * CG) + CG * (t - 1))
                        for g in range(CG):
                            mm = pe.matmul(ps[:, t % 2, :], ones[:, :], Y[:, g, t, :],
                                           start=g == 0, stop=g == CG - 1)
                        mm.then_inc(s_mu, 1)
                        if t:
                            var_sum(t - 1)
                    var_sum(CHUNK - 1)
                    pe.wait_ge(s_gxr, START + b + 1)
                    pe.matmul(ps[:, 4, 0:CG], ones[:, :], gx[:, 1, :], start=True, stop=True).then_inc(s_gsum, 1)
                    pe.wait_ge(s_grn, START + b * 12 + 11)
                    for g in range(CG):
                        pe.matmul(ps[:, 5, 0:1], w_out[:, g, 0:P], svec[:, 2, g:g + 1], start=g == 0, stop=g == CG - 1)
                    for g in range(CG):
                        mm = pe.matmul(ps[0:CH - P, 4, 0:1], w_out[:, g, P:CH], svec[:, 2, g:g + 1],
                                       start=g == 0, stop=g == CG - 1)
                    mm.then_inc(s_gsum, 1)
                    pe.wait_ge(s_vv, START + (b + 1) * CHUNK)
                    pe.wait_ge(s_vln, START + (b + 1) * CHUNK)
                    pe.wait_ge(s_z, START + (b + 1) * CHUNK)
                    yv = Y[:, :, :, :].rearrange("p g t (h k) -> p g h k t", k=CHUNK)
                    for j in range(NB):
                        if j >= 2:
                            pe.wait_ge(s_osb, START + b * (2 * NB) + 2 * (j - 1))
                        for g in range(CG):
                            pe.matmul(ps[:, j % 2, :], w_out_s[:, g, 0:P], yv[:, g, ROWS * j:ROWS * (j + 1), :, :],
                                      start=g == 0, stop=g == CG - 1)
                        for g in range(CG):
                            mm = pe.matmul(ps[0:CH - P, 2 + j % 2, :], w_out_s[:, g, P:CH],
                                           yv[:, g, ROWS * j:ROWS * (j + 1), :, :], start=g == 0, stop=g == CG - 1)
                        mm.then_inc(s_oproj, 1)

            @block.scalar
            def _(act):
                act.wait_ge(s_const, START + 4)
                act.wait_ge(s_w, START + 16 * NLOADS)
                with act.Fori(0, B) as b:
                    act.preload_act_table_set("natural_log_exp_and_others")
                    act.wait_ge(s_border, START + (b + 1) * 4)
                    for j in range(NB * CG):
                        g = j // NB
                        y0 = 1 + (j % NB) * ROWS
                        act.wait_ge(s_win, START + b * (NB * CG) + j + 1)
                        if j == 2 * NB:
                            act.wait_ge(s_conv, START + b * (9 * CG) + 9)
                        act.activation(pad[:, g % 2, y0:y0 + ROWS, 1:1 + SIDE],
                                       ps[:, j % 2, :].rearrange("p (h w) -> p h w", w=SIDE),
                                       ACT.Copy).then_inc(s_pad, 1)
                    for t in range(CHUNK):
                        act.wait_ge(s_prox, START + b * CHUNK + t + 1)
                        act.activation(S[:, t, :], ps[:, 2 + t % 2, :], ACT.Copy).then_inc(s_hi, 1)
                        act.wait_ge(s_res, START + b * CHUNK + t + 1)
                        if t:
                            act.wait_ge(s_lo, START + b * CHUNK + t)
                        n = b * (2 * CHUNK) + 2 * t
                        if t:
                            act.wait_ge(s_mid, START + n)
                        act.activation(mid_tmp, gabs[:, 0, 0, :], ACT.Copy).then_inc(s_mid, 1)
                        act.wait_ge(s_mid, START + n + 1)
                        act.activation(S[32:64, t, :], mid_tmp[32:64, :], ACT.Copy).then_inc(s_mid, 1)
                    act.wait_ge(s_lo, START + (b + 1) * CHUNK)
                    act.wait_ge(s_mid, START + (b + 1) * (2 * CHUNK))
                    with act.Fori(0, CG) as c:
                        bc = b * CG + c
                        u = bc * UNITS

                        def y_out(t):
                            act.wait_ge(s_acc, START + u + NDIR * (t + 1))
                            act.activation(Y[:, c, t, :], ps[:, 7, :], ACT.Copy).then_inc(s_yout, 1)

                        def copy_gate(k, n):
                            slot = (k % 2, 4 + k % 4, 2 + k % 2)[n]
                            user = (s_lx, s_uh, s_dx)[n]
                            ring = 4 if n == 1 else 2
                            act.wait_ge(s_lud, START + 3 * (u + k) + n + 1)
                            act.wait_ge(user, START + (u + k + 1 - ring if k >= ring else u))
                            act.activation(lud[:, slot, :], ps[:, 6, :], ACT.Copy).then_inc(s_ludsb, 1)

                        def log_sum(k):
                            act.wait_ge(s_s2, START + u + k + 1)
                            act.wait_ge(s_q, START + (u + k - 1 if k >= 2 else u))
                            act.activation(r0[:, k % 2, :], s2[:, k % 2, :], ACT.Ln,
                                           bias=epsv[:, 0:1]).then_inc(s_ln, 1)

                        def exp_log(k):
                            act.wait_ge(s_ln, START + u + k + 1)
                            act.activation(r0[:, k % 2, :], r0[:, k % 2, :], ACT.Exp, scale=-1.0).then_inc(s_r0, 1)

                        for k in range(UNITS):
                            t, q = k // NDIR, k % 2
                            copy_gate(k, 0)
                            act.wait_ge(s_gate, START + u + k + 1)
                            act.wait_ge(s_s2, START + (u + k - 1 if k >= 2 else u))
                            act.wait_ge(s_s1, START + (u + k - 1 if k >= 2 else u))
                            act.activation(gabs[:, q, :, :], ps[:, 3 * q:3 * q + 3, :], ACT.Abs).then_inc(s_abs, 1)
                            copy_gate(k, 1)
                            if k:
                                log_sum(k - 1)
                            copy_gate(k, 2)
                            if k:
                                exp_log(k - 1)
                            if k % NDIR == NDIR - 2 and t:
                                y_out(t - 1)
                        log_sum(UNITS - 1)
                        exp_log(UNITS - 1)
                        y_out(CHUNK - 1)
                    for t in range(CHUNK):
                        q = t % 2
                        act.wait_ge(s_cen, START + b * (CHUNK * CG) + CG * (t + 1))
                        if t >= 2:
                            act.wait_ge(s_var, START + b * CHUNK + t - 1)
                        act.activation(prod_sq(t), Y[:, :, t, :], ACT.Square).then_inc(s_sq, 1)
                        act.wait_ge(s_var, START + b * CHUNK + t + 1)
                        act.wait_ge(s_vv, START + b * CHUNK + t + 1)
                        if t >= 2:
                            act.wait_ge(s_z, START + b * CHUNK + t - 1)
                        act.activation(r0[:, q, :], ps[:, 2 + q, :], ACT.Ln, bias=epsv[:, 1:2],
                                       scale=1.0 / DIN).then_inc(s_vln, 1)
                        act.wait_ge(s_vln, START + b * CHUNK + t + 1)
                        act.activation(r0[:, q, :], r0[:, q, :], ACT.Exp, scale=-0.5).then_inc(s_vr0, 1)
                    for g in range(CG):
                        for t in range(CHUNK):
                            n = b * (CG * CHUNK) + g * CHUNK + t
                            act.wait_ge(s_z, START + b * CHUNK + t + 1)
                            act.wait_ge(s_gsq, START + n)
                            act.activation(prod[:, 2, :], Y[:, g, t, :], ACT.Square, scale=vecs[:, 2, g:g + 1],
                                           bias=vecs[:, 3, g:g + 1],
                                           accum_out=gacc[:, g, t:t + 1]).then_inc(s_gsq, 1)
                    act.wait_ge(s_grn, START + b * 12 + 1)
                    act.activation(gx[:, 1, :], gx[:, 0, :], ACT.Sqrt).then_inc(s_gxr, 1)
                    act.wait_ge(s_grn, START + b * 12 + 12)
                    for j in range(NB):
                        act.wait_ge(s_oproj, START + b * NB + j + 1)
                        act.wait_ge(s_out[j % 2], START + b * (NB * 16) + 32 * (j // 2))
                        o_a, o_b = opx(j % 2)
                        act.activation(o_a, ps[:, j % 2, :], ACT.Identity, bias=b_out[:, 0:1]).then_inc(s_osb, 1)
                        act.activation(o_b, ps[0:CH - P, 2 + j % 2, :], ACT.Identity,
                                       bias=b_out[0:CH - P, 1:2]).then_inc(s_osb, 1)

            @block.vector
            def _(dve):
                dve.wait_ge(s_w, START + 16 * NLOADS)
                WC = NDIR * NGATE * P
                hi = Y[:, 0, :, :].rearrange("p a b -> p (a b)").bitcast(BF16)[:, 0:WC]
                md = Y[:, 0, :, :].rearrange("p a b -> p (a b)").bitcast(BF16)[:, WC:2 * WC]
                acc = Y[:, 1, :, :].rearrange("p a b -> p (a b)")[:, 0:WC]
                for c in range(CG):
                    w = w_tmp[:, c * WC:(c + 1) * WC]
                    wd = w.rearrange("p (d n m) -> p d n m", d=NDIR, n=NGATE)
                    n = 8 * c
                    if c:
                        dve.wait_ge(s_wsplit, START + n)
                    for d in range(NDIR):
                        ins = dve.tensor_scalar(wd[:, d, 4:6, :], wd[:, d, 4:6, :], w_mix[:, d:d + 1], None, ALU.mult)
                    ins.then_inc(s_wsplit, 1)
                    dve.wait_ge(s_wsplit, START + n + 1)
                    dve.tensor_copy(hi, w).then_inc(s_wsplit, 1)
                    dve.wait_ge(s_wsplit, START + n + 2)
                    dve.tensor_tensor(w, w, hi, ALU.subtract).then_inc(s_wsplit, 1)
                    dve.wait_ge(s_wsplit, START + n + 3)
                    dve.tensor_copy(md, w).then_inc(s_wsplit, 1)
                    dve.wait_ge(s_wsplit, START + n + 4)
                    dve.tensor_tensor(w, w, md, ALU.subtract).then_inc(s_wsplit, 1)
                    dve.wait_ge(s_wsplit, START + n + 5)
                    dve.tensor_scalar(acc, w, part_mask[:, 2:3], None, ALU.mult).then_inc(s_wsplit, 1)
                    dve.wait_ge(s_wsplit, START + n + 6)
                    dve.scalar_tensor_tensor(out=acc, in0=md, scalar=part_mask[:, 1:2], in1=acc,
                                             op0=ALU.mult, op1=ALU.add).then_inc(s_wsplit, 1)
                    dve.wait_ge(s_wsplit, START + n + 7)
                    dve.scalar_tensor_tensor(out=w_gate[:, c, :, :, :].rearrange("p d n m -> p (d n m)"),
                                             in0=hi, scalar=part_mask[:, 0:1], in1=acc,
                                             op0=ALU.mult, op1=ALU.add).then_inc(s_wsplit, 1)
                dve.wait_ge(s_wsplit, START + 24)
                with dve.Fori(0, B) as b:
                    for g in range(CG):
                        xg = X[:, g, :].rearrange("p (h w) -> p h w", w=SIDE)
                        dve.wait_ge(s_pad, START + b * (NB * CG) + NB * (g + 1))
                        for k in range(9):
                            src = pad[:, g % 2, k // 3:k // 3 + SIDE, k % 3:k % 3 + SIDE]
                            n = b * (9 * CG) + 9 * g + k
                            if k == 0:
                                dve.tensor_scalar(xg, src, w_dw[:, g, 0:1], b_dw[:, g:g + 1],
                                                  ALU.mult, ALU.add).then_inc(s_conv, 1)
                            else:
                                dve.wait_ge(s_conv, START + n)
                                dve.scalar_tensor_tensor(out=xg, in0=src, scalar=w_dw[:, g, k:k + 1], in1=xg,
                                                         op0=ALU.mult, op1=ALU.add).then_inc(s_conv, 1)
                    for t in range(CHUNK):
                        dve.wait_ge(s_hi, START + b * CHUNK + t + 1)
                        if t:
                            dve.wait_ge(s_lo, START + b * CHUNK + t)
                        dve.tensor_tensor(gabs[:, 0, 0, :], ps[:, 2 + t % 2, :], S[:, t, :],
                                          ALU.subtract).then_inc(s_res, 1)
                        dve.wait_ge(s_mid, START + b * (2 * CHUNK) + 2 * t + 1)
                        dve.tensor_tensor(S[64:96, t, :], gabs[64:96, 0, 0, :], mid_tmp[64:96, :],
                                          ALU.subtract).then_inc(s_lo, 1)
                    with dve.Fori(0, CG) as c:
                        bc = b * CG + c
                        u = bc * UNITS

                        def sum2(k):
                            q = k % 2
                            dve.wait_ge(s_s1, START + u + k + 1)
                            dve.wait_ge(s_ln, START + (u + k - 1 if k >= 2 else u))
                            dve.wait_ge(s_rec, START + (u + k - 1 if k >= 2 else u))
                            dve.tensor_tensor(s2[:, q, :], s1[:, q, :], gabs[:, q, 2, :], ALU.add).then_inc(s_s2, 1)

                        dve.wait_ge(s_h0, START + bc + 1)
                        sum2(0)
                        for k in range(UNITS):
                            t, d, q = k // NDIR, k % NDIR, k % 2
                            h_old, h_new = H[:, d, t % 2, :], H[:, d, (t + 1) % 2, :]
                            shifted = bass.AP(tensor=h_old.tensor, offset=h_old.offset,
                                              ap=[h_old.ap[0], [CHUNK, 3], [1, BANK]])
                            dve.wait_ge(s_gate, START + u + k + 1)
                            dve.wait_ge(s_abs, START + u + k + 1)
                            dve.wait_ge(s_h, START + (u + k - NDIR + 1 if k >= NDIR else u))
                            dve.wait_ge(s_n2, START + u + k)
                            dve.tensor_tensor(prod[:, :, :], ps[:, 3 * q:3 * q + 3, :], shifted, ALU.mult).then_inc(s_prod, 1)
                            dve.wait_ge(s_r0, START + u + k + 1)
                            dve.scalar_tensor_tensor(out=s2[:, q, :], in0=s2[:, q, :], scalar=GATE_EPS,
                                                     in1=r0[:, q, :], op0=ALU.add, op1=ALU.mult).then_inc(s_err, 1)
                            dve.wait_ge(s_prod, START + u + k + 1)
                            dve.wait_ge(s_h, START + u + k)
                            dve.tensor_tensor(total[:, :], prod[:, 0, :], prod[:, 1, :], ALU.add).then_inc(s_n1, 1)
                            dve.wait_ge(s_err, START + u + k + 1)
                            dve.scalar_tensor_tensor(out=r0[:, q, :], in0=s2[:, q, :], scalar=2.0,
                                                     in1=r0[:, q, :], op0=ALU.subtract,
                                                     op1=ALU.mult).then_inc(s_rec, 1)
                            dve.wait_ge(s_n1, START + u + k + 1)
                            dve.tensor_tensor(total[:, :], total[:, :], prod[:, 2, :], ALU.add).then_inc(s_n2, 1)
                            if k + 1 < UNITS:
                                sum2(k + 1)
                            dve.wait_ge(s_n2, START + u + k + 1)
                            dve.wait_ge(s_rec, START + u + k + 1)
                            dve.wait_ge(s_h, START + u + k)
                            dve.tensor_tensor(total[:, :], total[:, :], r0[:, q, :], ALU.mult).then_inc(s_q, 1)
                            dve.wait_ge(s_q, START + u + k + 1)
                            dve.wait_ge(s_lx, START + u + k + 1)
                            dve.wait_ge(s_uh, START + (u + k - NDIR - 3 if k >= 2 * NDIR else u))
                            dve.tensor_tensor(h_new[:, CHUNK:CHUNK + BANK], LX[:, q, :], total[:, :],
                                              ALU.subtract).then_inc(s_h, 1)
                    dve.wait_ge(s_yout, START + (b + 1) * (CG * CHUNK))

                    def normalise(t):
                        q = t % 2
                        dve.wait_ge(s_newt, START + b * (4 * CHUNK) + 4 * (t + 1))
                        yt = Y[:, :, t, :]
                        r = r0[:, q, :]
                        rb = bass.AP(tensor=r.tensor, offset=r.offset, ap=[r.ap[0], [0, CG], [1, BANK]])
                        dve.tensor_tensor(yt, yt, rb, ALU.mult).then_inc(s_z, 1)

                    for t in range(CHUNK):
                        q = t % 2
                        dve.wait_ge(s_mu, START + b * CHUNK + t + 1)
                        for g in range(CG):
                            dve.scalar_tensor_tensor(out=Y[:, g, t, :], in0=ps[:, q, :], scalar=-1.0 / DIN,
                                                     in1=Y[:, g, t, :], op0=ALU.mult, op1=ALU.add).then_inc(s_cen, 1)
                        dve.wait_ge(s_var, START + b * CHUNK + t + 1)
                        if t >= 2:
                            dve.wait_ge(s_newt, START + b * (4 * CHUNK) + 4 * (t - 1))
                        dve.tensor_scalar(s1[:, q, :], ps[:, 2 + q, :], 1.0 / DIN, LN0_EPS, ALU.mult,
                                          ALU.add).then_inc(s_vv, 1)
                        if t:
                            normalise(t - 1)
                    normalise(CHUNK - 1)
                    n = b * 12
                    dve.wait_ge(s_gsq, START + (b + 1) * (CG * CHUNK))
                    dve.tensor_reduce(gx[:, 0, :], gacc[:, :, :], AX_X, ALU.add).then_inc(s_grn, 1)
                    dve.wait_ge(s_gsum, START + 2 * b + 1)
                    dve.tensor_reduce(small[:, 0:1], ps[:, 4, 0:CG], AX_X, ALU.add).then_inc(s_grn, 1)
                    dve.wait_ge(s_grn, START + n + 2)
                    dve.tensor_scalar(small[:, 1:2], small[:, 0:1], 1.0 / DIN, GRN_EPS, ALU.mult,
                                      ALU.add).then_inc(s_grn, 1)
                    dve.wait_ge(s_grn, START + n + 3)
                    dve.reciprocal(small[:, 2:3], small[:, 1:2]).then_inc(s_grn, 1)
                    dve.wait_ge(s_grn, START + n + 4)
                    dve.wait_ge(s_gxr, START + b + 1)
                    dve.tensor_scalar(svec[:, 0, :], gx[:, 1, :], small[:, 2:3], None, ALU.mult).then_inc(s_grn, 1)
                    dve.wait_ge(s_grn, START + n + 5)
                    dve.tensor_tensor(svec[:, 0, :], svec[:, 0, :], vecs[:, 0, :], ALU.mult).then_inc(s_grn, 1)
                    dve.wait_ge(s_grn, START + n + 6)
                    dve.tensor_scalar(svec[:, 0, :], svec[:, 0, :], 1.0, None, ALU.add).then_inc(s_grn, 1)
                    dve.wait_ge(s_grn, START + n + 7)
                    dve.tensor_tensor(svec[:, 1, :], svec[:, 0, :], vecs[:, 2, :], ALU.mult).then_inc(s_grn, 1)
                    dve.tensor_tensor(svec[:, 2, :], svec[:, 0, :], vecs[:, 3, :], ALU.mult).then_inc(s_grn, 1)
                    dve.wait_ge(s_grn, START + n + 9)
                    dve.tensor_tensor(svec[:, 2, :], svec[:, 2, :], vecs[:, 1, :], ALU.add).then_inc(s_grn, 1)
                    for g in range(CG):
                        ins = dve.tensor_scalar(w_out_s[:, g, :], w_out[:, g, :], svec[:, 1, g:g + 1], None, ALU.mult)
                    ins.then_inc(s_grn, 1)
                    dve.wait_ge(s_gsum, START + 2 * b + 2)
                    dve.tensor_copy(b_out[:, 0:1], ps[:, 5, 0:1])
                    dve.tensor_copy(b_out[0:CH - P, 1:2], ps[0:CH - P, 4, 0:1]).then_inc(s_grn, 1)
                    dve.wait_ge(s_oproj, START + (b + 1) * NB)


def layer0_inputs(v):
    import numpy as np
    T = np.ascontiguousarray
    gates = [v["L0_conv_W_w"].reshape(3, NDIR, CG, P, PROXY)[i] for i in range(3)]
    gates += [v[f"L0_conv_W_{n}"].reshape(NDIR, CG, P, PROXY) for n in "lud"]
    wg = np.stack(gates).transpose(4, 2, 1, 0, 3).reshape(PROXY, -1)
    col = lambda a: a.reshape(CG, P).T
    mask = np.zeros((P, 3), np.float32)
    for i, part in enumerate([0, 1, 0, 1, 0, 1, 2]):
        mask[16 * i:16 * i + 16, part] = 1.0
    return {
        "x": T(v["x"].reshape(-1, CH, PIX)),
        "w_in": T(v["L0_conv_W_in"].T), "w_dw": T(v["L0_conv_W_dw"].reshape(DIN, 9)), "b_dw": T(col(v["L0_conv_b_dw"])),
        "w_proxy": T(np.tile(v["L0_conv_W_xd"].T, (1, P // PROXY))), "w_gate": T(np.tile(wg, (P // PROXY, 1))),
        "w_mix": T(np.tile(v["L0_conv_w_m"], (P, 1))), "part_mask": mask, "w_out": T(v["L0_conv_W_out"].T),
        "vecs": T(np.stack([col(v["L0_conv_" + n]) for n in ("grn_gamma", "grn_beta", "ln_w", "ln_b")], 1)),
        "ident": np.eye(P, dtype=np.float32),
    }


def layer1(nc, B, io, mid, out):
    T = 1024
    NJ = PIX // T
    HALF = T // BANK
    TT = T // P
    NS = 16
    RANK = 12
    KCONV = 4
    NM = 2
    NG = NM * CG
    UNITS = NS * CG
    DTROW = 96

    with ExitStack() as ctx:
        def sb(name, shape, dt=F32):
            return ctx.enter_context(nc.sbuf_tensor(name, shape, dt))

        sems = []

        def sem(name):
            sems.append(ctx.enter_context(nc.semaphore(name)))
            return sems[-1]

        wi_a = sb("wi_a", [P, NM, 2, CG, P])
        wi_b = sb("wi_b", [CH - P, NM, 2, CG, P])
        wc = sb("wc", [P, NG, KCONV])
        bc_ = sb("bc_", [P, NG])
        wx = sb("wx", [P, NG, DTROW + RANK])
        wdt = sb("wdt", [P, NG, P])
        bdt = sb("bdt", [P, NG])
        A = sb("A", [P, NG, NS])
        Dv = sb("Dv", [P, NG, 1])
        wo = sb("wo", [P, NG, CH])
        sel = sb("sel", [P, 2 * NS, P], BF16)
        ln_gb = sb("ln_gb", [P, 2, CH])
        ident = sb("ident1", [P, P])
        tok = sb("tok", [P, TT, CH])
        xs = sb("xs", [P, TT, CH])
        st = sb("st", [P, 6, TT])
        xt_a = sb("xt_a", [P, T])
        xt_b = sb("xt_b", [CH - P, T])
        raw = sb("raw", [P, 2, T + KCONV])
        halo = sb("halo", [P, NG, KCONV])
        xc = sb("xc", [P, NG, T])
        dt = sb("dt", [P, NG, T])
        dtx = sb("dtx", [P, NG, T])
        S = sb("S1", [P, NM, T], BF16)
        last = sb("last", [P, NG, NS])
        dA = sb("dA", [P, 2, T])
        u = sb("u", [P, 2, T])
        h = sb("h", [P, 3, T])
        p = sb("p", [P, 2, T])
        bb = sb("bb", [P, 2, T])
        cb = sb("cb", [P, 2, T])
        o = raw[:, :, 0:CH]
        resid = bb[:, :, :]
        midt = cb[:, :, :].bitcast(BF16)
        dtl = p[:, :, :]
        sq = u[:, :, :].rearrange("p a b -> p (a b)")[:, 0:TT * CH].rearrange("p (a b) -> p a b", a=TT)

        ps = ctx.enter_context(nc.psum_tensor("ps1", [P, 8, BANK], F32))

        s_w = sem("t_w")
        s_passed = sem("t_passed")
        s_A = sem("t_A")
        s_tok = sem("t_tok")
        s_zero = sem("t_zero")
        s_ln = sem("t_ln")
        s_lsq = sem("t_lsq")
        s_tr = sem("t_tr")
        s_xt = sem("t_xt")
        s_in = sem("t_in")
        s_raw = sem("t_raw")
        s_conv = sem("t_conv")
        s_xc = sem("t_xc")
        s_xp = sem("t_xp")
        s_hi = sem("t_hi")
        s_res = sem("t_res")
        s_mid = sem("t_mid")
        s_lo = sem("t_lo")
        s_dtp = sem("t_dtp")
        s_abs = sem("t_abs")
        s_e = sem("t_e")
        s_l = sem("t_l")
        s_max = sem("t_max")
        s_w1 = sem("t_w1")
        s_dt = sem("t_dt")
        s_dtx = sem("t_dtx")
        s_bc = sem("t_bc")
        s_bcs = sem("t_bcs")
        s_da = sem("t_da")
        s_u = sem("t_u")
        s_scan = sem("t_scan")
        s_last = sem("t_last")
        s_p = sem("t_p")
        s_y = sem("t_y")
        s_yd = sem("t_yd")
        s_z = sem("t_z")
        s_zs = sem("t_zs")
        s_yz = sem("t_yz")
        s_op = sem("t_op")
        s_o = sem("t_o")
        s_st = [sem("t_st0"), sem("t_st1")]

        def bank2(q):
            return ps[:, 4 + 2 * q:6 + 2 * q, :]

        def halves(ap):
            return ap.rearrange("p (a b) -> p a b", a=HALF)

        NLOADS = 14

        def waits_passed(eng):
            eng.sem_inc(s_passed, 1)

        with nc.Block() as block:
            @block.sync
            def _(sp):
                loads = [
                    (wi_a[:, :, :, :, :].rearrange("p a b c d -> p (a b c d)"), io["wi"][0:P, :]),
                    (wi_b[:, :, :, :, :].rearrange("p a b c d -> p (a b c d)"), io["wi"][P:CH, :]),
                    (wc[:, :, :], io["wc"].rearrange("(g p) k -> p g k", p=P)),
                    (bc_[:, :], io["bc"]), (bdt[:, :], io["bdt"]), (Dv[:, :, 0], io["D"]),
                    (wx[:, :, :], io["wx"].rearrange("(g p) m -> p g m", p=P)),
                    (wdt[DTROW:DTROW + RANK, :, :], io["wdt"].rearrange("r (g m) -> r g m", g=NG)),
                    (A[:, :, :], io["A_log"].rearrange("(g p) n -> p g n", p=P)),
                    (wo[:, :, :], io["wo"].rearrange("(g p) m -> p g m", p=P)),
                    (ln_gb[:, 0, :], io["ln_g"]), (ln_gb[:, 1, :], io["ln_b"]),
                    (ident[:, :], io["ident"]), (xc[:, 0:4, :].rearrange("p g n -> p (g n)"), io["sel"]),
                ]
                assert len(loads) == NLOADS
                for dst, src in loads:
                    sp.dma_start(dst, src).then_inc(s_w, 16)
                with sp.Fori(0, B) as b:
                    tokens = mid[b].rearrange("c n -> (c n)").rearrange("(j i p c) -> j p i c", i=TT, p=P, c=CH)
                    stored = out[b].rearrange("c n -> (c n)").rearrange("(j i p c) -> j i p c", i=TT, p=P, c=CH)
                    with sp.Fori(0, NJ) as j:
                        cj = b * NJ + j
                        sp.wait_ge(s_ln, START + 9 * cj)
                        sp.dma_start(tok[:, :, :], tokens[j]).then_inc(s_tok, 16)
                        for i in range(TT):
                            sp.wait_ge(s_o, START + TT * cj + i + 1)
                            sp.dma_start(stored[j, i], o[:, i % 2, :]).then_inc(s_st[i % 2], 16)
                for s in s_st:
                    sp.wait_ge(s, START + B * NJ * (TT // 2) * 16)

            @block.gpsimd
            def _(pool):
                for s in sems:
                    pool.sem_inc(s, START)
                pool.wait_ge(s_w, START + 16 * NLOADS)
                with pool.Fori(0, B) as b:
                    pool.wait_ge(s_scan, START + b * (NJ * NM * UNITS))
                    pool.wait_ge(s_last, START + b * (NJ * NM * UNITS))
                    pool.wait_ge(s_conv, START + b * (NJ * NG * 6))
                    waits_passed(pool)
                    pool.memset(last[:, :, :], 0.0).then_inc(s_zero, 1)
                    pool.memset(halo[:, :, :], 0.0).then_inc(s_zero, 1)
                    with pool.Fori(0, NJ) as j:
                        cj = b * NJ + j
                        for g in range(NG):
                            n, q = cj * NG + g, g % 2
                            e, w, c = h[:, 0, :], h[:, 1, :], h[:, 2, :]
                            pool.wait_ge(s_e, START + n + 1)
                            pool.wait_ge(s_l, START + n)
                            pool.wait_ge(s_dt, START + n)
                            waits_passed(pool)
                            pool.tensor_scalar(w, e, 1.0, 1.0, ALU.mult, ALU.add).then_inc(s_w1, 1)
                            pool.wait_ge(s_w1, START + 4 * n + 1)
                            waits_passed(pool)
                            pool.tensor_scalar(c, w, 1.0, -1.0, ALU.mult, ALU.add).then_inc(s_w1, 1)
                            pool.wait_ge(s_w1, START + 4 * n + 2)
                            pool.tensor_tensor(c, c, e, ALU.subtract).then_inc(s_w1, 1)
                            pool.wait_ge(s_w1, START + 4 * n + 3)
                            pool.wait_ge(s_max, START + n + 1)
                            pool.tensor_tensor(c, u[:, 0, :], c, ALU.subtract).then_inc(s_w1, 1)
                        with pool.Fori(0, NM) as m:
                            um = (cj * NM + m) * UNITS
                            for k in range(UNITS):
                                n, g, q = k // CG, k % CG, k % 2
                                if k == 0:
                                    pool.wait_ge(s_dtx, START + cj * NG + NG)
                                pool.wait_ge(s_bcs, START + (cj * NM + m) * (2 * NS) + 2 * n + 1)
                                pool.wait_ge(s_scan, START + (um + k - 1 if k >= 2 else um))
                                waits_passed(pool)
                                pool.tensor_tensor(u[:, q, :], dtx[:, m * CG + g, :], bb[:, n % 2, :],
                                                   ALU.mult).then_inc(s_u, 1)

            @block.tensor
            def _(pe):
                pe.wait_ge(s_w, START + 16 * NLOADS)
                pe.wait_ge(s_A, START + 3)
                with pe.Fori(0, B * NJ) as cj:
                    pe.wait_ge(s_ln, START + 9 * cj + 9)
                    pe.wait_ge(s_o, START + TT * cj)
                    for i in range(TT):
                        pe.transpose(ps[:, i // 4, (i % 4) * P:(i % 4 + 1) * P], xs[:, i, 0:P], ident[:, :])
                        mm = pe.transpose(ps[0:CH - P, 2 + i // 4, (i % 4) * P:(i % 4 + 1) * P], xs[:, i, P:CH],
                                          ident[:, :])
                    mm.then_inc(s_tr, 1)
                    pe.wait_ge(s_xt, START + 2 * cj + 2)

                    def in_proj(m, part, g, banks):
                        for a in range(HALF):
                            cols = slice(a * BANK, (a + 1) * BANK)
                            pe.matmul(banks[:, a, :], wi_a[:, m, part, g, :], xt_a[:, cols], start=True, stop=False)
                            mm = pe.matmul(banks[:, a, :], wi_b[:, m, part, g, :], xt_b[:, cols],
                                           start=False, stop=True)
                        return mm

                    for g in range(NG):
                        pe.wait_ge(s_raw, START + (cj * NG + (g - 1 if g >= 2 else 0)))
                        if g == 0:
                            pe.wait_ge(s_zs, START + cj * NG)
                        in_proj(g // CG, 0, g % CG, bank2(g % 2)).then_inc(s_in, 1)
                    for m in range(NM):
                        pe.wait_ge(s_xc, START + cj * NG + (m + 1) * CG)
                        for a in range(HALF):
                            for g in range(CG):
                                mm = pe.matmul(ps[0:DTROW + RANK, 2 * m + a, :], wx[:, m * CG + g, :],
                                               xc[:, m * CG + g, a * BANK:(a + 1) * BANK],
                                               start=g == 0, stop=g == CG - 1)
                        mm.then_inc(s_xp, 1)
                    for g in range(NG):
                        pe.wait_ge(s_hi, START + cj * (2 * NM) + 2 * (g // CG) + 2)
                        pe.wait_ge(s_raw, START + cj * NG + NG)
                        pe.wait_ge(s_abs, START + (cj * NG + (g - 1 if g >= 2 else 0)))
                        pe.wait_ge(s_max, START + (cj * NG + (g - 1 if g >= 2 else 0)))
                        for a in range(HALF):
                            mm = pe.matmul(bank2(g % 2)[:, a, :], wdt[DTROW:DTROW + RANK, g, :],
                                           dtl[DTROW:DTROW + RANK, g // CG, a * BANK:(a + 1) * BANK],
                                           start=True, stop=True)
                        mm.then_inc(s_dtp, 1)
                    pe.wait_ge(s_lo, START + cj * NM + NM)
                    pe.wait_ge(s_mid, START + cj * (2 * NM) + 2 * NM)
                    pe.wait_ge(s_abs, START + cj * NG + NG)
                    pe.wait_ge(s_max, START + cj * NG + NG)
                    waits_passed(pe)
                    with pe.Fori(0, NM) as m:
                        cm = cj * NM + m
                        um = cm * UNITS
                        pe.wait_ge(s_yd, START + cm * CG)

                        def spread(i):
                            pe.wait_ge(s_bcs, START + cm * (2 * NS) + i)
                            for a in range(HALF):
                                mm = pe.matmul(ps[:, 6 + a, :], sel[0:DTROW, i, :],
                                               S[0:DTROW, m, a * BANK:(a + 1) * BANK], start=True, stop=True)
                            mm.then_inc(s_bc, 1)

                        def add_y(k):
                            n, g, q = k // CG, k % CG, k % 2
                            pe.wait_ge(s_p, START + um + k + 1)
                            for a in range(HALF):
                                mm = pe.matmul(ps[:, 2 * g + a, :], ident[:, :], p[:, q, a * BANK:(a + 1) * BANK],
                                               start=n == 0, stop=n == NS - 1)
                            mm.then_inc(s_y, 1)

                        spread(0)
                        spread(1)
                        for k in range(UNITS):
                            n, g = k // CG, k % CG
                            if n + 1 < NS and g != 1:
                                spread(2 * n + 2 + g // 2)
                            if k >= 2:
                                add_y(k - 2)
                        add_y(UNITS - 2)
                        add_y(UNITS - 1)
                    pe.wait_ge(s_yd, START + (cj + 1) * NG)
                    pe.wait_ge(s_bcs, START + (cj + 1) * (NM * 2 * NS))
                    for g in range(NG):
                        if g >= 4:
                            pe.wait_ge(s_zs, START + cj * NG + g - 3)
                        in_proj(g // CG, 1, g % CG, ps[:, 2 * (g % 4):2 * (g % 4) + 2, :]).then_inc(s_z, 1)
                    pe.wait_ge(s_yz, START + (cj + 1) * NG)
                    for i in range(TT):
                        pe.wait_ge(s_o, START + (TT * cj + (i - 3 if i >= 4 else 0)))
                        for g in range(NG):
                            mm = pe.matmul(ps[:, i % 4, 0:CH], xc[:, g, i * P:(i + 1) * P], wo[:, g, :],
                                           start=g == 0, stop=g == NG - 1)
                        mm.then_inc(s_op, 1)

            @block.scalar
            def _(act):
                act.wait_ge(s_w, START + 16 * NLOADS)
                act.activation(A[:, :, :], A[:, :, :], ACT.Exp).then_inc(s_A, 1)
                with act.Fori(0, B * NJ) as cj:
                    act.wait_ge(s_ln, START + 9 * cj + 3)
                    act.wait_ge(s_scan, START + cj * (NM * UNITS))
                    act.activation(sq, xs[:, :, :], ACT.Square).then_inc(s_lsq, 1)
                    act.wait_ge(s_ln, START + 9 * cj + 5)
                    act.activation(st[:, 4, :], st[:, 3, :], ACT.Sqrt).then_inc(s_lsq, 1)
                    act.wait_ge(s_tr, START + cj + 1)
                    act.wait_ge(s_z, START + cj * NG)
                    act.activation(halves(xt_a[:, :]), ps[:, 0:2, :], ACT.Copy).then_inc(s_xt, 1)
                    act.activation(halves(xt_b[:, :]), ps[0:CH - P, 2:4, :], ACT.Copy).then_inc(s_xt, 1)

                    def silu(g):
                        act.wait_ge(s_conv, START + (cj * NG + g) * 6 + 5)
                        act.activation(xc[:, g, :], xc[:, g, :], ACT.Silu).then_inc(s_xc, 1)

                    for g in range(NG):
                        act.wait_ge(s_in, START + cj * NG + g + 1)
                        act.wait_ge(s_conv, START + ((cj * NG + (g - 1 if g >= 2 else 0)) * 6))
                        if g < 2:
                            act.wait_ge(s_st[g], START + cj * (TT // 2 * 16))
                        act.activation(halves(raw[:, g % 2, KCONV - 1:KCONV - 1 + T]), bank2(g % 2),
                                       ACT.Copy).then_inc(s_raw, 1)
                        if g:
                            silu(g - 1)
                    silu(NG - 1)
                    for m in range(NM):
                        n = (cj * NM + m)
                        act.wait_ge(s_xp, START + n + 1)
                        act.activation(halves(S[0:DTROW, m, :]), ps[0:DTROW, 2 * m:2 * m + 2, :],
                                       ACT.Copy).then_inc(s_hi, 1)
                        act.activation(halves(dtl[DTROW:DTROW + RANK, m, :]),
                                       ps[DTROW:DTROW + RANK, 2 * m:2 * m + 2, :], ACT.Copy).then_inc(s_hi, 1)
                        act.wait_ge(s_res, START + n + 1)
                        act.activation(midt[0:DTROW, m, 0:T], resid[0:DTROW, m, :], ACT.Copy).then_inc(s_mid, 1)
                        act.wait_ge(s_mid, START + 2 * n + 1)
                        act.activation(S[32:64, m, :], midt[32:64, m, 0:T], ACT.Copy).then_inc(s_mid, 1)
                    act.preload_act_table_set("natural_log_exp_and_others")
                    for g in range(NG):
                        n, q = cj * NG + g, g % 2
                        act.wait_ge(s_dtp, START + n + 1)
                        act.wait_ge(s_w1, START + 4 * n)
                        act.activation(halves(h[:, 0, :]), bank2(q), ACT.Abs, bias=bdt[:, g:g + 1]).then_inc(s_abs, 1)
                        act.wait_ge(s_abs, START + n + 1)
                        act.activation(h[:, 0, :], h[:, 0, :], ACT.Exp, scale=-1.0).then_inc(s_e, 1)
                        act.wait_ge(s_w1, START + 4 * n + 1)
                        act.wait_ge(s_dt, START + n)
                        act.activation(dA[:, 0, :], h[:, 1, :], ACT.Ln).then_inc(s_l, 1)
                    act.wait_ge(s_dt, START + (cj + 1) * NG)
                    act.wait_ge(s_A, START + 3)
                    with act.Fori(0, NM) as m:
                        cm = cj * NM + m
                        um = cm * UNITS
                        act.preload_act_table_set("natural_log_exp_and_others")

                        def spread_out(i):
                            n = i // 2
                            act.wait_ge(s_bc, START + cm * (2 * NS) + i + 1)
                            user = s_p if i % 2 else s_u
                            act.wait_ge(user, START + (um + CG * (n - 1) if n >= 2 else um))
                            act.activation(halves((cb if i % 2 else bb)[:, n % 2, :]), ps[:, 6:8, :],
                                           ACT.Copy).then_inc(s_bcs, 1)

                        def keep_last(k):
                            n, g = k // CG, k % CG
                            act.wait_ge(s_scan, START + um + k + 1)
                            act.activation(last[:, m * CG + g, n:n + 1], h[:, k % 3, T - 1:T], ACT.Copy)\
                               .then_inc(s_last, 1)

                        spread_out(0)
                        spread_out(1)
                        for k in range(UNITS):
                            n, g, q = k // CG, k % CG, k % 2
                            act.wait_ge(s_scan, START + (um + k - 1 if k >= 2 else um))
                            act.activation(dA[:, q, :], dt[:, m * CG + g, :], ACT.Exp,
                                           scale=A[:, m * CG + g, n:n + 1]).then_inc(s_da, 1)
                            if k >= 2:
                                keep_last(k - 2)
                            if n + 1 < NS and g != 1:
                                spread_out(2 * n + 2 + g // 2)
                        keep_last(UNITS - 2)
                        keep_last(UNITS - 1)
                    for g in range(NG):
                        n = cj * NG + g
                        act.wait_ge(s_z, START + n + 1)
                        act.wait_ge(s_yz, START + (cj * NG + (g - 1 if g >= 2 else 0)))
                        act.activation(halves(dA[:, g % 2, :]), ps[:, 2 * (g % 4):2 * (g % 4) + 2, :],
                                       ACT.Silu).then_inc(s_zs, 1)

            @block.vector
            def _(dve):
                dve.wait_ge(s_w, START + 16 * NLOADS)
                dve.wait_ge(s_A, START + 1)
                dve.tensor_scalar(A[:, :, :], A[:, :, :], -1.0, None, ALU.mult).then_inc(s_A, 1)
                dve.tensor_copy(sel[:, :, :].rearrange("p i m -> p (i m)"),
                                xc[:, 0:4, :].rearrange("p g n -> p (g n)")).then_inc(s_A, 1)
                with dve.Fori(0, B) as b, dve.Fori(0, NJ) as j:
                    cj = b * NJ + j
                    l = 9 * cj

                    def over_channels(i):
                        v = st[:, i, :]
                        return bass.AP(tensor=v.tensor, offset=v.offset, ap=[v.ap[0], [1, TT], [0, CH]])

                    def over_tokens(i):
                        v = ln_gb[:, i, :]
                        return bass.AP(tensor=v.tensor, offset=v.offset, ap=[v.ap[0], [0, TT], [1, CH]])

                    dve.wait_ge(s_tok, START + 16 * cj + 16)
                    dve.tensor_reduce(st[:, 0, :], tok[:, :, :], AX_X, ALU.add).then_inc(s_ln, 1)
                    dve.wait_ge(s_ln, START + l + 1)
                    dve.tensor_scalar(st[:, 1, :], st[:, 0, :], -1.0 / CH, None, ALU.mult).then_inc(s_ln, 1)
                    dve.wait_ge(s_ln, START + l + 2)
                    dve.wait_ge(s_o, START + TT * cj)
                    dve.tensor_tensor(xs[:, :, :], tok[:, :, :], over_channels(1), ALU.add).then_inc(s_ln, 1)
                    dve.wait_ge(s_lsq, START + 2 * cj + 1)
                    dve.tensor_reduce(st[:, 2, :], sq, AX_X, ALU.add).then_inc(s_ln, 1)
                    dve.wait_ge(s_ln, START + l + 4)
                    dve.tensor_scalar(st[:, 3, :], st[:, 2, :], 1.0 / CH, LN1_EPS, ALU.mult, ALU.add).then_inc(s_ln, 1)
                    dve.wait_ge(s_lsq, START + 2 * cj + 2)
                    dve.reciprocal(st[:, 5, :], st[:, 4, :]).then_inc(s_ln, 1)
                    dve.wait_ge(s_ln, START + l + 6)
                    dve.tensor_tensor(xs[:, :, :], xs[:, :, :], over_channels(5), ALU.mult).then_inc(s_ln, 1)
                    dve.wait_ge(s_ln, START + l + 7)
                    dve.tensor_tensor(xs[:, :, :], xs[:, :, :], over_tokens(0), ALU.mult).then_inc(s_ln, 1)
                    dve.wait_ge(s_ln, START + l + 8)
                    dve.tensor_tensor(xs[:, :, :], xs[:, :, :], over_tokens(1), ALU.add).then_inc(s_ln, 1)
                    dve.wait_ge(s_zero, START + 2 * b + 2)
                    for g in range(NG):
                        n = (cj * NG + g) * 6
                        r, x = raw[:, g % 2, :], xc[:, g, :]
                        if g == 0:
                            dve.wait_ge(s_op, START + TT * cj)
                        dve.wait_ge(s_raw, START + cj * NG + g + 1)
                        dve.tensor_copy(r[:, 0:KCONV - 1], halo[:, g, 0:KCONV - 1]).then_inc(s_conv, 1)
                        dve.wait_ge(s_conv, START + n + 1)
                        dve.tensor_scalar(x, r[:, 0:T], wc[:, g, 0:1], bc_[:, g:g + 1], ALU.mult,
                                          ALU.add).then_inc(s_conv, 1)
                        for k in range(1, KCONV):
                            dve.wait_ge(s_conv, START + n + k + 1)
                            dve.scalar_tensor_tensor(out=x, in0=r[:, k:k + T], scalar=wc[:, g, k:k + 1], in1=x,
                                                     op0=ALU.mult, op1=ALU.add).then_inc(s_conv, 1)
                        dve.tensor_copy(halo[:, g, 0:KCONV - 1], r[:, T:T + KCONV - 1]).then_inc(s_conv, 1)
                    for m in range(NM):
                        n = cj * NM + m
                        dve.wait_ge(s_hi, START + 2 * n + 2)
                        dve.tensor_tensor(halves(resid[0:DTROW, m, :]), ps[0:DTROW, 2 * m:2 * m + 2, :],
                                          halves(S[0:DTROW, m, :]), ALU.subtract).then_inc(s_res, 1)
                        dve.wait_ge(s_mid, START + 2 * n + 1)
                        dve.wait_ge(s_res, START + n + 1)
                        dve.tensor_tensor(S[64:96, m, :], resid[64:96, m, :], midt[64:96, m, 0:T],
                                          ALU.subtract).then_inc(s_lo, 1)
                    for g in range(NG):
                        n, q = cj * NG + g, g % 2
                        dve.wait_ge(s_abs, START + n + 1)
                        dve.wait_ge(s_w1, START + 4 * n)
                        dve.tensor_scalar(halves(u[:, 0, :]), bank2(q), bdt[:, g:g + 1], 0.0, ALU.add,
                                          ALU.max).then_inc(s_max, 1)
                        dve.wait_ge(s_l, START + n + 1)
                        dve.wait_ge(s_w1, START + 4 * n + 4)
                        dve.tensor_tensor(dt[:, g, :], h[:, 2, :], dA[:, 0, :], ALU.add).then_inc(s_dt, 1)
                        dve.wait_ge(s_dt, START + n + 1)
                        dve.tensor_tensor(dtx[:, g, :], dt[:, g, :], xc[:, g, :], ALU.mult).then_inc(s_dtx, 1)
                    with dve.Fori(0, NM) as m:
                        cm = cj * NM + m
                        um = cm * UNITS

                        def times_c(k):
                            n, g, q = k // CG, k % CG, k % 2
                            dve.wait_ge(s_scan, START + um + k + 1)
                            dve.wait_ge(s_bcs, START + cm * (2 * NS) + 2 * n + 2)
                            dve.wait_ge(s_y, START + (um + k - 1 if k >= 2 else um))
                            dve.tensor_tensor(p[:, q, :], h[:, k % 3, :], cb[:, n % 2, :], ALU.mult).then_inc(s_p, 1)

                        for k in range(UNITS):
                            n, g, q = k // CG, k % CG, k % 2
                            dve.wait_ge(s_da, START + um + k + 1)
                            dve.wait_ge(s_u, START + um + k + 1)
                            dve.wait_ge(s_last, START + (um + k - 2 if k >= 3 else um))
                            dve.wait_ge(s_p, START + (um + k - 2 if k >= 3 else um))
                            dve.tensor_tensor_scan(h[:, k % 3, :], dA[:, q, :], u[:, q, :],
                                                   last[:, m * CG + g, n:n + 1], ALU.mult,
                                                   ALU.add).then_inc(s_scan, 1)
                            if k:
                                times_c(k - 1)
                        times_c(UNITS - 1)
                        dve.wait_ge(s_y, START + um + UNITS)
                        for g in range(CG):
                            x = xc[:, m * CG + g, :]
                            dve.scalar_tensor_tensor(out=halves(x), in0=halves(x), scalar=Dv[:, m * CG + g, :],
                                                     in1=ps[:, 2 * g:2 * g + 2, :], op0=ALU.mult,
                                                     op1=ALU.add).then_inc(s_yd, 1)
                    dve.wait_ge(s_yd, START + (cj + 1) * NG)
                    for g in range(NG):
                        dve.wait_ge(s_zs, START + cj * NG + g + 1)
                        dve.tensor_tensor(xc[:, g, :], xc[:, g, :], dA[:, g % 2, :], ALU.mult).then_inc(s_yz, 1)
                    for i in range(TT):
                        dve.wait_ge(s_op, START + TT * cj + i + 1)
                        dve.wait_ge(s_st[i % 2], START + cj * (TT // 2 * 16) + 16 * (i // 2))
                        dve.tensor_tensor(o[:, i % 2, :], ps[:, i % 4, 0:CH], xs[:, i, :], ALU.add).then_inc(s_o, 1)


def layer1_inputs(v):
    import numpy as np
    T = np.ascontiguousarray
    w = lambda m, n: v[f"L1_conv_m{m}_{n}"]
    wi = np.concatenate([w(1, "in_w").T, w(2, "in_w").T[::-1]], 1)
    col = lambda n: T(np.concatenate([w(1, n), w(2, n)]).reshape(2 * CG, P).T)
    xw = [np.concatenate([w(m, "x_w").T[:, 12:]] * 3 + [w(m, "x_w").T[:, :12]], 1) for m in (1, 2)]
    both = lambda n: T(np.concatenate([w(1, n), w(2, n)]))
    sel = np.zeros((P, 32, P), np.float32)
    for i in range(32):
        for part in range(3):
            sel[32 * part + 16 * (i % 2) + i // 2, i, :] = 1.0
    return {
        "wi": T(wi), "wc": both("conv_w"), "bc": col("conv_b"), "wx": T(np.concatenate(xw)),
        "wdt": T(np.concatenate([w(1, "dt_w").T, w(2, "dt_w").T], 1)), "bdt": col("dt_b"),
        "A_log": both("A_log"), "D": col("D"), "wo": T(np.concatenate([w(1, "out_w").T, w(2, "out_w").T])),
        "ln_g": T(np.tile(v["L1_conv_ln_g"], (P, 1))), "ln_b": T(np.tile(v["L1_conv_ln_b"], (P, 1))),
        "ident": np.eye(P, dtype=np.float32), "sel": sel.reshape(P, 32 * P),
    }


def program(nc, B, io):
    mid = nc.dram_tensor("mid_dram", [B, CH, PIX], F32, kind="Internal").ap()
    layer0(nc, B, io["layer0"], mid)
    layer1(nc, B, io["layer1"], mid, io["out"])


def kernel(**inputs):
    import numpy as _np
    import concourse.bacc as _bacc
    from concourse import mybir as _mybir
    from concourse.bass_utils import run_bass_kernel_spmd as _run

    nc = _bacc.Bacc("TRN2", target_bir_lowering=False, num_devices=1)
    v = {k: _np.asarray(a) for k, a in inputs.items()}
    B = v["x"].shape[0]
    arrays, io = {}, {}
    for layer, made in (("layer0", layer0_inputs(v)), ("layer1", layer1_inputs(v))):
        io[layer] = {}
        for name, a in made.items():
            full = f"{layer}_{name}_dram"
            arrays[full] = a
            io[layer][name] = nc.dram_tensor(full, list(a.shape), _mybir.dt.from_np(a.dtype), kind="ExternalInput").ap()
    io["out"] = nc.dram_tensor("out_dram", [B, CH, PIX], F32, kind="ExternalOutput").ap()
    program(nc, B, io)
    r = _run(nc, [arrays], core_ids=[0])
    return r.results[0]["out_dram"].reshape(v["x"].shape)
```

```python
from contextlib import ExitStack

import concourse.bass as bass
from concourse import mybir
from concourse.alu_op_type import AluOpType as ALU

ACT = mybir.ActivationFunctionType
F32 = mybir.dt.float32
BF16 = mybir.dt.bfloat16
AX_X = mybir.AxisListType.X

P = 128
BANK = 512
CH = 192
DIN = 384
CG = DIN // P
SIDE = 64
PIX = SIDE * SIDE
CHUNK = 8
NDIR = 4
PROXY = 16
NGATE = 6
START = 8
LN0_EPS, GRN_EPS, GATE_EPS, LN1_EPS = 1e-5, 1e-6, 1e-7, 1e-5


def layer0(nc, B, io, mid):
    UNITS = CHUNK * NDIR
    ROWS = BANK // SIDE
    NB = PIX // BANK
    PADW = SIDE + 2

    with ExitStack() as ctx:
        def sb(name, shape, dt=F32):
            return ctx.enter_context(nc.sbuf_tensor(name, shape, dt))

        sems = []

        def sem(name):
            sems.append(ctx.enter_context(nc.semaphore(name)))
            return sems[-1]

        w_in_a = sb("w_in_a", [P, DIN])
        w_in_b = sb("w_in_b", [CH - P, DIN])
        w_dw = sb("w_dw", [P, CG, 9])
        b_dw = sb("b_dw", [P, CG])
        w_proxy = sb("w_proxy", [P, CG, P])
        w_gate = sb("w_gate", [P, CG, NDIR, NGATE, P], BF16)
        w_mix = sb("w_mix", [P, NDIR])
        part_mask = sb("part_mask", [P, 3])
        w_out = sb("w_out", [P, CG, CH])
        vecs = sb("vecs", [P, 4, CG])
        ident = sb("ident", [P, P])
        ones = sb("ones", [P, P])
        epsv = sb("epsv", [P, 2])
        X = sb("X", [P, CG, PIX])
        S = sb("S", [P, CHUNK, BANK], BF16)
        Y = sb("Y", [P, CG, CHUNK, BANK])
        pad = Y[:, :, :, :].rearrange("p a b c -> p (a b c)")[:, 0:2 * PADW * PADW].rearrange(
            "p (n h w) -> p n h w", n=2, h=PADW)
        w_tmp = X[:, :, :].rearrange("p a b -> p (a b)")
        gabs = sb("gabs", [P, 2, 3, BANK])
        lud = sb("lud", [P, 8, BANK])
        s1 = sb("s1", [P, 2, BANK])
        s2 = sb("s2", [P, 2, BANK])
        r0 = sb("r0", [P, 2, BANK])
        prod = sb("prod", [P, 3, BANK])
        total = sb("total", [P, BANK])
        x_a = lud[:, 0:2, :]
        x_b = lud[0:CH - P, 2:4, :]
        w_out_s = prod[:, :, :].rearrange("p a b -> p (a b)")[:, 0:CG * CH].rearrange("p (g m) -> p g m", g=CG)
        LX = sb("LX", [P, 2, BANK])
        DX = sb("DX", [P, 2, BANK])
        UH = sb("UH", [P, 2, BANK])
        HP = BANK + 2 * CHUNK
        H = sb("H", [P, NDIR, 2, HP])
        gacc = sb("gacc", [P, CG, CHUNK])
        gx = sb("gx", [P, 2, CG])
        small = sb("small", [P, 8])
        svec = sb("svec", [P, 3, CG])
        b_out = sb("b_out", [P, 2])

        ps = ctx.enter_context(nc.psum_tensor("ps0", [P, 8, BANK], F32))

        s_w = sem("s_w")
        s_passed = sem("s_passed")
        s_const = sem("s_const")
        s_wsplit = sem("s_wsplit")
        s_x = [sem("s_x0"), sem("s_x1")]
        s_win = sem("s_win")
        s_pad = sem("s_pad")
        s_border = sem("s_border")
        s_conv = sem("s_conv")
        s_prox = sem("s_prox")
        s_hi = sem("s_hi")
        s_res = sem("s_res")
        s_mid = sem("s_mid")
        s_lo = sem("s_lo")
        s_gate = sem("s_gate")
        s_lud = sem("s_lud")
        s_y = sem("s_y")
        s_acc = sem("s_acc")
        s_abs = sem("s_abs")
        s_ludsb = sem("s_ludsb")
        s_ln = sem("s_ln")
        s_r0 = sem("s_r0")
        s_yout = sem("s_yout")
        s_s1 = sem("s_s1")
        s_lx = sem("s_lx")
        s_dx = sem("s_dx")
        s_uh = sem("s_uh")
        s_h0 = sem("s_h0")
        s_s2 = sem("s_s2")
        s_err = sem("s_err")
        s_rec = sem("s_rec")
        s_prod = sem("s_prod")
        s_n1 = sem("s_n1")
        s_n2 = sem("s_n2")
        s_q = sem("s_q")
        s_h = sem("s_h")
        s_mu = sem("s_mu")
        s_cen = sem("s_cen")
        s_sq = sem("s_sq")
        s_var = sem("s_var")
        s_vln = sem("s_vln")
        s_vr0 = sem("s_vr0")
        s_vv = sem("s_vv")
        s_newt = sem("s_newt")
        s_z = sem("s_z")
        s_gsq = sem("s_gsq")
        s_grn = sem("s_grn")
        s_gxr = sem("s_gxr")
        s_gsum = sem("s_gsum")
        s_oproj = sem("s_oproj")
        s_osb = sem("s_osb")
        s_out = [sem("s_out0"), sem("s_out1")]

        def xview(c, t, d):
            img = X[:, c, :]
            if d % 2 == 0:
                v = img.rearrange("p (h k t) -> p h k t", k=CHUNK, t=CHUNK)
            else:
                v = img.rearrange("p (k t h) -> p h k t", k=CHUNK, t=CHUNK)
            return v[:, :, :, t if d < 2 else CHUNK - 1 - t]

        def hk(ap, d):
            v = ap.rearrange("p (h k) -> p h k", k=CHUNK)
            return v if d < 2 else v[:, :, ::-1]

        def opx(q):
            return gabs[:, q, 0, :], gabs[0:CH - P, q, 1, :]

        def prod_sq(t):
            return lud[:, 4 * (t % 2):4 * (t % 2) + 3, :]

        mid_tmp = LX[:, :, :].rearrange("p a b -> p (a b)").bitcast(BF16)[:, 0:BANK]

        NLOADS = 11

        def waits_passed(eng):
            eng.sem_inc(s_passed, 1)

        with nc.Block() as block:
            @block.sync
            def _(sp):
                loads = [
                    (w_in_a[:, :], io["w_in"][0:P, :]), (w_in_b[:, :], io["w_in"][P:CH, :]),
                    (w_dw[:, :, :], io["w_dw"].rearrange("(g p) k -> p g k", p=P)),
                    (b_dw[:, :], io["b_dw"]), (w_proxy[:, :, :], io["w_proxy"].rearrange("(g p) m -> p g m", p=P)),
                    (w_tmp[:, 0:CG * NDIR * NGATE * P], io["w_gate"]),
                    (w_mix[:, :], io["w_mix"]),
                    (part_mask[:, :], io["part_mask"]),
                    (w_out[:, :, :], io["w_out"].rearrange("(g p) m -> p g m", p=P)),
                    (vecs[:, :, :], io["vecs"]),
                    (ident[:, :], io["ident"]),
                ]
                for dst, src in loads:
                    sp.dma_start(dst, src).then_inc(s_w, 16)
                with sp.Fori(0, B) as b:
                    for j in range(NB * CG):
                        if j == 0:
                            sp.wait_ge(s_var, START + b * CHUNK)
                            waits_passed(sp)
                        if j >= 2:
                            sp.wait_ge(s_win, START + b * (NB * CG) + (j - 1))
                        else:
                            sp.wait_ge(s_win, START + b * (NB * CG))
                        px = (j % NB) * BANK
                        sp.dma_start(x_a[:, j % 2, :], io["x"][b, 0:P, px:px + BANK]).then_inc(s_x[j % 2], 16)
                        sp.dma_start(x_b[:, j % 2, :], io["x"][b, P:CH, px:px + BANK]).then_inc(s_x[j % 2], 16)
                    for j in range(NB):
                        sp.wait_ge(s_osb, START + b * (2 * NB) + 2 * j + 2)
                        o_a, o_b = opx(j % 2)
                        sp.dma_start(mid[b, 0:P, j * BANK:(j + 1) * BANK], o_a).then_inc(s_out[j % 2], 16)
                        sp.dma_start(mid[b, P:CH, j * BANK:(j + 1) * BANK], o_b).then_inc(s_out[j % 2], 16)
                for s in s_out:
                    sp.wait_ge(s, START + B * NB * 16)

            @block.gpsimd
            def _(pool):
                for s in sems:
                    pool.sem_inc(s, START)
                pool.memset(ones[:, :], 1.0).then_inc(s_const, 1)
                pool.memset(epsv[:, 0:1], GATE_EPS).then_inc(s_const, 1)
                pool.memset(epsv[:, 1:2], LN0_EPS).then_inc(s_const, 1)
                pool.memset(H[:, :, :, :], 0.0).then_inc(s_const, 1)
                pool.wait_ge(s_const, START + 4)
                pool.wait_ge(s_wsplit, START + 8 * CG)
                with pool.Fori(0, B) as b:
                    pool.wait_ge(s_oproj, START + b * NB)
                    waits_passed(pool)
                    for n in range(2):
                        pool.memset(pad[:, n, 0:PADW:PADW - 1, :], 0.0).then_inc(s_border, 1)
                        pool.memset(pad[:, n, 1:PADW - 1, 0:PADW:PADW - 1], 0.0).then_inc(s_border, 1)
                    with pool.Fori(0, CG) as c:
                        bc = b * CG + c
                        u = bc * UNITS
                        pool.wait_ge(s_h, START + u)
                        pool.wait_ge(s_prod, START + u)
                        pool.wait_ge(s_uh, START + u)
                        waits_passed(pool)
                        pool.memset(H[:, :, 0, CHUNK:CHUNK + BANK], 0.0).then_inc(s_h0, 1)

                        def u_h(k):
                            t, d, q = k // NDIR, k % NDIR, k % 2
                            pool.wait_ge(s_h, START + u + k + 1)
                            if k >= 2:
                                pool.wait_ge(s_acc, START + u + k - 1)
                            else:
                                pool.wait_ge(s_acc, START + u)
                            pool.tensor_tensor(UH[:, q, :], lud[:, 4 + k % 4, :],
                                               H[:, d, (t + 1) % 2, CHUNK:CHUNK + BANK],
                                               ALU.mult).then_inc(s_uh, 1)

                        for k in range(UNITS):
                            t, d, q = k // NDIR, k % NDIR, k % 2
                            pool.wait_ge(s_abs, START + u + k + 1)
                            pool.wait_ge(s_s2, START + (u + k - 1 if k >= 2 else u))
                            pool.tensor_tensor(s1[:, q, :], gabs[:, q, 0, :], gabs[:, q, 1, :],
                                               ALU.add).then_inc(s_s1, 1)
                            pool.wait_ge(s_ludsb, START + 3 * (u + k) + 3)
                            pool.wait_ge(s_h, START + (u + k - 1 if k >= 2 else u))
                            waits_passed(pool)
                            pool.tensor_tensor(hk(LX[:, q, :], d), hk(lud[:, q, :], d), xview(c, t, d),
                                               ALU.mult).then_inc(s_lx, 1)
                            pool.wait_ge(s_acc, START + (u + k - 1 if k >= 2 else u))
                            waits_passed(pool)
                            pool.tensor_tensor(hk(DX[:, q, :], d), hk(lud[:, 2 + q, :], d), xview(c, t, d),
                                               ALU.mult).then_inc(s_dx, 1)
                            if k:
                                u_h(k - 1)
                        u_h(UNITS - 1)
                    for t in range(CHUNK):
                        n = b * (CHUNK * 4) + 4 * t
                        q = t % 2
                        v, r = s1[:, q, :], r0[:, q, :]
                        pool.wait_ge(s_vv, START + b * CHUNK + t + 1)
                        pool.wait_ge(s_vr0, START + b * CHUNK + t + 1)
                        pool.tensor_tensor(v, v, r, ALU.mult).then_inc(s_newt, 1)
                        pool.wait_ge(s_newt, START + n + 1)
                        pool.tensor_tensor(v, v, r, ALU.mult).then_inc(s_newt, 1)
                        pool.wait_ge(s_newt, START + n + 2)
                        waits_passed(pool)
                        pool.tensor_scalar(v, v, -0.5, 1.5, ALU.mult, ALU.add).then_inc(s_newt, 1)
                        pool.wait_ge(s_newt, START + n + 3)
                        pool.tensor_tensor(r, v, r, ALU.mult).then_inc(s_newt, 1)

            @block.tensor
            def _(pe):
                pe.wait_ge(s_w, START + 16 * NLOADS)
                pe.wait_ge(s_const, START + 4)
                with pe.Fori(0, B) as b:
                    for j in range(NB * CG):
                        g, q = j // NB, j % 2
                        pe.wait_ge(s_x[q], START + b * (NB * CG * 16) + 32 * (j // 2 + 1))
                        pe.wait_ge(s_pad, START + (b * (NB * CG) + (j - 1 if j >= 2 else 0)))
                        if j == 0:
                            pe.wait_ge(s_osb, START + b * (2 * NB))
                        pe.matmul(ps[:, q, :], w_in_a[:, g * P:(g + 1) * P], x_a[:, q, :], start=True, stop=False)
                        pe.matmul(ps[:, q, :], w_in_b[:, g * P:(g + 1) * P], x_b[:, q, :],
                                  start=False, stop=True).then_inc(s_win, 1)
                    pe.wait_ge(s_conv, START + (b + 1) * (9 * CG))
                    for t in range(CHUNK):
                        if t >= 2:
                            pe.wait_ge(s_hi, START + b * CHUNK + t - 1)
                            pe.wait_ge(s_res, START + b * CHUNK + t - 1)
                        for g in range(CG):
                            mm = pe.matmul(ps[:, 2 + t % 2, :], w_proxy[:, g, :], xview(g, t, 0),
                                           start=g == 0, stop=g == CG - 1)
                        mm.then_inc(s_prox, 1)
                    pe.wait_ge(s_wsplit, START + 24)
                    pe.wait_ge(s_lo, START + (b + 1) * CHUNK)
                    pe.wait_ge(s_mid, START + (b + 1) * (2 * CHUNK))
                    waits_passed(pe)
                    with pe.Fori(0, CG) as c:
                        bc = b * CG + c
                        u = bc * UNITS

                        def add_y(k, part, done):
                            t, d, q = k // NDIR, k % NDIR, k % 2
                            if part is DX and d == 0:
                                pe.wait_ge(s_yout, START + bc * CHUNK + t)
                            pe.wait_ge(done, START + u + k + 1)
                            return pe.matmul(ps[:, 7, :], ident[:, :], part[:, q, :], start=part is DX and d == 0,
                                             stop=part is UH and d == NDIR - 1)

                        def one_gate(k, n):
                            pe.wait_ge(s_ludsb, START + 3 * (u + k) + n)
                            pe.matmul(ps[:, 6, :], w_gate[:, c, k % NDIR, 3 + n, :], S[:, k // NDIR, :],
                                      start=True, stop=True).then_inc(s_lud, 1)

                        for k in range(UNITS):
                            t, d, q = k // NDIR, k % NDIR, k % 2
                            one_gate(k, 0)
                            pe.wait_ge(s_prod, START + (u + k - 1 if k >= 2 else u))
                            pe.wait_ge(s_abs, START + (u + k - 1 if k >= 2 else u))
                            for n in range(3):
                                mm = pe.matmul(ps[:, 3 * q + n, :], w_gate[:, c, d, n, :], S[:, t, :],
                                               start=True, stop=True)
                            mm.then_inc(s_gate, 1)
                            one_gate(k, 1)
                            if k >= 3:
                                add_y(k - 3, DX, s_dx)
                                add_y(k - 3, UH, s_uh).then_inc(s_acc, 1)
                            one_gate(k, 2)
                        for k in range(UNITS - 3, UNITS):
                            add_y(k, DX, s_dx)
                            add_y(k, UH, s_uh).then_inc(s_acc, 1)
                    pe.wait_ge(s_prod, START + (b + 1) * (CG * UNITS))
                    pe.wait_ge(s_yout, START + (b + 1) * (CG * CHUNK))

                    def var_sum(t):
                        pe.wait_ge(s_sq, START + b * CHUNK + t + 1)
                        if t >= 2:
                            pe.wait_ge(s_vv, START + b * CHUNK + t - 1)
                            pe.wait_ge(s_vln, START + b * CHUNK + t - 1)
                        for g in range(CG):
                            mm = pe.matmul(ps[:, 2 + t % 2, :], ones[:, :], prod_sq(t)[:, g, :],
                                           start=g == 0, stop=g == CG - 1)
                        mm.then_inc(s_var, 1)

                    for t in range(CHUNK):
                        if t >= 2:
                            pe.wait_ge(s_cen, START + b * (CHUNK * CG) + CG * (t - 1))
                        for g in range(CG):
                            mm = pe.matmul(ps[:, t % 2, :], ones[:, :], Y[:, g, t, :],
                                           start=g == 0, stop=g == CG - 1)
                        mm.then_inc(s_mu, 1)
                        if t:
                            var_sum(t - 1)
                    var_sum(CHUNK - 1)
                    pe.wait_ge(s_gxr, START + b + 1)
                    pe.matmul(ps[:, 4, 0:CG], ones[:, :], gx[:, 1, :], start=True, stop=True).then_inc(s_gsum, 1)
                    pe.wait_ge(s_grn, START + b * 12 + 11)
                    for g in range(CG):
                        pe.matmul(ps[:, 5, 0:1], w_out[:, g, 0:P], svec[:, 2, g:g + 1], start=g == 0, stop=g == CG - 1)
                    for g in range(CG):
                        mm = pe.matmul(ps[0:CH - P, 4, 0:1], w_out[:, g, P:CH], svec[:, 2, g:g + 1],
                                       start=g == 0, stop=g == CG - 1)
                    mm.then_inc(s_gsum, 1)
                    pe.wait_ge(s_vv, START + (b + 1) * CHUNK)
                    pe.wait_ge(s_vln, START + (b + 1) * CHUNK)
                    pe.wait_ge(s_z, START + (b + 1) * CHUNK)
                    yv = Y[:, :, :, :].rearrange("p g t (h k) -> p g h k t", k=CHUNK)
                    for j in range(NB):
                        if j >= 2:
                            pe.wait_ge(s_osb, START + b * (2 * NB) + 2 * (j - 1))
                        for g in range(CG):
                            pe.matmul(ps[:, j % 2, :], w_out_s[:, g, 0:P], yv[:, g, ROWS * j:ROWS * (j + 1), :, :],
                                      start=g == 0, stop=g == CG - 1)
                        for g in range(CG):
                            mm = pe.matmul(ps[0:CH - P, 2 + j % 2, :], w_out_s[:, g, P:CH],
                                           yv[:, g, ROWS * j:ROWS * (j + 1), :, :], start=g == 0, stop=g == CG - 1)
                        mm.then_inc(s_oproj, 1)

            @block.scalar
            def _(act):
                act.wait_ge(s_const, START + 4)
                act.wait_ge(s_w, START + 16 * NLOADS)
                with act.Fori(0, B) as b:
                    act.preload_act_table_set("natural_log_exp_and_others")
                    act.wait_ge(s_border, START + (b + 1) * 4)
                    for j in range(NB * CG):
                        g = j // NB
                        y0 = 1 + (j % NB) * ROWS
                        act.wait_ge(s_win, START + b * (NB * CG) + j + 1)
                        if j == 2 * NB:
                            act.wait_ge(s_conv, START + b * (9 * CG) + 9)
                        act.activation(pad[:, g % 2, y0:y0 + ROWS, 1:1 + SIDE],
                                       ps[:, j % 2, :].rearrange("p (h w) -> p h w", w=SIDE),
                                       ACT.Copy).then_inc(s_pad, 1)
                    for t in range(CHUNK):
                        act.wait_ge(s_prox, START + b * CHUNK + t + 1)
                        act.activation(S[:, t, :], ps[:, 2 + t % 2, :], ACT.Copy).then_inc(s_hi, 1)
                        act.wait_ge(s_res, START + b * CHUNK + t + 1)
                        if t:
                            act.wait_ge(s_lo, START + b * CHUNK + t)
                        n = b * (2 * CHUNK) + 2 * t
                        if t:
                            act.wait_ge(s_mid, START + n)
                        act.activation(mid_tmp, gabs[:, 0, 0, :], ACT.Copy).then_inc(s_mid, 1)
                        act.wait_ge(s_mid, START + n + 1)
                        act.activation(S[32:64, t, :], mid_tmp[32:64, :], ACT.Copy).then_inc(s_mid, 1)
                    act.wait_ge(s_lo, START + (b + 1) * CHUNK)
                    act.wait_ge(s_mid, START + (b + 1) * (2 * CHUNK))
                    with act.Fori(0, CG) as c:
                        bc = b * CG + c
                        u = bc * UNITS

                        def y_out(t):
                            act.wait_ge(s_acc, START + u + NDIR * (t + 1))
                            act.activation(Y[:, c, t, :], ps[:, 7, :], ACT.Copy).then_inc(s_yout, 1)

                        def copy_gate(k, n):
                            slot = (k % 2, 4 + k % 4, 2 + k % 2)[n]
                            user = (s_lx, s_uh, s_dx)[n]
                            ring = 4 if n == 1 else 2
                            act.wait_ge(s_lud, START + 3 * (u + k) + n + 1)
                            act.wait_ge(user, START + (u + k + 1 - ring if k >= ring else u))
                            act.activation(lud[:, slot, :], ps[:, 6, :], ACT.Copy).then_inc(s_ludsb, 1)

                        def log_sum(k):
                            act.wait_ge(s_s2, START + u + k + 1)
                            act.wait_ge(s_q, START + (u + k - 1 if k >= 2 else u))
                            act.activation(r0[:, k % 2, :], s2[:, k % 2, :], ACT.Ln,
                                           bias=epsv[:, 0:1]).then_inc(s_ln, 1)

                        def exp_log(k):
                            act.wait_ge(s_ln, START + u + k + 1)
                            act.activation(r0[:, k % 2, :], r0[:, k % 2, :], ACT.Exp, scale=-1.0).then_inc(s_r0, 1)

                        for k in range(UNITS):
                            t, q = k // NDIR, k % 2
                            copy_gate(k, 0)
                            act.wait_ge(s_gate, START + u + k + 1)
                            act.wait_ge(s_s2, START + (u + k - 1 if k >= 2 else u))
                            act.wait_ge(s_s1, START + (u + k - 1 if k >= 2 else u))
                            act.activation(gabs[:, q, :, :], ps[:, 3 * q:3 * q + 3, :], ACT.Abs).then_inc(s_abs, 1)
                            copy_gate(k, 1)
                            if k:
                                log_sum(k - 1)
                            copy_gate(k, 2)
                            if k:
                                exp_log(k - 1)
                            if k % NDIR == NDIR - 2 and t:
                                y_out(t - 1)
                        log_sum(UNITS - 1)
                        exp_log(UNITS - 1)
                        y_out(CHUNK - 1)
                    for t in range(CHUNK):
                        q = t % 2
                        act.wait_ge(s_cen, START + b * (CHUNK * CG) + CG * (t + 1))
                        if t >= 2:
                            act.wait_ge(s_var, START + b * CHUNK + t - 1)
                        act.activation(prod_sq(t), Y[:, :, t, :], ACT.Square).then_inc(s_sq, 1)
                        act.wait_ge(s_var, START + b * CHUNK + t + 1)
                        act.wait_ge(s_vv, START + b * CHUNK + t + 1)
                        if t >= 2:
                            act.wait_ge(s_z, START + b * CHUNK + t - 1)
                        act.activation(r0[:, q, :], ps[:, 2 + q, :], ACT.Ln, bias=epsv[:, 1:2],
                                       scale=1.0 / DIN).then_inc(s_vln, 1)
                        act.wait_ge(s_vln, START + b * CHUNK + t + 1)
                        act.activation(r0[:, q, :], r0[:, q, :], ACT.Exp, scale=-0.5).then_inc(s_vr0, 1)
                    for g in range(CG):
                        for t in range(CHUNK):
                            n = b * (CG * CHUNK) + g * CHUNK + t
                            act.wait_ge(s_z, START + b * CHUNK + t + 1)
                            act.wait_ge(s_gsq, START + n)
                            act.activation(prod[:, 2, :], Y[:, g, t, :], ACT.Square, scale=vecs[:, 2, g:g + 1],
                                           bias=vecs[:, 3, g:g + 1],
                                           accum_out=gacc[:, g, t:t + 1]).then_inc(s_gsq, 1)
                    act.wait_ge(s_grn, START + b * 12 + 1)
                    act.activation(gx[:, 1, :], gx[:, 0, :], ACT.Sqrt).then_inc(s_gxr, 1)
                    act.wait_ge(s_grn, START + b * 12 + 12)
                    for j in range(NB):
                        act.wait_ge(s_oproj, START + b * NB + j + 1)
                        act.wait_ge(s_out[j % 2], START + b * (NB * 16) + 32 * (j // 2))
                        o_a, o_b = opx(j % 2)
                        act.activation(o_a, ps[:, j % 2, :], ACT.Identity, bias=b_out[:, 0:1]).then_inc(s_osb, 1)
                        act.activation(o_b, ps[0:CH - P, 2 + j % 2, :], ACT.Identity,
                                       bias=b_out[0:CH - P, 1:2]).then_inc(s_osb, 1)

            @block.vector
            def _(dve):
                dve.wait_ge(s_w, START + 16 * NLOADS)
                WC = NDIR * NGATE * P
                hi = Y[:, 0, :, :].rearrange("p a b -> p (a b)").bitcast(BF16)[:, 0:WC]
                md = Y[:, 0, :, :].rearrange("p a b -> p (a b)").bitcast(BF16)[:, WC:2 * WC]
                acc = Y[:, 1, :, :].rearrange("p a b -> p (a b)")[:, 0:WC]
                for c in range(CG):
                    w = w_tmp[:, c * WC:(c + 1) * WC]
                    wd = w.rearrange("p (d n m) -> p d n m", d=NDIR, n=NGATE)
                    n = 8 * c
                    if c:
                        dve.wait_ge(s_wsplit, START + n)
                    for d in range(NDIR):
                        ins = dve.tensor_scalar(wd[:, d, 4:6, :], wd[:, d, 4:6, :], w_mix[:, d:d + 1], None, ALU.mult)
                    ins.then_inc(s_wsplit, 1)
                    dve.wait_ge(s_wsplit, START + n + 1)
                    dve.tensor_copy(hi, w).then_inc(s_wsplit, 1)
                    dve.wait_ge(s_wsplit, START + n + 2)
                    dve.tensor_tensor(w, w, hi, ALU.subtract).then_inc(s_wsplit, 1)
                    dve.wait_ge(s_wsplit, START + n + 3)
                    dve.tensor_copy(md, w).then_inc(s_wsplit, 1)
                    dve.wait_ge(s_wsplit, START + n + 4)
                    dve.tensor_tensor(w, w, md, ALU.subtract).then_inc(s_wsplit, 1)
                    dve.wait_ge(s_wsplit, START + n + 5)
                    dve.tensor_scalar(acc, w, part_mask[:, 2:3], None, ALU.mult).then_inc(s_wsplit, 1)
                    dve.wait_ge(s_wsplit, START + n + 6)
                    dve.scalar_tensor_tensor(out=acc, in0=md, scalar=part_mask[:, 1:2], in1=acc,
                                             op0=ALU.mult, op1=ALU.add).then_inc(s_wsplit, 1)
                    dve.wait_ge(s_wsplit, START + n + 7)
                    dve.scalar_tensor_tensor(out=w_gate[:, c, :, :, :].rearrange("p d n m -> p (d n m)"),
                                             in0=hi, scalar=part_mask[:, 0:1], in1=acc,
                                             op0=ALU.mult, op1=ALU.add).then_inc(s_wsplit, 1)
                dve.wait_ge(s_wsplit, START + 24)
                with dve.Fori(0, B) as b:
                    for g in range(CG):
                        xg = X[:, g, :].rearrange("p (h w) -> p h w", w=SIDE)
                        dve.wait_ge(s_pad, START + b * (NB * CG) + NB * (g + 1))
                        for k in range(9):
                            src = pad[:, g % 2, k // 3:k // 3 + SIDE, k % 3:k % 3 + SIDE]
                            n = b * (9 * CG) + 9 * g + k
                            if k == 0:
                                dve.tensor_scalar(xg, src, w_dw[:, g, 0:1], b_dw[:, g:g + 1],
                                                  ALU.mult, ALU.add).then_inc(s_conv, 1)
                            else:
                                dve.wait_ge(s_conv, START + n)
                                dve.scalar_tensor_tensor(out=xg, in0=src, scalar=w_dw[:, g, k:k + 1], in1=xg,
                                                         op0=ALU.mult, op1=ALU.add).then_inc(s_conv, 1)
                    for t in range(CHUNK):
                        dve.wait_ge(s_hi, START + b * CHUNK + t + 1)
                        if t:
                            dve.wait_ge(s_lo, START + b * CHUNK + t)
                        dve.tensor_tensor(gabs[:, 0, 0, :], ps[:, 2 + t % 2, :], S[:, t, :],
                                          ALU.subtract).then_inc(s_res, 1)
                        dve.wait_ge(s_mid, START + b * (2 * CHUNK) + 2 * t + 1)
                        dve.tensor_tensor(S[64:96, t, :], gabs[64:96, 0, 0, :], mid_tmp[64:96, :],
                                          ALU.subtract).then_inc(s_lo, 1)
                    with dve.Fori(0, CG) as c:
                        bc = b * CG + c
                        u = bc * UNITS

                        def sum2(k):
                            q = k % 2
                            dve.wait_ge(s_s1, START + u + k + 1)
                            dve.wait_ge(s_ln, START + (u + k - 1 if k >= 2 else u))
                            dve.wait_ge(s_rec, START + (u + k - 1 if k >= 2 else u))
                            dve.tensor_tensor(s2[:, q, :], s1[:, q, :], gabs[:, q, 2, :], ALU.add).then_inc(s_s2, 1)

                        dve.wait_ge(s_h0, START + bc + 1)
                        sum2(0)
                        for k in range(UNITS):
                            t, d, q = k // NDIR, k % NDIR, k % 2
                            h_old, h_new = H[:, d, t % 2, :], H[:, d, (t + 1) % 2, :]
                            shifted = bass.AP(tensor=h_old.tensor, offset=h_old.offset,
                                              ap=[h_old.ap[0], [CHUNK, 3], [1, BANK]])
                            dve.wait_ge(s_gate, START + u + k + 1)
                            dve.wait_ge(s_abs, START + u + k + 1)
                            dve.wait_ge(s_h, START + (u + k - NDIR + 1 if k >= NDIR else u))
                            dve.wait_ge(s_n2, START + u + k)
                            dve.tensor_tensor(prod[:, :, :], ps[:, 3 * q:3 * q + 3, :], shifted, ALU.mult).then_inc(s_prod, 1)
                            dve.wait_ge(s_r0, START + u + k + 1)
                            dve.scalar_tensor_tensor(out=s2[:, q, :], in0=s2[:, q, :], scalar=GATE_EPS,
                                                     in1=r0[:, q, :], op0=ALU.add, op1=ALU.mult).then_inc(s_err, 1)
                            dve.wait_ge(s_prod, START + u + k + 1)
                            dve.wait_ge(s_h, START + u + k)
                            dve.tensor_tensor(total[:, :], prod[:, 0, :], prod[:, 1, :], ALU.add).then_inc(s_n1, 1)
                            dve.wait_ge(s_err, START + u + k + 1)
                            dve.scalar_tensor_tensor(out=r0[:, q, :], in0=s2[:, q, :], scalar=2.0,
                                                     in1=r0[:, q, :], op0=ALU.subtract,
                                                     op1=ALU.mult).then_inc(s_rec, 1)
                            dve.wait_ge(s_n1, START + u + k + 1)
                            dve.tensor_tensor(total[:, :], total[:, :], prod[:, 2, :], ALU.add).then_inc(s_n2, 1)
                            if k + 1 < UNITS:
                                sum2(k + 1)
                            dve.wait_ge(s_n2, START + u + k + 1)
                            dve.wait_ge(s_rec, START + u + k + 1)
                            dve.wait_ge(s_h, START + u + k)
                            dve.tensor_tensor(total[:, :], total[:, :], r0[:, q, :], ALU.mult).then_inc(s_q, 1)
                            dve.wait_ge(s_q, START + u + k + 1)
                            dve.wait_ge(s_lx, START + u + k + 1)
                            dve.wait_ge(s_uh, START + (u + k - NDIR - 3 if k >= 2 * NDIR else u))
                            dve.tensor_tensor(h_new[:, CHUNK:CHUNK + BANK], LX[:, q, :], total[:, :],
                                              ALU.subtract).then_inc(s_h, 1)
                    dve.wait_ge(s_yout, START + (b + 1) * (CG * CHUNK))

                    def normalise(t):
                        q = t % 2
                        dve.wait_ge(s_newt, START + b * (4 * CHUNK) + 4 * (t + 1))
                        yt = Y[:, :, t, :]
                        r = r0[:, q, :]
                        rb = bass.AP(tensor=r.tensor, offset=r.offset, ap=[r.ap[0], [0, CG], [1, BANK]])
                        dve.tensor_tensor(yt, yt, rb, ALU.mult).then_inc(s_z, 1)

                    for t in range(CHUNK):
                        q = t % 2
                        dve.wait_ge(s_mu, START + b * CHUNK + t + 1)
                        for g in range(CG):
                            dve.scalar_tensor_tensor(out=Y[:, g, t, :], in0=ps[:, q, :], scalar=-1.0 / DIN,
                                                     in1=Y[:, g, t, :], op0=ALU.mult, op1=ALU.add).then_inc(s_cen, 1)
                        dve.wait_ge(s_var, START + b * CHUNK + t + 1)
                        if t >= 2:
                            dve.wait_ge(s_newt, START + b * (4 * CHUNK) + 4 * (t - 1))
                        dve.tensor_scalar(s1[:, q, :], ps[:, 2 + q, :], 1.0 / DIN, LN0_EPS, ALU.mult,
                                          ALU.add).then_inc(s_vv, 1)
                        if t:
                            normalise(t - 1)
                    normalise(CHUNK - 1)
                    n = b * 12
                    dve.wait_ge(s_gsq, START + (b + 1) * (CG * CHUNK))
                    dve.tensor_reduce(gx[:, 0, :], gacc[:, :, :], AX_X, ALU.add).then_inc(s_grn, 1)
                    dve.wait_ge(s_gsum, START + 2 * b + 1)
                    dve.tensor_reduce(small[:, 0:1], ps[:, 4, 0:CG], AX_X, ALU.add).then_inc(s_grn, 1)
                    dve.wait_ge(s_grn, START + n + 2)
                    dve.tensor_scalar(small[:, 1:2], small[:, 0:1], 1.0 / DIN, GRN_EPS, ALU.mult,
                                      ALU.add).then_inc(s_grn, 1)
                    dve.wait_ge(s_grn, START + n + 3)
                    dve.reciprocal(small[:, 2:3], small[:, 1:2]).then_inc(s_grn, 1)
                    dve.wait_ge(s_grn, START + n + 4)
                    dve.wait_ge(s_gxr, START + b + 1)
                    dve.tensor_scalar(svec[:, 0, :], gx[:, 1, :], small[:, 2:3], None, ALU.mult).then_inc(s_grn, 1)
                    dve.wait_ge(s_grn, START + n + 5)
                    dve.tensor_tensor(svec[:, 0, :], svec[:, 0, :], vecs[:, 0, :], ALU.mult).then_inc(s_grn, 1)
                    dve.wait_ge(s_grn, START + n + 6)
                    dve.tensor_scalar(svec[:, 0, :], svec[:, 0, :], 1.0, None, ALU.add).then_inc(s_grn, 1)
                    dve.wait_ge(s_grn, START + n + 7)
                    dve.tensor_tensor(svec[:, 1, :], svec[:, 0, :], vecs[:, 2, :], ALU.mult).then_inc(s_grn, 1)
                    dve.tensor_tensor(svec[:, 2, :], svec[:, 0, :], vecs[:, 3, :], ALU.mult).then_inc(s_grn, 1)
                    dve.wait_ge(s_grn, START + n + 9)
                    dve.tensor_tensor(svec[:, 2, :], svec[:, 2, :], vecs[:, 1, :], ALU.add).then_inc(s_grn, 1)
                    for g in range(CG):
                        ins = dve.tensor_scalar(w_out_s[:, g, :], w_out[:, g, :], svec[:, 1, g:g + 1], None, ALU.mult)
                    ins.then_inc(s_grn, 1)
                    dve.wait_ge(s_gsum, START + 2 * b + 2)
                    dve.tensor_copy(b_out[:, 0:1], ps[:, 5, 0:1])
                    dve.tensor_copy(b_out[0:CH - P, 1:2], ps[0:CH - P, 4, 0:1]).then_inc(s_grn, 1)
                    dve.wait_ge(s_oproj, START + (b + 1) * NB)


def layer0_inputs(v):
    import numpy as np
    T = np.ascontiguousarray
    gates = [v["L0_conv_W_w"].reshape(3, NDIR, CG, P, PROXY)[i] for i in range(3)]
    gates += [v[f"L0_conv_W_{n}"].reshape(NDIR, CG, P, PROXY) for n in "lud"]
    wg = np.stack(gates).transpose(4, 2, 1, 0, 3).reshape(PROXY, -1)
    col = lambda a: a.reshape(CG, P).T
    mask = np.zeros((P, 3), np.float32)
    for i, part in enumerate([0, 1, 0, 1, 0, 1, 2]):
        mask[16 * i:16 * i + 16, part] = 1.0
    return {
        "x": T(v["x"].reshape(-1, CH, PIX)),
        "w_in": T(v["L0_conv_W_in"].T), "w_dw": T(v["L0_conv_W_dw"].reshape(DIN, 9)), "b_dw": T(col(v["L0_conv_b_dw"])),
        "w_proxy": T(np.tile(v["L0_conv_W_xd"].T, (1, P // PROXY))), "w_gate": T(np.tile(wg, (P // PROXY, 1))),
        "w_mix": T(np.tile(v["L0_conv_w_m"], (P, 1))), "part_mask": mask, "w_out": T(v["L0_conv_W_out"].T),
        "vecs": T(np.stack([col(v["L0_conv_" + n]) for n in ("grn_gamma", "grn_beta", "ln_w", "ln_b")], 1)),
        "ident": np.eye(P, dtype=np.float32),
    }


def layer1(nc, B, io, mid, out):
    T = BANK
    NJ = PIX // T
    NCH = B * NJ
    TT = T // P
    NS = 16
    RANK = 12
    KCONV = 4
    NM = 2
    NG = NM * CG
    UNITS = NS * CG
    DTROW = 96
    R_DA, R_U, R_H, R_P = 8, 6, 4, 4
    LEAD_A, LEAD_U = 6, 4
    Y0, ROW0, PREP0 = 0, 3, 5

    with ExitStack() as ctx:
        def sb(name, shape, dt=F32):
            return ctx.enter_context(nc.sbuf_tensor(name, shape, dt))

        sems = []

        def sem(name):
            sems.append(ctx.enter_context(nc.semaphore(name)))
            return sems[-1]

        wi_a = sb("wi_a", [P, NM, 2, CG, P])
        wi_b = sb("wi_b", [CH - P, NM, 2, CG, P])
        wc = sb("wc", [P, NG, KCONV])
        b_conv = sb("b_conv", [P, NG])
        wx = sb("wx", [P, NG, DTROW + RANK])
        wdt = sb("wdt", [P, NG, P])
        bdt = sb("bdt", [P, NG])
        A = sb("A", [P, NG, NS])
        Dv = sb("Dv", [P, NG])
        diag_d = sb("diag_d", [P, NG, P])
        wo = sb("wo", [P, NG, CH])
        sel = sb("sel", [P, 2 * NS, P], BF16)
        ln_gb = sb("ln_gb", [P, 2, CH])
        keep = sb("keep", [P, NCH])
        ident = sb("ident1", [P, P])
        tok = sb("tok", [P, TT, CH])
        xs = sb("xs", [P, TT, CH])
        resid = sb("resid", [P, TT, CH])
        stats = sb("stats", [P, TT, 6])
        mv = sb("mv", [P, TT, 2])
        vr = sb("vr", [P, 3, TT])
        xt_a = sb("xt_a", [P, T])
        xt_b = sb("xt_b", [CH - P, T])
        raw = sb("raw", [P, CG, T + KCONV])
        halo = sb("halo", [P, NG, KCONV])
        xc = sb("xc", [P, NG, T])
        dt = sb("dt", [P, NG, T])
        dtx = sb("dtx", [P, NG, T])
        yz = sb("yz", [P, NG, T])
        zs = sb("zs", [P, NG, T])
        S = sb("S1", [P, NM, T], BF16)
        rest = sb("rest", [P, T])
        midt = sb("midt", [P, T], BF16)
        dtl = sb("dtl", [P, NM, T])
        w1 = sb("w1", [P, 2, T])
        c1 = sb("c1", [P, 2, T])
        vmax = sb("vmax", [P, 2, T])
        lnw = sb("lnw", [P, 2, T])
        last = sb("last", [P, NG, NS])
        dA = sb("dA", [P, R_DA, T])
        u = sb("u", [P, R_U, T])
        h = sb("h", [P, R_H, T])
        p = sb("p", [P, R_P, T])
        bb = sb("bb", [P, 2, T])
        cb = sb("cb", [P, 2, T])
        o = sb("o", [P, 2, CH])

        ps = ctx.enter_context(nc.psum_tensor("ps1", [P, 8, BANK], F32))

        s_w = sem("t_w")
        s_passed = sem("t_passed")
        s_set = sem("t_set")
        s_zero = sem("t_zero")
        s_tok = sem("t_tok")
        s_ln = sem("t_ln")
        s_lr = sem("t_lr")
        s_gb = sem("t_gb")
        s_tr = sem("t_tr")
        s_xt = sem("t_xt")
        s_rs = sem("t_rs")
        s_kp = sem("t_kp")
        s_in = sem("t_in")
        s_raw = sem("t_raw")
        s_conv = sem("t_conv")
        s_xc = sem("t_xc")
        s_z = sem("t_z")
        s_zs = sem("t_zs")
        s_xp = sem("t_xp")
        s_hi = sem("t_hi")
        s_res = sem("t_res")
        s_mid = sem("t_mid")
        s_lo = sem("t_lo")
        s_dtp = sem("t_dtp")
        s_abs = sem("t_abs")
        s_e = sem("t_e")
        s_l = sem("t_l")
        s_max = sem("t_max")
        s_w1 = sem("t_w1")
        s_dt = sem("t_dt")
        s_dtx = sem("t_dtx")
        s_row = [sem("t_row_b"), sem("t_row_c")]
        s_rows = [sem("t_rows_b"), sem("t_rows_c")]
        s_da = sem("t_da")
        s_u = sem("t_u")
        s_scan = sem("t_scan")
        s_last = sem("t_last")
        s_p = sem("t_p")
        s_y = sem("t_y")
        s_yz = sem("t_yz")
        s_op = sem("t_op")
        s_o = sem("t_o")
        s_st = [sem("t_st0"), sem("t_st1")]

        NLOADS = 16

        def waits_passed(eng):
            eng.sem_inc(s_passed, 1)

        def is_last(s):
            return isinstance(s, int) and s == 2 * NCH - 1

        def ahead(s, m, k, lead):
            if k + lead < UNITS:
                return s, m, k + lead
            return None if is_last(s) else (s + 1, 1 - m, k + lead - UNITS)

        def run(stage, prepare, finish, eng, begin=lambda: None):
            for k in range(UNITS):
                prepare(k, 0, 0, 0)
            begin()
            stage(0, 0, 0, None)
            with eng.Fori(0, NCH - 1) as c:
                stage(2 * c + 1, 1, c, None)
                stage(2 * c + 2, 0, c + 1, c)
            stage(2 * NCH - 1, 1, NCH - 1, None)
            finish()

        with nc.Block() as block:
            @block.sync
            def _(sp):
                loads = [
                    (wi_a[:, :, :, :, :].rearrange("p a b c d -> p (a b c d)"), io["wi"][0:P, :]),
                    (wi_b[:, :, :, :, :].rearrange("p a b c d -> p (a b c d)"), io["wi"][P:CH, :]),
                    (wc[:, :, :], io["wc"].rearrange("(g p) k -> p g k", p=P)),
                    (b_conv[:, :], io["bc"]), (bdt[:, :], io["bdt"]), (Dv[:, :], io["D"]),
                    (wx[:, :, :], io["wx"].rearrange("(g p) m -> p g m", p=P)),
                    (wdt[DTROW:DTROW + RANK, :, :], io["wdt"].rearrange("r (g m) -> r g m", g=NG)),
                    (A[:, :, :], io["A_log"].rearrange("(g p) n -> p g n", p=P)),
                    (wo[:, :, :], io["wo"].rearrange("(g p) m -> p g m", p=P)),
                    (ln_gb[:, 0, :], io["ln_g"]), (ln_gb[:, 1, :], io["ln_b"]),
                    (ident[:, :], io["ident"]), (keep[:, :], io["keep"][:, 0:NCH]),
                    (xc[:, 0:4, :].rearrange("p g n -> p (g n)"), io["sel"][:, 0:4 * T]),
                    (dt[:, 0:4, :].rearrange("p g n -> p (g n)"), io["sel"][:, 4 * T:8 * T]),
                ]
                assert len(loads) == NLOADS
                for dst, src in loads:
                    sp.dma_start(dst, src).then_inc(s_w, 16)
                tokens = mid.rearrange("b c n -> (b c n)").rearrange("(j i p c) -> j p i c", i=TT, p=P, c=CH)
                stored = out.rearrange("b c n -> (b c n)").rearrange("(j i p c) -> j i p c", i=TT, p=P, c=CH)

                def store(c):
                    for i in range(TT):
                        sp.wait_ge(s_o, START + TT * c + i + 1)
                        sp.dma_start(stored[c, i], o[:, i % 2, :]).then_inc(s_st[i % 2], 16)

                sp.dma_start(tok[:, :, :], tokens[0]).then_inc(s_tok, 16)
                sp.wait_ge(s_ln, START + 8)
                sp.dma_start(tok[:, :, :], tokens[1]).then_inc(s_tok, 16)
                with sp.Fori(0, NCH - 2) as c:
                    sp.wait_ge(s_ln, START + 8 * c + 16)
                    sp.dma_start(tok[:, :, :], tokens[c + 2]).then_inc(s_tok, 16)
                    store(c)
                store(NCH - 2)
                store(NCH - 1)
                for s in s_st:
                    sp.wait_ge(s, START + NCH * (TT // 2) * 16)

            @block.gpsimd
            def _(pool):
                for s in sems:
                    pool.sem_inc(s, START)
                pool.memset(last[:, :, :], 0.0).then_inc(s_zero, 1)
                pool.memset(halo[:, :, :], 0.0).then_inc(s_zero, 1)
                pool.wait_ge(s_w, START + 16 * NLOADS)

                def prepare(k, r, m, c):
                    if m == 0 and k in (5, 6):
                        v = ln_gb[:, k - 5, :]
                        over_tokens = bass.AP(tensor=v.tensor, offset=v.offset, ap=[v.ap[0], [0, TT], [1, CH]])
                        if k == 5:
                            pool.wait_ge(s_ln, START + 8 * c + 8)
                            pool.tensor_tensor(xs[:, :, :], xs[:, :, :], over_tokens, ALU.mult).then_inc(s_gb, 1)
                        else:
                            pool.wait_ge(s_gb, START + 2 * c + 1)
                            pool.tensor_tensor(xs[:, :, :], xs[:, :, :], over_tokens, ALU.add).then_inc(s_gb, 1)
                    if k in (30, 32, 35):
                        g = (30, 32, 35).index(k)
                        q, n = g % 2, 3 * r + g
                        e = dt[:, m * CG + g, :]
                        pool.wait_ge(s_e, START + n + 1)
                        pool.wait_ge(s_l, START + n - 1)
                        pool.wait_ge(s_dt, START + n - 1)
                        waits_passed(pool)
                        pool.tensor_scalar(w1[:, q, :], e, 1.0, 1.0, ALU.mult, ALU.add).then_inc(s_w1, 1)
                        pool.wait_ge(s_w1, START + 4 * n + 1)
                        waits_passed(pool)
                        pool.tensor_scalar(c1[:, q, :], w1[:, q, :], 1.0, -1.0, ALU.mult, ALU.add).then_inc(s_w1, 1)
                        pool.wait_ge(s_w1, START + 4 * n + 2)
                        pool.tensor_tensor(c1[:, q, :], c1[:, q, :], e, ALU.subtract).then_inc(s_w1, 1)
                        pool.wait_ge(s_w1, START + 4 * n + 3)
                        pool.wait_ge(s_max, START + n + 1)
                        pool.tensor_tensor(c1[:, q, :], vmax[:, q, :], c1[:, q, :], ALU.subtract).then_inc(s_w1, 1)
                    if k in (37, 39, 41):
                        g = (k - 37) // 2
                        pool.wait_ge(s_dt, START + 3 * r + g + 1)
                        pool.tensor_tensor(dtx[:, m * CG + g, :], dt[:, m * CG + g, :], xc[:, m * CG + g, :],
                                           ALU.mult).then_inc(s_dtx, 1)

                def times_b(s, m, k):
                    n, g = k // CG, k % CG
                    if k == 0:
                        pool.wait_ge(s_dtx, START + CG * s + CG)
                    pool.wait_ge(s_rows[0], START + NS * s + n + 1)
                    pool.wait_ge(s_scan, START + UNITS * s + k + 1 - R_U)
                    pool.tensor_tensor(u[:, k % R_U, :], dtx[:, m * CG + g, :], bb[:, n % 2, :],
                                       ALU.mult).then_inc(s_u, 1)

                def stage(s, m, c, done):
                    for k in range(UNITS):
                        unit = ahead(s, m, k, LEAD_U)
                        if unit:
                            times_b(*unit)
                        if not is_last(s):
                            prepare(k, s + 1, 1 - m, c + m)

                def begin():
                    for k in range(LEAD_U):
                        times_b(0, 0, k)

                run(stage, prepare, lambda: None, pool, begin)

            @block.tensor
            def _(pe):
                pe.wait_ge(s_w, START + 16 * NLOADS)
                pe.wait_ge(s_set, START + 4)

                def in_proj(m, part, g):
                    pe.matmul(ps[:, PREP0 + g, :], wi_a[:, m, part, g, :], xt_a[:, :], start=True, stop=False)
                    return pe.matmul(ps[:, PREP0 + g, :], wi_b[:, m, part, g, :], xt_b[:, :], start=False, stop=True)

                def prepare(k, r, m, c):
                    if m == 0 and k == 8:
                        pe.wait_ge(s_gb, START + 2 * c + 2)
                        pe.wait_ge(s_max, START + CG * r)
                        for i in range(TT):
                            pe.transpose(ps[:, PREP0, i * P:(i + 1) * P], xs[:, i, 0:P], ident[:, :])
                            mm = pe.transpose(ps[0:CH - P, PREP0 + 1, i * P:(i + 1) * P], xs[:, i, P:CH], ident[:, :])
                        mm.then_inc(s_tr, 1)
                    if k in (10, 12, 14):
                        g = (k - 10) // 2
                        if m == 0:
                            pe.wait_ge(s_xt, START + 2 * c + 2)
                        else:
                            pe.wait_ge(s_o, START + TT * c)
                        pe.wait_ge(s_max, START + CG * r)
                        in_proj(m, 0, g).then_inc(s_in, 1)
                    if k in (18, 19, 20):
                        g = k - 18
                        pe.wait_ge(s_raw, START + CG * r + g + 1)
                        in_proj(m, 1, g).then_inc(s_z, 1)
                    if k == 24:
                        pe.wait_ge(s_xc, START + CG * r + CG)
                        pe.wait_ge(s_zs, START + CG * r + 1)
                        for g in range(CG):
                            mm = pe.matmul(ps[0:DTROW + RANK, PREP0, :], wx[:, m * CG + g, :], xc[:, m * CG + g, :],
                                           start=g == 0, stop=g == CG - 1)
                        mm.then_inc(s_xp, 1)
                    if k in (26, 27, 29):
                        g = (26, 27, 29).index(k)
                        pe.wait_ge(s_hi, START + 2 * r + 2)
                        pe.wait_ge(s_zs, START + CG * r + CG)
                        if g == 2:
                            pe.wait_ge(s_res, START + r + 1)
                        pe.matmul(ps[:, PREP0 + (g + 1) % 3, :], wdt[DTROW:DTROW + RANK, m * CG + g, :],
                                  dtl[DTROW:DTROW + RANK, m, :], start=True, stop=True).then_inc(s_dtp, 1)

                def row(s, m, k, is_c):
                    n = k // CG
                    if n == 0:
                        pe.wait_ge(s_lo, START + s + 1)
                        pe.wait_ge(s_mid, START + 2 * s + 2)
                    pe.wait_ge(s_rows[is_c], START + NS * s + n)
                    pe.matmul(ps[:, ROW0 + is_c, :], sel[0:DTROW, 2 * n + is_c, :], S[0:DTROW, m, :],
                              start=True, stop=True).then_inc(s_row[is_c], 1)

                def output(c, i):
                    if i == 0:
                        pe.wait_ge(s_yz, START + NG * (c + 1))
                    pe.wait_ge(s_max, START + NG * (c + 1))
                    pe.wait_ge(s_o, START + TT * c + i - 2)
                    for g in range(NG):
                        mm = pe.matmul(ps[:, PREP0 + i % 3, 0:CH], yz[:, g, i * P:(i + 1) * P], wo[:, g, :],
                                       start=g == 0, stop=g == NG - 1)
                    mm.then_inc(s_op, 1)

                def stage(s, m, c, done):
                    um = UNITS * s

                    def add_y(k):
                        g = k % CG
                        pe.wait_ge(s_p, START + um + k + 1)
                        pe.matmul(ps[:, Y0 + g, :], ident[:, :], p[:, k % R_P, :], start=False,
                                  stop=k // CG == NS - 1).then_inc(s_y, 1)

                    for k in range(UNITS):
                        if k % CG < 2:
                            unit = ahead(s, m, k - k % CG, CG * (2 - k % CG))
                            if unit:
                                row(*unit, k % CG)
                        if not is_last(s):
                            prepare(k, s + 1, 1 - m, c + m)
                        if done is not None and k in (2, 4, 6, 8):
                            output(done, k // 2 - 1)
                        if k == 2:
                            for g in range(CG):
                                pe.wait_ge(s_yz, START + CG * s)
                                pe.matmul(ps[:, Y0 + g, :], diag_d[:, m * CG + g, :], xc[:, m * CG + g, :],
                                          start=True, stop=False)
                        if k >= 2:
                            add_y(k - 2)
                    add_y(UNITS - 2)
                    add_y(UNITS - 1)

                def finish():
                    for i in range(TT):
                        output(NCH - 1, i)

                def begin():
                    row(0, 0, 0, 0)
                    row(0, 0, 0, 1)
                    row(0, 0, CG, 0)

                run(stage, prepare, finish, pe, begin)

            @block.scalar
            def _(act):
                act.wait_ge(s_w, START + 16 * NLOADS)
                act.preload_act_table_set("natural_log_exp_and_others")
                act.activation(A[:, :, :], A[:, :, :], ACT.Exp).then_inc(s_set, 1)
                act.wait_ge(s_set, START + 4)

                def prepare(k, r, m, c):
                    if m == 0 and k == 2:
                        act.wait_ge(s_ln, START + 8 * c + 3)
                        act.activation(vr[:, 1, :], vr[:, 0, :], ACT.Ln).then_inc(s_lr, 1)
                        act.wait_ge(s_lr, START + 2 * c + 1)
                        act.activation(vr[:, 1, :], vr[:, 1, :], ACT.Exp, scale=-0.5).then_inc(s_lr, 1)
                    if m == 0 and k == 9:
                        act.wait_ge(s_tr, START + c + 1)
                        act.wait_ge(s_z, START + CG * r)
                        act.activation(xt_a[:, :], ps[:, PREP0, :], ACT.Copy).then_inc(s_xt, 1)
                        act.activation(xt_b[:, :], ps[0:CH - P, PREP0 + 1, :], ACT.Copy).then_inc(s_xt, 1)
                    if k in (11, 13, 15):
                        g = (k - 11) // 2
                        act.wait_ge(s_in, START + CG * r + g + 1)
                        act.wait_ge(s_conv, START + 6 * CG * r)
                        act.activation(raw[:, g, KCONV - 1:KCONV - 1 + T], ps[:, PREP0 + g, :],
                                       ACT.Copy).then_inc(s_raw, 1)
                    if k == 22:
                        for g in range(CG):
                            act.wait_ge(s_conv, START + 6 * (CG * r + g) + 5)
                            act.activation(xc[:, m * CG + g, :], xc[:, m * CG + g, :], ACT.Silu).then_inc(s_xc, 1)
                        for g in range(CG):
                            act.wait_ge(s_z, START + CG * r + g + 1)
                            act.wait_ge(s_yz, START + CG * (r - 1))
                            act.activation(zs[:, m * CG + g, :], ps[:, PREP0 + g, :], ACT.Silu).then_inc(s_zs, 1)
                        act.preload_act_table_set("natural_log_exp_and_others")
                    if k == 25:
                        act.wait_ge(s_xp, START + r + 1)
                        act.activation(S[0:DTROW, m, :], ps[0:DTROW, PREP0, :], ACT.Copy).then_inc(s_hi, 1)
                        act.activation(dtl[DTROW:DTROW + RANK, m, :], ps[DTROW:DTROW + RANK, PREP0, :],
                                       ACT.Copy).then_inc(s_hi, 1)
                    if k == 27:
                        act.wait_ge(s_res, START + r + 1)
                        act.activation(midt[0:DTROW, :], rest[0:DTROW, :], ACT.Copy).then_inc(s_mid, 1)
                        act.wait_ge(s_mid, START + 2 * r + 1)
                        act.activation(S[32:64, m, :], midt[32:64, :], ACT.Copy).then_inc(s_mid, 1)
                    if k in (28, 30, 32):
                        g = (k - 28) // 2
                        n, e = CG * r + g, dt[:, m * CG + g, :]
                        act.wait_ge(s_dtp, START + n + 1)
                        act.activation(e, ps[:, PREP0 + (g + 1) % 3, :], ACT.Abs,
                                       bias=bdt[:, m * CG + g:m * CG + g + 1]).then_inc(s_abs, 1)
                        act.wait_ge(s_abs, START + n + 1)
                        act.activation(e, e, ACT.Exp, scale=-1.0).then_inc(s_e, 1)
                    if k in (31, 33, 36):
                        g = (31, 33, 36).index(k)
                        n = CG * r + g
                        act.wait_ge(s_w1, START + 4 * n + 1)
                        act.wait_ge(s_dt, START + n - 1)
                        act.activation(lnw[:, g % 2, :], w1[:, g % 2, :], ACT.Ln).then_inc(s_l, 1)

                def row_out(s, m, k, is_c):
                    n = k // CG
                    act.wait_ge(s_row[is_c], START + NS * s + n + 1)
                    act.wait_ge(s_p if is_c else s_u, START + UNITS * s + k - CG)
                    act.activation((cb if is_c else bb)[:, n % 2, :], ps[:, ROW0 + is_c, :],
                                   ACT.Copy).then_inc(s_rows[is_c], 1)

                def decay(s, m, k):
                    n, g = k // CG, k % CG
                    if k == 0:
                        act.wait_ge(s_dt, START + CG * s + CG)
                    act.wait_ge(s_scan, START + UNITS * s + k + 1 - R_DA)
                    act.activation(dA[:, k % R_DA, :], dt[:, m * CG + g, :], ACT.Exp,
                                   scale=A[:, m * CG + g, n:n + 1]).then_inc(s_da, 1)

                def stage(s, m, c, done):
                    um = UNITS * s

                    def keep_last(k):
                        n, g = k // CG, k % CG
                        act.wait_ge(s_scan, START + um + k + 1)
                        act.activation(last[:, m * CG + g, n:n + 1], h[:, k % R_H, T - 1:T], ACT.Copy)\
                           .then_inc(s_last, 1)

                    for k in range(UNITS):
                        unit = ahead(s, m, k, LEAD_A)
                        if unit:
                            decay(*unit)
                        if k >= 3:
                            keep_last(k - 3)
                        if k % CG:
                            unit = ahead(s, m, k - k % CG, CG * (3 - k % CG))
                            if unit:
                                row_out(*unit, k % CG - 1)
                        if m == 0 and k == 21:
                            act.wait_ge(s_o, START + TT * c)
                            act.activation(resid[:, :, :], xs[:, :, :], ACT.Copy).then_inc(s_rs, 1)
                        if not is_last(s):
                            prepare(k, s + 1, 1 - m, c + m)
                    for k in range(UNITS - 3, UNITS):
                        keep_last(k)

                def begin():
                    row_out(0, 0, 0, 0)
                    row_out(0, 0, 0, 1)
                    row_out(0, 0, CG, 0)
                    for k in range(LEAD_A):
                        decay(0, 0, k)

                run(stage, prepare, lambda: None, act, begin)

            @block.vector
            def _(dve):
                dve.wait_ge(s_w, START + 16 * NLOADS)
                for i, src in enumerate((xc, dt)):
                    ins = dve.tensor_copy(sel[:, i * NS:(i + 1) * NS, :].rearrange("p i m -> p (i m)"),
                                          src[:, 0:4, :].rearrange("p g n -> p (g n)"))
                ins.then_inc(s_set, 1)
                for g in range(NG):
                    ins = dve.tensor_scalar(diag_d[:, g, :], ident[:, :], Dv[:, g:g + 1], None, ALU.mult)
                ins.then_inc(s_set, 1)
                dve.wait_ge(s_set, START + 3)
                dve.tensor_scalar(A[:, :, :], A[:, :, :], -1.0, None, ALU.mult).then_inc(s_set, 1)
                dve.wait_ge(s_zero, START + 2)

                def prepare(k, r, m, c):
                    l = START + 8 * c
                    if m == 0 and k == 0:
                        dve.wait_ge(s_tok, START + 16 * c + 16)
                        for i in range(TT):
                            ins = dve.bn_stats(stats[:, i, :], tok[:, i, :])
                        ins.then_inc(s_ln, 1)
                    if m == 0 and k == 1:
                        dve.wait_ge(s_ln, l + 1)
                        waits_passed(dve)
                        for i in range(TT):
                            ins = dve.bn_aggr(mv[:, i, :], stats[:, i, :])
                        ins.then_inc(s_ln, 1)
                        dve.wait_ge(s_ln, l + 2)
                        dve.tensor_scalar(vr[:, 0, :], mv[:, :, 1], LN1_EPS, None, ALU.add).then_inc(s_ln, 1)
                    if m == 0 and k == 3:
                        dve.wait_ge(s_lr, START + 2 * c + 2)
                        dve.tensor_tensor(vr[:, 2, :], vr[:, 0, :], vr[:, 1, :], ALU.mult).then_inc(s_ln, 1)
                        dve.wait_ge(s_ln, l + 4)
                        dve.tensor_tensor(vr[:, 2, :], vr[:, 2, :], vr[:, 1, :], ALU.mult).then_inc(s_ln, 1)
                        dve.wait_ge(s_ln, l + 5)
                        dve.tensor_scalar(vr[:, 2, :], vr[:, 2, :], -0.5, 1.5, ALU.mult, ALU.add).then_inc(s_ln, 1)
                        dve.wait_ge(s_ln, l + 6)
                        dve.tensor_tensor(vr[:, 1, :], vr[:, 2, :], vr[:, 1, :], ALU.mult).then_inc(s_ln, 1)
                    if m == 0 and k == 4:
                        dve.wait_ge(s_ln, l + 7)
                        dve.wait_ge(s_rs, START + c)
                        dve.wait_ge(s_tr, START + c)
                        for i in range(TT):
                            ins = dve.tensor_scalar(xs[:, i, :], tok[:, i, :], mv[:, i, 0:1], vr[:, 1, i:i + 1],
                                                    ALU.subtract, ALU.mult)
                        ins.then_inc(s_ln, 1)
                    if k == 5:
                        mine = slice(m * CG, (m + 1) * CG)
                        f = keep[:, c:c + 1] if isinstance(c, int) else keep[:, bass.ds(c, 1)]
                        dve.tensor_scalar(last[:, mine, :], last[:, mine, :], f, None, ALU.mult).then_inc(s_kp, 1)
                        dve.tensor_scalar(halo[:, mine, :], halo[:, mine, :], f, None, ALU.mult).then_inc(s_kp, 1)
                    if 12 <= k < 21:
                        g, part = (k - 12) // 3, (k - 12) % 3
                        n = START + 6 * (CG * r + g)
                        x_raw, x, gg = raw[:, g, :], xc[:, m * CG + g, :], m * CG + g

                        def tap(i):
                            dve.wait_ge(s_conv, n + i + 1)
                            dve.scalar_tensor_tensor(out=x, in0=x_raw[:, i:i + T], scalar=wc[:, gg, i:i + 1], in1=x,
                                                     op0=ALU.mult, op1=ALU.add).then_inc(s_conv, 1)

                        if part == 0:
                            dve.wait_ge(s_raw, START + CG * r + g + 1)
                            dve.wait_ge(s_kp, START + 2 * r + 2)
                            dve.tensor_copy(x_raw[:, 0:KCONV - 1], halo[:, gg, 0:KCONV - 1]).then_inc(s_conv, 1)
                            dve.wait_ge(s_conv, n + 1)
                            dve.tensor_scalar(x, x_raw[:, 0:T], wc[:, gg, 0:1], b_conv[:, gg:gg + 1], ALU.mult,
                                              ALU.add).then_inc(s_conv, 1)
                        elif part == 1:
                            tap(1)
                        else:
                            tap(2)
                            tap(3)
                            dve.tensor_copy(halo[:, gg, 0:KCONV - 1], x_raw[:, T:T + KCONV - 1]).then_inc(s_conv, 1)
                    if k == 26:
                        dve.wait_ge(s_hi, START + 2 * r + 2)
                        dve.tensor_tensor(rest[0:DTROW, :], ps[0:DTROW, PREP0, :], S[0:DTROW, m, :],
                                          ALU.subtract).then_inc(s_res, 1)
                    if k == 28:
                        dve.wait_ge(s_mid, START + 2 * r + 1)
                        dve.wait_ge(s_res, START + r + 1)
                        dve.tensor_tensor(S[64:96, m, :], rest[64:96, :], midt[64:96, :],
                                          ALU.subtract).then_inc(s_lo, 1)
                    if k in (29, 31, 33):
                        g = (k - 29) // 2
                        n = CG * r + g
                        dve.wait_ge(s_abs, START + n + 1)
                        dve.wait_ge(s_w1, START + 4 * (n - 1))
                        dve.tensor_scalar(vmax[:, g % 2, :], ps[:, PREP0 + (g + 1) % 3, :],
                                          bdt[:, m * CG + g:m * CG + g + 1], 0.0, ALU.add, ALU.max).then_inc(s_max, 1)
                    if k in (34, 36, 39):
                        g = (34, 36, 39).index(k)
                        n = CG * r + g
                        dve.wait_ge(s_l, START + n + 1)
                        dve.wait_ge(s_w1, START + 4 * n + 4)
                        dve.tensor_tensor(dt[:, m * CG + g, :], c1[:, g % 2, :], lnw[:, g % 2, :],
                                          ALU.add).then_inc(s_dt, 1)

                def gate(s, m):
                    dve.wait_ge(s_y, START + UNITS * (s + 1))
                    for g in range(CG):
                        gg = m * CG + g
                        dve.tensor_tensor(yz[:, gg, :], ps[:, Y0 + g, :], zs[:, gg, :], ALU.mult).then_inc(s_yz, 1)

                def output(c, i):
                    dve.wait_ge(s_op, START + TT * c + i + 1)
                    dve.wait_ge(s_rs, START + c + 1)
                    dve.wait_ge(s_st[i % 2], START + 16 * (TT // 2 * c + i // 2))
                    dve.tensor_tensor(o[:, i % 2, :], ps[:, PREP0 + i % 3, 0:CH], resid[:, i, :],
                                      ALU.add).then_inc(s_o, 1)

                def stage(s, m, c, done):
                    um = UNITS * s

                    def times_c(k):
                        n = k // CG
                        dve.wait_ge(s_scan, START + um + k + 1)
                        dve.wait_ge(s_rows[1], START + NS * s + n + 1)
                        dve.wait_ge(s_y, START + um + k + 1 - R_P)
                        dve.tensor_tensor(p[:, k % R_P, :], h[:, k % R_H, :], cb[:, n % 2, :],
                                          ALU.mult).then_inc(s_p, 1)

                    for k in range(UNITS):
                        n, g = k // CG, k % CG
                        if k == 0:
                            dve.wait_ge(s_kp, START + 2 * s + 2)
                        dve.wait_ge(s_da, START + um + k + 1)
                        dve.wait_ge(s_u, START + um + k + 1)
                        dve.wait_ge(s_last, START + um + k + 1 - R_H)
                        dve.tensor_tensor_scan(h[:, k % R_H, :], dA[:, k % R_DA, :], u[:, k % R_U, :],
                                               last[:, m * CG + g, n:n + 1], ALU.mult, ALU.add).then_inc(s_scan, 1)
                        if k:
                            times_c(k - 1)
                        if k == 1 and not (isinstance(s, int) and s == 0):
                            gate(s - 1, 1 - m)
                        if done is not None and k in (3, 5, 7, 9):
                            output(done, (k - 3) // 2)
                        if not is_last(s):
                            prepare(k, s + 1, 1 - m, c + m)
                    times_c(UNITS - 1)

                def finish():
                    gate(2 * NCH - 1, 1)
                    for i in range(TT):
                        output(NCH - 1, i)

                run(stage, prepare, finish, dve)


def layer1_inputs(v):
    import numpy as np
    T = np.ascontiguousarray
    w = lambda m, n: v[f"L1_conv_m{m}_{n}"]
    wi = np.concatenate([w(1, "in_w").T, w(2, "in_w").T[::-1]], 1)
    col = lambda n: T(np.concatenate([w(1, n), w(2, n)]).reshape(2 * CG, P).T)
    xw = [np.concatenate([w(m, "x_w").T[:, 12:]] * 3 + [w(m, "x_w").T[:, :12]], 1) for m in (1, 2)]
    both = lambda n: T(np.concatenate([w(1, n), w(2, n)]))
    sel = np.zeros((P, 32, P), np.float32)
    for i in range(32):
        for part in range(3):
            sel[32 * part + 16 * (i % 2) + i // 2, i, :] = 1.0
    keep = np.ones((P, PIX // BANK * v["x"].shape[0]), np.float32)
    keep[:, ::PIX // BANK] = 0.0
    return {
        "wi": T(wi), "wc": both("conv_w"), "bc": col("conv_b"), "wx": T(np.concatenate(xw)),
        "wdt": T(np.concatenate([w(1, "dt_w").T, w(2, "dt_w").T], 1)), "bdt": col("dt_b"),
        "A_log": both("A_log"), "D": col("D"), "wo": T(np.concatenate([w(1, "out_w").T, w(2, "out_w").T])),
        "ln_g": T(np.tile(v["L1_conv_ln_g"], (P, 1))), "ln_b": T(np.tile(v["L1_conv_ln_b"], (P, 1))),
        "keep": keep, "ident": np.eye(P, dtype=np.float32), "sel": sel.reshape(P, 32 * P),
    }


def program(nc, B, io):
    mid = nc.dram_tensor("mid_dram", [B, CH, PIX], F32, kind="Internal").ap()
    layer0(nc, B, io["layer0"], mid)
    layer1(nc, B, io["layer1"], mid, io["out"])


def kernel(**inputs):
    import numpy as _np
    import concourse.bacc as _bacc
    from concourse import mybir as _mybir
    from concourse.bass_utils import run_bass_kernel_spmd as _run

    nc = _bacc.Bacc("TRN2", target_bir_lowering=False, num_devices=1)
    v = {k: _np.asarray(a) for k, a in inputs.items()}
    B = v["x"].shape[0]
    arrays, io = {}, {}
    for layer, made in (("layer0", layer0_inputs(v)), ("layer1", layer1_inputs(v))):
        io[layer] = {}
        for name, a in made.items():
            full = f"{layer}_{name}_dram"
            arrays[full] = a
            io[layer][name] = nc.dram_tensor(full, list(a.shape), _mybir.dt.from_np(a.dtype), kind="ExternalInput").ap()
    io["out"] = nc.dram_tensor("out_dram", [B, CH, PIX], F32, kind="ExternalOutput").ap()
    program(nc, B, io)
    r = _run(nc, [arrays], core_ids=[0])
    return r.results[0]["out_dram"].reshape(v["x"].shape)
```

```python
from contextlib import ExitStack

import concourse.bass as bass
from concourse import mybir
from concourse.alu_op_type import AluOpType as ALU

ACT = mybir.ActivationFunctionType
F32 = mybir.dt.float32
BF16 = mybir.dt.bfloat16
AX_X = mybir.AxisListType.X

P = 128
BANK = 512
CH = 192
DIN = 384
CG = DIN // P
SIDE = 64
PIX = SIDE * SIDE
CHUNK = 8
NDIR = 4
PROXY = 16
NGATE = 6
START = 32
LN0_EPS, GRN_EPS, GATE_EPS, LN1_EPS = 1e-5, 1e-6, 1e-7, 1e-5


def layer0(nc, B, io, mid):
    UNITS = CHUNK * NDIR
    MIX = UNITS - NDIR
    SUMB, LUDB, YB = 3, 5, 7
    ROWS = BANK // SIDE
    NB = PIX // BANK
    PADW = SIDE + 2
    PE_BANDS = 2
    DVE_ROWS = SIDE - PE_BANDS * ROWS

    with ExitStack() as ctx:
        def sb(name, shape, dt=F32):
            return ctx.enter_context(nc.sbuf_tensor(name, shape, dt))

        sems = []

        def sem(name):
            sems.append(ctx.enter_context(nc.semaphore(name)))
            return sems[-1]

        w_in_a = sb("w_in_a", [P, DIN])
        w_in_b = sb("w_in_b", [CH - P, DIN])
        w_dw = sb("w_dw", [P, CG, 9])
        b_dw = sb("b_dw", [P, CG])
        w_proxy = sb("w_proxy", [P, CG, P])
        w_gate = sb("w_gate", [P, CG, NDIR, NGATE, P], BF16)
        w_mix = sb("w_mix", [P, NDIR])
        part_mask = sb("part_mask", [P, 3])
        w_out = sb("w_out", [P, CG, CH])
        vecs = sb("vecs", [P, 4, CG])
        ident = sb("ident", [P, P])
        ones = sb("ones", [P, P])
        epsv = sb("epsv", [P, 2])
        X = sb("X", [P, CG, PIX])
        S = sb("S", [P, CHUNK, BANK], BF16)
        Y = sb("Y", [P, CG, CHUNK, BANK])
        pad = Y[:, :, :, :].rearrange("p a b c -> p (a b c)")[:, 0:2 * PADW * PADW].rearrange(
            "p (n h w) -> p n h w", n=2, h=PADW)
        w_tmp = X[:, :, :].rearrange("p a b -> p (a b)")
        gabs = sb("gabs", [P, 2, 3, BANK])
        lud = sb("lud", [P, 8, BANK])
        s1 = sb("s1", [P, 2, BANK])
        s2 = sb("s2", [P, 2, BANK])
        r0 = sb("r0", [P, 2, BANK])
        prod = sb("prod", [P, 3, BANK])
        total = sb("total", [P, BANK])
        x_a = lud[:, 0:4, :]
        x_b = lud[0:CH - P, 4:8, :]
        w_out_s = prod[:, :, :].rearrange("p a b -> p (a b)")[:, 0:CG * CH].rearrange("p (g m) -> p g m", g=CG)
        LX = sb("LX", [P, 2, BANK])
        DX = sb("DX", [P, 2, BANK])
        UH = sb("UH", [P, 2, BANK])
        HP = BANK + 2 * CHUNK
        H = sb("H", [P, NDIR, 2, HP])
        gacc = sb("gacc", [P, CG, CHUNK])
        gx = sb("gx", [P, 2, CG])
        small = sb("small", [P, 8])
        svec = sb("svec", [P, 3, CG])
        b_out = sb("b_out", [P, 2])

        ps = ctx.enter_context(nc.psum_tensor("ps0", [P, 8, BANK], F32))

        s_w = sem("s_w")
        s_passed = sem("s_passed")
        s_const = sem("s_const")
        s_wsplit = sem("s_wsplit")
        s_x = [sem("s_x0"), sem("s_x1")]
        s_win = sem("s_win")
        s_pad = sem("s_pad")
        s_border = sem("s_border")
        s_diag = sem("s_diag")
        s_conv = sem("s_conv")
        s_band = sem("s_band")
        s_bandx = sem("s_bandx")
        s_prox = sem("s_prox")
        s_hi = sem("s_hi")
        s_res = sem("s_res")
        s_mid = sem("s_mid")
        s_lo = sem("s_lo")
        s_gate = sem("s_gate")
        s_lud = sem("s_lud")
        s_y = sem("s_y")
        s_acc = sem("s_acc")
        s_abs = sem("s_abs")
        s_ludsb = sem("s_ludsb")
        s_ln = sem("s_ln")
        s_r0 = sem("s_r0")
        s_yout = sem("s_yout")
        s_s1 = sem("s_s1")
        s_lx = sem("s_lx")
        s_dx = sem("s_dx")
        s_lud0 = sem("s_lud0")
        s_u0 = sem("s_u0")
        s_dx0 = sem("s_dx0")
        s_uh = sem("s_uh")
        s_s2 = sem("s_s2")
        s_err = sem("s_err")
        s_rec = sem("s_rec")
        s_prod = sem("s_prod")
        s_sum = sem("s_sum")
        s_q = sem("s_q")
        s_h = sem("s_h")
        s_mu = sem("s_mu")
        s_cen = sem("s_cen")
        s_sq = sem("s_sq")
        s_var = sem("s_var")
        s_vln = sem("s_vln")
        s_vr0 = sem("s_vr0")
        s_vv = sem("s_vv")
        s_newt = sem("s_newt")
        s_z = sem("s_z")
        s_gsq = sem("s_gsq")
        s_grn = sem("s_grn")
        s_gxr = sem("s_gxr")
        s_gsum = sem("s_gsum")
        s_oproj = sem("s_oproj")
        s_osb = sem("s_osb")
        s_out = [sem("s_out0"), sem("s_out1")]

        def xview(c, t, d):
            img = X[:, c, :]
            if d % 2 == 0:
                v = img.rearrange("p (h k t) -> p h k t", k=CHUNK, t=CHUNK)
            else:
                v = img.rearrange("p (k t h) -> p h k t", k=CHUNK, t=CHUNK)
            return v[:, :, :, t if d < 2 else CHUNK - 1 - t]

        def hk(ap, d):
            v = ap.rearrange("p (h k) -> p h k", k=CHUNK)
            return v if d < 2 else v[:, :, ::-1]

        def opx(q):
            return gabs[:, q, 0, :], gabs[0:CH - P, q, 1, :]

        def prod_sq(t):
            return lud[:, 4 * (t % 2):4 * (t % 2) + 3, :]

        def var_slot(t):
            return (s1, s2)[t // 2 % 2][:, t % 2, :]

        def root_slot(t):
            return (r0, LX)[t // 2 % 2][:, t % 2, :]

        def diag(g):
            return gabs[:, g % 2, :, :].rearrange("p a b -> p (a b)")[:, 0:9 * P].rearrange("p (k m) -> p k m", k=9)

        blocks = [("in", 0), ("in", 1), ("band", 0), ("in", 2), ("band", 1), ("band", 2)]

        def proxy_bank(t):
            return 2 + t if t < 6 else t - 6

        def mid_tmp(t):
            return LX[:, t % 2, :].bitcast(BF16)[:, 0:BANK]

        def rest_tmp(t):
            return gabs[:, 0, t % 2, :]

        NLOADS = 11

        def waits_passed(eng):
            eng.sem_inc(s_passed, 1)

        with nc.Block() as block:
            @block.sync
            def _(sp):
                loads = [
                    (w_in_a[:, :], io["w_in"][0:P, :]), (w_in_b[:, :], io["w_in"][P:CH, :]),
                    (w_dw[:, :, :], io["w_dw"].rearrange("(g p) k -> p g k", p=P)),
                    (b_dw[:, :], io["b_dw"]), (w_proxy[:, :, :], io["w_proxy"].rearrange("(g p) m -> p g m", p=P)),
                    (w_tmp[:, 0:CG * NDIR * NGATE * P], io["w_gate"]),
                    (w_mix[:, :], io["w_mix"]),
                    (part_mask[:, :], io["part_mask"]),
                    (w_out[:, :, :], io["w_out"].rearrange("(g p) m -> p g m", p=P)),
                    (vecs[:, :, :], io["vecs"]),
                    (ident[:, :], io["ident"]),
                ]
                for dst, src in loads:
                    sp.dma_start(dst, src).then_inc(s_w, 16)
                with sp.Fori(0, B) as b:
                    for j in range(NB * CG // 2):
                        if j == 0:
                            sp.wait_ge(s_var, START + b * CHUNK)
                            waits_passed(sp)
                        sp.wait_ge(s_win, START + b * (NB * CG) + max(2 * (j - 1), 0))
                        px, q = 2 * j % NB * BANK, j % 2
                        for part, rows in ((x_a, slice(0, P)), (x_b, slice(P, CH))):
                            sp.dma_start(part[:, 2 * q:2 * q + 2, :].rearrange("p a n -> p (a n)"),
                                         io["x"][b, rows, px:px + 2 * BANK]).then_inc(s_x[q], 16)
                    for j in range(NB):
                        sp.wait_ge(s_osb, START + b * (2 * NB) + 2 * j + 2)
                        o_a, o_b = opx(j % 2)
                        sp.dma_start(mid[b, 0:P, j * BANK:(j + 1) * BANK], o_a).then_inc(s_out[j % 2], 16)
                        sp.dma_start(mid[b, P:CH, j * BANK:(j + 1) * BANK], o_b).then_inc(s_out[j % 2], 16)
                for s in s_out:
                    sp.wait_ge(s, START + B * NB * 16)

            @block.gpsimd
            def _(pool):
                for s in sems:
                    pool.sem_inc(s, START)
                pool.memset(ones[:, :], 1.0).then_inc(s_const, 1)
                pool.memset(epsv[:, 0:1], GATE_EPS).then_inc(s_const, 1)
                pool.memset(epsv[:, 1:2], LN0_EPS).then_inc(s_const, 1)
                pool.memset(H[:, :, :, :], 0.0).then_inc(s_const, 1)
                pool.wait_ge(s_const, START + 4)
                pool.wait_ge(s_wsplit, START + 8 * CG)
                with pool.Fori(0, B) as b:
                    pool.wait_ge(s_oproj, START + b * NB)
                    waits_passed(pool)
                    for n in range(2):
                        pool.memset(pad[:, n, 0:PADW:PADW - 1, :], 0.0).then_inc(s_border, 1)
                        pool.memset(pad[:, n, 1:PADW - 1, 0:PADW:PADW - 1], 0.0).then_inc(s_border, 1)
                    for q in range(2):
                        pool.wait_ge(s_out[q], START + b * (NB * 16))
                    for g in range(CG):
                        if g == 2:
                            pool.wait_ge(s_band, START + b * (CG * PE_BANDS) + PE_BANDS)
                        waits_passed(pool)
                        for k in range(9):
                            ins = pool.tensor_scalar(diag(g)[:, k, :], ident[:, :], w_dw[:, g, k:k + 1], None, ALU.mult)
                        ins.then_inc(s_diag, 1)
                    with pool.Fori(0, CG) as c:
                        bc = b * CG + c
                        u, v = bc * UNITS, bc * MIX

                        def u_h(k):
                            t, d, q = k // NDIR, k % NDIR, k % 2
                            pool.wait_ge(s_h, START + u + k + 1)
                            if t:
                                pool.wait_ge(s_ludsb, START + 3 * (v + k - NDIR) + 2)
                            else:
                                pool.wait_ge(s_u0, START + bc * NDIR + k + 1)
                            pool.wait_ge(s_acc, START + u + k - 1)
                            pool.tensor_tensor(UH[:, q, :], lud[:, 4 + k % 4, :],
                                               H[:, d, (t + 1) % 2, CHUNK:CHUNK + BANK],
                                               ALU.mult).then_inc(s_uh, 1)

                        for k in range(UNITS):
                            t, d, q, j = k // NDIR, k % NDIR, k % 2, k - NDIR
                            if t:
                                pool.wait_ge(s_abs, START + v + j + 1)
                                pool.wait_ge(s_s2, START + v + j - 1)
                                pool.tensor_tensor(s1[:, q, :], gabs[:, q, 0, :], gabs[:, q, 1, :],
                                                   ALU.add).then_inc(s_s1, 1)
                            if k >= 2:
                                u_h(k - 2)
                            if t:
                                pool.wait_ge(s_ludsb, START + 3 * (v + j) + 3)
                                pool.wait_ge(s_h, START + u + k - 1)
                                waits_passed(pool)
                                pool.tensor_tensor(hk(LX[:, q, :], d), hk(lud[:, q, :], d), xview(c, t, d),
                                                   ALU.mult).then_inc(s_lx, 1)
                                pool.wait_ge(s_acc, START + u + k - 1)
                                waits_passed(pool)
                                pool.tensor_tensor(hk(DX[:, q, :], d), hk(lud[:, 2 + q, :], d), xview(c, t, d),
                                                   ALU.mult).then_inc(s_dx, 1)
                        u_h(UNITS - 2)
                        u_h(UNITS - 1)
                    for t in range(CHUNK):
                        n = b * (CHUNK * 4) + 4 * t
                        v, r = var_slot(t), root_slot(t)
                        pool.wait_ge(s_vv, START + b * CHUNK + t + 1)
                        pool.wait_ge(s_vr0, START + b * CHUNK + t + 1)
                        pool.tensor_tensor(v, v, r, ALU.mult).then_inc(s_newt, 1)
                        pool.wait_ge(s_newt, START + n + 1)
                        pool.tensor_tensor(v, v, r, ALU.mult).then_inc(s_newt, 1)
                        pool.wait_ge(s_newt, START + n + 2)
                        waits_passed(pool)
                        pool.tensor_scalar(v, v, -0.5, 1.5, ALU.mult, ALU.add).then_inc(s_newt, 1)
                        pool.wait_ge(s_newt, START + n + 3)
                        pool.tensor_tensor(r, v, r, ALU.mult).then_inc(s_newt, 1)

            @block.tensor
            def _(pe):
                pe.wait_ge(s_w, START + 16 * NLOADS)
                pe.wait_ge(s_const, START + 4)
                with pe.Fori(0, B) as b:
                    pe.wait_ge(s_osb, START + b * (2 * NB))

                    def add_proxy(t, g):
                        return pe.matmul(ps[:, proxy_bank(t), :], w_proxy[:, g, :], xview(g, t, 0),
                                         start=g == 0, stop=g == CG - 1)

                    for n, (kind, g) in enumerate(blocks):
                        for i in range(NB if kind == "in" else PE_BANDS):
                            j, q = g * NB + i, i % 2
                            if i >= 2:
                                pe.wait_ge(s_pad, START + b * (NB * CG) + j - 1)
                            elif n and blocks[n - 1][0] == "in":
                                pe.wait_ge(s_pad, START + b * (NB * CG) + NB * (blocks[n - 1][1] + 1) - 1 + i)
                            elif n:
                                pe.wait_ge(s_bandx, START + b * (CG * PE_BANDS) + PE_BANDS * blocks[n - 1][1] + i + 1)
                            if kind == "in":
                                pe.wait_ge(s_x[j // 2 % 2], START + b * (NB * CG // 4 * 32) + 32 * (j // 4 + 1))
                                pe.matmul(ps[:, q, :], w_in_a[:, g * P:(g + 1) * P], x_a[:, j % 4, :],
                                          start=True, stop=False)
                                pe.matmul(ps[:, q, :], w_in_b[:, g * P:(g + 1) * P], x_b[:, j % 4, :],
                                          start=False, stop=True).then_inc(s_win, 1)
                            else:
                                if i == 0:
                                    pe.wait_ge(s_pad, START + b * (NB * CG) + NB * (g + 1))
                                    pe.wait_ge(s_diag, START + b * CG + g + 1)
                                y0 = DVE_ROWS + i * ROWS
                                for k in range(9):
                                    mm = pe.matmul(ps[:, q, :], diag(g)[:, k, :],
                                                   pad[:, g % 2, k // 3 + y0:k // 3 + y0 + ROWS, k % 3:k % 3 + SIDE],
                                                   start=k == 0, stop=k == 8)
                                mm.then_inc(s_band, 1)
                    for g in range(CG):
                        pe.wait_ge(s_conv, START + b * (9 * CG) + 9 * (g + 1))
                        pe.wait_ge(s_bandx, START + b * (CG * PE_BANDS) + PE_BANDS * (g + 1))
                        if g < 2:
                            waits_passed(pe)
                            for t in range(6):
                                add_proxy(t, g)
                    waits_passed(pe)
                    for t in range(CHUNK):
                        for gg in range(CG) if t >= 6 else (2,):
                            mm = add_proxy(t, gg)
                        mm.then_inc(s_prox, 1)
                    pe.wait_ge(s_wsplit, START + 24)
                    pe.wait_ge(s_lo, START + (b + 1) * CHUNK)
                    pe.wait_ge(s_mid, START + (b + 1) * (2 * CHUNK))
                    waits_passed(pe)
                    with pe.Fori(0, CG) as c:
                        bc = b * CG + c
                        u, v = bc * UNITS, bc * MIX

                        def add_y(k, part):
                            t, d, q = k // NDIR, k % NDIR, k % 2
                            if part is DX and d == 0:
                                pe.wait_ge(s_yout, START + bc * CHUNK + t)
                            if part is UH:
                                pe.wait_ge(s_uh, START + u + k + 1)
                            elif t == 0:
                                pe.wait_ge(s_dx0, START + bc * NDIR + k + 1)
                            else:
                                pe.wait_ge(s_dx, START + v + k - NDIR + 1)
                            return pe.matmul(ps[:, YB, :], ident[:, :], part[:, q, :], start=part is DX and d == 0,
                                             stop=part is UH and d == NDIR - 1)

                        def sum_products(k):
                            n = v + k - NDIR
                            pe.wait_ge(s_prod, START + n + 1)
                            pe.wait_ge(s_q, START + n - 1)
                            for i in range(3):
                                mm = pe.matmul(ps[:, SUMB + k % 2, :], ident[:, :], prod[:, i, :],
                                               start=i == 0, stop=i == 2)
                            mm.then_inc(s_sum, 1)

                        def one_gate(k, n):
                            pe.wait_ge(s_ludsb, START + 3 * (v + k - NDIR) + n - 1)
                            pe.matmul(ps[:, LUDB + (k + n) % 2, :], w_gate[:, c, k % NDIR, 3 + n, :], S[:, k // NDIR, :],
                                      start=True, stop=True).then_inc(s_lud, 1)

                        for k in range(UNITS):
                            t, d, q = k // NDIR, k % NDIR, k % 2
                            j = k - NDIR
                            if k == NDIR:
                                add_y(k - 3, DX)
                                add_y(k - 3, UH).then_inc(s_acc, 1)
                            if k < 2:
                                pe.wait_ge(s_prod, START + v)
                                pe.wait_ge(s_abs, START + v)
                                pe.wait_ge(s_q, START + v)
                                pe.wait_ge(s_ludsb, START + 3 * v)
                            elif k <= NDIR:
                                done = k - 1 if k < NDIR else NDIR
                                pe.wait_ge(s_h, START + u + done)
                                pe.wait_ge(s_dx0, START + bc * NDIR + done)
                                pe.wait_ge(s_u0, START + bc * NDIR + done)
                            else:
                                pe.wait_ge(s_prod, START + v + j)
                                pe.wait_ge(s_abs, START + v + j)
                            for n in range(3):
                                bank = n if t else 3 * q + n
                                mm = pe.matmul(ps[:, bank, :], w_gate[:, c, d, n + (0 if t else 3), :],
                                               S[:, t, :], start=True, stop=True)
                            mm.then_inc(s_gate if t else s_lud0, 1)
                            if t:
                                one_gate(k, 0)
                                one_gate(k, 1)
                            if k > NDIR:
                                sum_products(k - 1)
                            if t:
                                one_gate(k, 2)
                            if k >= 3 and k != NDIR:
                                add_y(k - 3, DX)
                                add_y(k - 3, UH).then_inc(s_acc, 1)
                        sum_products(UNITS - 1)
                        for k in range(UNITS - 3, UNITS):
                            add_y(k, DX)
                            add_y(k, UH).then_inc(s_acc, 1)
                    pe.wait_ge(s_prod, START + (b + 1) * (CG * MIX))
                    pe.wait_ge(s_yout, START + (b + 1) * (CG * CHUNK))

                    def var_sum(t):
                        pe.wait_ge(s_sq, START + b * CHUNK + t + 1)
                        if t >= 2:
                            pe.wait_ge(s_vv, START + b * CHUNK + t - 1)
                            pe.wait_ge(s_vln, START + b * CHUNK + t - 1)
                        for g in range(CG):
                            mm = pe.matmul(ps[:, 2 + t % 2, :], ones[:, :], prod_sq(t)[:, g, :],
                                           start=g == 0, stop=g == CG - 1)
                        mm.then_inc(s_var, 1)

                    for t in range(CHUNK):
                        if t >= 2:
                            pe.wait_ge(s_cen, START + b * (CHUNK * CG) + CG * (t - 1))
                        for g in range(CG):
                            mm = pe.matmul(ps[:, t % 2, :], ones[:, :], Y[:, g, t, :],
                                           start=g == 0, stop=g == CG - 1)
                        mm.then_inc(s_mu, 1)
                        if t:
                            var_sum(t - 1)
                    var_sum(CHUNK - 1)
                    pe.wait_ge(s_gxr, START + b + 1)
                    pe.matmul(ps[:, 4, 0:CG], ones[:, :], gx[:, 1, :], start=True, stop=True).then_inc(s_gsum, 1)
                    pe.wait_ge(s_grn, START + b * 12 + 11)
                    for g in range(CG):
                        pe.matmul(ps[:, 5, 0:1], w_out[:, g, 0:P], svec[:, 2, g:g + 1], start=g == 0, stop=g == CG - 1)
                    for g in range(CG):
                        mm = pe.matmul(ps[0:CH - P, 4, 0:1], w_out[:, g, P:CH], svec[:, 2, g:g + 1],
                                       start=g == 0, stop=g == CG - 1)
                    mm.then_inc(s_gsum, 1)
                    pe.wait_ge(s_vv, START + (b + 1) * CHUNK)
                    pe.wait_ge(s_vln, START + (b + 1) * CHUNK)
                    pe.wait_ge(s_z, START + (b + 1) * CHUNK)
                    yv = Y[:, :, :, :].rearrange("p g t (h k) -> p g h k t", k=CHUNK)
                    for j in range(NB):
                        if j >= 2:
                            pe.wait_ge(s_osb, START + b * (2 * NB) + 2 * (j - 1))
                        for g in range(CG):
                            pe.matmul(ps[:, j % 2, :], w_out_s[:, g, 0:P], yv[:, g, ROWS * j:ROWS * (j + 1), :, :],
                                      start=g == 0, stop=g == CG - 1)
                        for g in range(CG):
                            mm = pe.matmul(ps[0:CH - P, 2 + j % 2, :], w_out_s[:, g, P:CH],
                                           yv[:, g, ROWS * j:ROWS * (j + 1), :, :], start=g == 0, stop=g == CG - 1)
                        mm.then_inc(s_oproj, 1)

            @block.scalar
            def _(act):
                act.wait_ge(s_const, START + 4)
                act.wait_ge(s_w, START + 16 * NLOADS)
                with act.Fori(0, B) as b:
                    act.preload_act_table_set("natural_log_exp_and_others")
                    act.wait_ge(s_border, START + (b + 1) * 4)
                    for kind, g in blocks:
                        for i in range(NB if kind == "in" else PE_BANDS):
                            j, q = g * NB + i, i % 2
                            if kind == "in":
                                act.wait_ge(s_win, START + b * (NB * CG) + j + 1)
                                if j == 2 * NB:
                                    act.wait_ge(s_conv, START + b * (9 * CG) + 9)
                                    act.wait_ge(s_band, START + b * (CG * PE_BANDS) + PE_BANDS)
                                y0 = 1 + i * ROWS
                                act.activation(pad[:, g % 2, y0:y0 + ROWS, 1:1 + SIDE],
                                               ps[:, q, :].rearrange("p (h w) -> p h w", w=SIDE),
                                               ACT.Copy).then_inc(s_pad, 1)
                            else:
                                act.wait_ge(s_band, START + b * (CG * PE_BANDS) + PE_BANDS * g + i + 1)
                                x0 = (DVE_ROWS + i * ROWS) * SIDE
                                act.activation(X[:, g, x0:x0 + BANK], ps[:, q, :], ACT.Identity,
                                               bias=b_dw[:, g:g + 1]).then_inc(s_bandx, 1)
                    for i in range(CHUNK + 1):
                        if i < CHUNK:
                            act.wait_ge(s_prox, START + b * CHUNK + i + 1)
                            act.activation(S[:, i, :], ps[:, proxy_bank(i), :], ACT.Copy).then_inc(s_hi, 1)
                        t = i - 1
                        if t >= 0:
                            n = b * (2 * CHUNK) + 2 * t
                            act.wait_ge(s_res, START + b * CHUNK + t + 1)
                            act.wait_ge(s_lo, START + b * CHUNK + t - 1)
                            act.wait_ge(s_mid, START + n - 2)
                            act.activation(mid_tmp(t), rest_tmp(t), ACT.Copy).then_inc(s_mid, 1)
                            act.wait_ge(s_mid, START + n + 1)
                            act.activation(S[32:64, t, :], mid_tmp(t)[32:64, :], ACT.Copy).then_inc(s_mid, 1)
                    act.wait_ge(s_lo, START + (b + 1) * CHUNK)
                    act.wait_ge(s_mid, START + (b + 1) * (2 * CHUNK))
                    with act.Fori(0, CG) as c:
                        bc = b * CG + c
                        u, v = bc * UNITS, bc * MIX

                        def y_out(t):
                            act.wait_ge(s_acc, START + u + NDIR * (t + 1))
                            act.activation(Y[:, c, t, :], ps[:, YB, :], ACT.Copy).then_inc(s_yout, 1)

                        def copy_gate(k, n):
                            slot = (k % 2, 4 + k % 4, 2 + k % 2)[n]
                            done = v + k - NDIR + 1
                            act.wait_ge(s_lud, START + 3 * (v + k - NDIR) + n + 1)
                            if n == 1:
                                act.wait_ge(s_uh, START + u + k - 3)
                            else:
                                act.wait_ge(s_dx if n else s_lx, START + done - 2)
                            act.activation(lud[:, slot, :], ps[:, LUDB + (k + n) % 2, :], ACT.Copy).then_inc(s_ludsb, 1)

                        def log_sum(k):
                            j = k - NDIR
                            act.wait_ge(s_s2, START + v + j + 1)
                            act.wait_ge(s_q, START + v + j - 1)
                            act.activation(r0[:, k % 2, :], s2[:, k % 2, :], ACT.Ln,
                                           bias=epsv[:, 0:1]).then_inc(s_ln, 1)

                        def exp_log(k):
                            act.wait_ge(s_ln, START + v + k - NDIR + 1)
                            act.activation(r0[:, k % 2, :], r0[:, k % 2, :], ACT.Exp, scale=-1.0).then_inc(s_r0, 1)

                        for k in range(UNITS):
                            t, q = k // NDIR, k % 2
                            if not t:
                                act.wait_ge(s_lud0, START + bc * NDIR + k + 1)
                                act.wait_ge(s_uh, START + u + k - 3)
                                act.activation(lud[:, 4 + k % 4, :], ps[:, 3 * q + 1, :], ACT.Copy).then_inc(s_u0, 1)
                            else:
                                j = k - NDIR
                                act.wait_ge(s_gate, START + v + j + 1)
                                act.wait_ge(s_s2, START + v + j - 1)
                                act.wait_ge(s_s1, START + v + j - 1)
                                act.activation(gabs[:, q, :, :], ps[:, 0:3, :],
                                               ACT.Abs).then_inc(s_abs, 1)
                                copy_gate(k, 0)
                                copy_gate(k, 1)
                            if k > NDIR:
                                log_sum(k - 1)
                            if k > NDIR:
                                exp_log(k - 1)
                            if t:
                                copy_gate(k, 2)
                            if k % NDIR == NDIR - 2 and t:
                                y_out(t - 1)
                        log_sum(UNITS - 1)
                        exp_log(UNITS - 1)
                        y_out(CHUNK - 1)
                    for i in range(CHUNK + 4):
                        t = i
                        if t < CHUNK:
                            act.wait_ge(s_cen, START + b * (CHUNK * CG) + CG * (t + 1))
                            act.wait_ge(s_var, START + b * CHUNK + t - 1)
                            act.activation(prod_sq(t), Y[:, :, t, :], ACT.Square).then_inc(s_sq, 1)
                        t = i - 4
                        if t >= 0:
                            act.wait_ge(s_z, START + b * CHUNK + t + 1)
                            for g in range(CG):
                                act.wait_ge(s_gsq, START + b * (CG * CHUNK) + CG * t + g)
                                act.activation(prod[:, 2, :], Y[:, g, t, :], ACT.Square, scale=vecs[:, 2, g:g + 1],
                                               bias=vecs[:, 3, g:g + 1],
                                               accum_out=gacc[:, g, t:t + 1]).then_inc(s_gsq, 1)
                        t = i - 1
                        if 0 <= t < CHUNK:
                            act.wait_ge(s_var, START + b * CHUNK + t + 1)
                            act.wait_ge(s_vv, START + b * CHUNK + t + 1)
                            act.wait_ge(s_z, START + b * CHUNK + t - 3)
                            act.activation(root_slot(t), ps[:, 2 + t % 2, :], ACT.Ln, bias=epsv[:, 1:2],
                                           scale=1.0 / DIN).then_inc(s_vln, 1)
                            act.wait_ge(s_vln, START + b * CHUNK + t + 1)
                            act.activation(root_slot(t), root_slot(t), ACT.Exp, scale=-0.5).then_inc(s_vr0, 1)
                    act.wait_ge(s_grn, START + b * 12 + 1)
                    act.activation(gx[:, 1, :], gx[:, 0, :], ACT.Sqrt).then_inc(s_gxr, 1)
                    act.wait_ge(s_grn, START + b * 12 + 12)
                    for j in range(NB):
                        act.wait_ge(s_oproj, START + b * NB + j + 1)
                        act.wait_ge(s_out[j % 2], START + b * (NB * 16) + 32 * (j // 2))
                        o_a, o_b = opx(j % 2)
                        act.activation(o_a, ps[:, j % 2, :], ACT.Identity, bias=b_out[:, 0:1]).then_inc(s_osb, 1)
                        act.activation(o_b, ps[0:CH - P, 2 + j % 2, :], ACT.Identity,
                                       bias=b_out[0:CH - P, 1:2]).then_inc(s_osb, 1)

            @block.vector
            def _(dve):
                dve.wait_ge(s_w, START + 16 * NLOADS)
                WC = NDIR * NGATE * P
                hi = Y[:, 0, :, :].rearrange("p a b -> p (a b)").bitcast(BF16)[:, 0:WC]
                md = Y[:, 0, :, :].rearrange("p a b -> p (a b)").bitcast(BF16)[:, WC:2 * WC]
                acc = Y[:, 1, :, :].rearrange("p a b -> p (a b)")[:, 0:WC]
                for c in range(CG):
                    w = w_tmp[:, c * WC:(c + 1) * WC]
                    wd = w.rearrange("p (d n m) -> p d n m", d=NDIR, n=NGATE)
                    n = 8 * c
                    if c:
                        dve.wait_ge(s_wsplit, START + n)
                    for d in range(NDIR):
                        ins = dve.tensor_scalar(wd[:, d, 4:6, :], wd[:, d, 4:6, :], w_mix[:, d:d + 1], None, ALU.mult)
                    ins.then_inc(s_wsplit, 1)
                    dve.wait_ge(s_wsplit, START + n + 1)
                    dve.tensor_copy(hi, w).then_inc(s_wsplit, 1)
                    dve.wait_ge(s_wsplit, START + n + 2)
                    dve.tensor_tensor(w, w, hi, ALU.subtract).then_inc(s_wsplit, 1)
                    dve.wait_ge(s_wsplit, START + n + 3)
                    dve.tensor_copy(md, w).then_inc(s_wsplit, 1)
                    dve.wait_ge(s_wsplit, START + n + 4)
                    dve.tensor_tensor(w, w, md, ALU.subtract).then_inc(s_wsplit, 1)
                    dve.wait_ge(s_wsplit, START + n + 5)
                    dve.tensor_scalar(acc, w, part_mask[:, 2:3], None, ALU.mult).then_inc(s_wsplit, 1)
                    dve.wait_ge(s_wsplit, START + n + 6)
                    dve.scalar_tensor_tensor(out=acc, in0=md, scalar=part_mask[:, 1:2], in1=acc,
                                             op0=ALU.mult, op1=ALU.add).then_inc(s_wsplit, 1)
                    dve.wait_ge(s_wsplit, START + n + 7)
                    dve.scalar_tensor_tensor(out=w_gate[:, c, :, :, :].rearrange("p d n m -> p (d n m)"),
                                             in0=hi, scalar=part_mask[:, 0:1], in1=acc,
                                             op0=ALU.mult, op1=ALU.add).then_inc(s_wsplit, 1)
                dve.wait_ge(s_wsplit, START + 24)
                with dve.Fori(0, B) as b:
                    for g in range(CG):
                        xg = X[:, g, 0:DVE_ROWS * SIDE].rearrange("p (h w) -> p h w", w=SIDE)
                        dve.wait_ge(s_pad, START + b * (NB * CG) + NB * (g + 1))
                        for k in range(9):
                            src = pad[:, g % 2, k // 3:k // 3 + DVE_ROWS, k % 3:k % 3 + SIDE]
                            n = b * (9 * CG) + 9 * g + k
                            if k == 0:
                                dve.tensor_scalar(xg, src, w_dw[:, g, 0:1], b_dw[:, g:g + 1],
                                                  ALU.mult, ALU.add).then_inc(s_conv, 1)
                            else:
                                dve.wait_ge(s_conv, START + n)
                                dve.scalar_tensor_tensor(out=xg, in0=src, scalar=w_dw[:, g, k:k + 1], in1=xg,
                                                         op0=ALU.mult, op1=ALU.add).then_inc(s_conv, 1)
                    for i in range(CHUNK + 1):
                        if i < CHUNK:
                            dve.wait_ge(s_hi, START + b * CHUNK + i + 1)
                            dve.wait_ge(s_lo, START + b * CHUNK + i - 1)
                            dve.wait_ge(s_mid, START + b * (2 * CHUNK) + 2 * (i - 1))
                            dve.tensor_tensor(rest_tmp(i), ps[:, proxy_bank(i), :], S[:, i, :],
                                              ALU.subtract).then_inc(s_res, 1)
                        t = i - 1
                        if t >= 0:
                            dve.wait_ge(s_res, START + b * CHUNK + t + 1)
                            dve.wait_ge(s_mid, START + b * (2 * CHUNK) + 2 * t + 1)
                            dve.tensor_tensor(S[64:96, t, :], rest_tmp(t)[64:96, :], mid_tmp(t)[64:96, :],
                                              ALU.subtract).then_inc(s_lo, 1)
                    with dve.Fori(0, CG) as c:
                        bc = b * CG + c
                        u, v = bc * UNITS, bc * MIX

                        def first_state(k):
                            dve.wait_ge(s_lud0, START + bc * NDIR + k + 1)
                            dve.wait_ge(s_uh, START + u + k - 7)
                            dve.wait_ge(s_prod, START + v)
                            waits_passed(dve)
                            dve.tensor_tensor(hk(H[:, k, 1, CHUNK:CHUNK + BANK], k), hk(ps[:, 3 * (k % 2), :], k),
                                              xview(c, 0, k), ALU.mult).then_inc(s_h, 1)

                        def first_dx(k):
                            dve.wait_ge(s_acc, START + u + k - 1)
                            waits_passed(dve)
                            dve.tensor_tensor(hk(DX[:, k % 2, :], k), hk(ps[:, 3 * (k % 2) + 2, :], k), xview(c, 0, k),
                                              ALU.mult).then_inc(s_dx0, 1)

                        def sum2(k):
                            q, n = k % 2, v + k - NDIR
                            dve.wait_ge(s_s1, START + n + 1)
                            dve.wait_ge(s_ln, START + n - 1)
                            dve.wait_ge(s_rec, START + n - 1)
                            dve.tensor_tensor(s2[:, q, :], s1[:, q, :], gabs[:, q, 2, :], ALU.add).then_inc(s_s2, 1)

                        def mixed(k):
                            t, d, q, n = k // NDIR, k % NDIR, k % 2, v + k - NDIR
                            dve.wait_ge(s_r0, START + n + 1)
                            dve.scalar_tensor_tensor(out=s2[:, q, :], in0=s2[:, q, :], scalar=GATE_EPS,
                                                     in1=r0[:, q, :], op0=ALU.add, op1=ALU.mult).then_inc(s_err, 1)
                            dve.wait_ge(s_err, START + n + 1)
                            dve.scalar_tensor_tensor(out=r0[:, q, :], in0=s2[:, q, :], scalar=2.0,
                                                     in1=r0[:, q, :], op0=ALU.subtract,
                                                     op1=ALU.mult).then_inc(s_rec, 1)
                            dve.wait_ge(s_sum, START + n + 1)
                            dve.wait_ge(s_rec, START + n + 1)
                            dve.wait_ge(s_h, START + u + k)
                            dve.tensor_tensor(total[:, :], ps[:, SUMB + q, :], r0[:, q, :], ALU.mult).then_inc(s_q, 1)
                            dve.wait_ge(s_q, START + n + 1)
                            dve.wait_ge(s_lx, START + n + 1)
                            dve.wait_ge(s_uh, START + u + k - 7)
                            dve.tensor_tensor(H[:, d, (t + 1) % 2, CHUNK:CHUNK + BANK], LX[:, q, :], total[:, :],
                                              ALU.subtract).then_inc(s_h, 1)

                        for k in range(NDIR):
                            first_state(k)
                            first_dx(k)
                        for k in range(NDIR, UNITS):
                            t, d, q, n = k // NDIR, k % NDIR, k % 2, v + k - NDIR
                            h_old = H[:, d, t % 2, :]
                            shifted = bass.AP(tensor=h_old.tensor, offset=h_old.offset,
                                              ap=[h_old.ap[0], [CHUNK, 3], [1, BANK]])
                            dve.wait_ge(s_gate, START + n + 1)
                            dve.wait_ge(s_abs, START + n + 1)
                            dve.wait_ge(s_h, START + u + k - NDIR + 1)
                            dve.wait_ge(s_sum, START + n)
                            dve.tensor_tensor(prod[:, :, :], ps[:, 0:3, :], shifted, ALU.mult).then_inc(s_prod, 1)
                            if k > NDIR:
                                mixed(k - 1)
                            sum2(k)
                        mixed(UNITS - 1)
                    dve.wait_ge(s_yout, START + (b + 1) * (CG * CHUNK))

                    for i in range(CHUNK + 3):
                        t = i
                        if t < CHUNK:
                            dve.wait_ge(s_mu, START + b * CHUNK + t + 1)
                            for g in range(CG):
                                dve.scalar_tensor_tensor(out=Y[:, g, t, :], in0=ps[:, t % 2, :], scalar=-1.0 / DIN,
                                                         in1=Y[:, g, t, :], op0=ALU.mult,
                                                         op1=ALU.add).then_inc(s_cen, 1)
                        t = i - 3
                        if t >= 0:
                            dve.wait_ge(s_newt, START + b * (4 * CHUNK) + 4 * (t + 1))
                            r = root_slot(t)
                            rb = bass.AP(tensor=r.tensor, offset=r.offset, ap=[r.ap[0], [0, CG], [1, BANK]])
                            dve.tensor_tensor(Y[:, :, t, :], Y[:, :, t, :], rb, ALU.mult).then_inc(s_z, 1)
                        t = i - 1
                        if 0 <= t < CHUNK:
                            dve.wait_ge(s_var, START + b * CHUNK + t + 1)
                            dve.wait_ge(s_newt, START + b * (4 * CHUNK) + 4 * (t - 3))
                            dve.tensor_scalar(var_slot(t), ps[:, 2 + t % 2, :], 1.0 / DIN, LN0_EPS, ALU.mult,
                                              ALU.add).then_inc(s_vv, 1)
                    n = b * 12
                    dve.wait_ge(s_gsq, START + (b + 1) * (CG * CHUNK))
                    dve.tensor_reduce(gx[:, 0, :], gacc[:, :, :], AX_X, ALU.add).then_inc(s_grn, 1)
                    dve.wait_ge(s_gsum, START + 2 * b + 1)
                    dve.tensor_reduce(small[:, 0:1], ps[:, 4, 0:CG], AX_X, ALU.add).then_inc(s_grn, 1)
                    dve.wait_ge(s_grn, START + n + 2)
                    dve.tensor_scalar(small[:, 1:2], small[:, 0:1], 1.0 / DIN, GRN_EPS, ALU.mult,
                                      ALU.add).then_inc(s_grn, 1)
                    dve.wait_ge(s_grn, START + n + 3)
                    dve.reciprocal(small[:, 2:3], small[:, 1:2]).then_inc(s_grn, 1)
                    dve.wait_ge(s_grn, START + n + 4)
                    dve.wait_ge(s_gxr, START + b + 1)
                    dve.tensor_scalar(svec[:, 0, :], gx[:, 1, :], small[:, 2:3], None, ALU.mult).then_inc(s_grn, 1)
                    dve.wait_ge(s_grn, START + n + 5)
                    dve.tensor_tensor(svec[:, 0, :], svec[:, 0, :], vecs[:, 0, :], ALU.mult).then_inc(s_grn, 1)
                    dve.wait_ge(s_grn, START + n + 6)
                    dve.tensor_scalar(svec[:, 0, :], svec[:, 0, :], 1.0, None, ALU.add).then_inc(s_grn, 1)
                    dve.wait_ge(s_grn, START + n + 7)
                    dve.tensor_tensor(svec[:, 1, :], svec[:, 0, :], vecs[:, 2, :], ALU.mult).then_inc(s_grn, 1)
                    dve.tensor_tensor(svec[:, 2, :], svec[:, 0, :], vecs[:, 3, :], ALU.mult).then_inc(s_grn, 1)
                    dve.wait_ge(s_grn, START + n + 9)
                    dve.tensor_tensor(svec[:, 2, :], svec[:, 2, :], vecs[:, 1, :], ALU.add).then_inc(s_grn, 1)
                    for g in range(CG):
                        ins = dve.tensor_scalar(w_out_s[:, g, :], w_out[:, g, :], svec[:, 1, g:g + 1], None, ALU.mult)
                    ins.then_inc(s_grn, 1)
                    dve.wait_ge(s_gsum, START + 2 * b + 2)
                    dve.tensor_copy(b_out[:, 0:1], ps[:, 5, 0:1])
                    dve.tensor_copy(b_out[0:CH - P, 1:2], ps[0:CH - P, 4, 0:1]).then_inc(s_grn, 1)
                    dve.wait_ge(s_oproj, START + (b + 1) * NB)


def layer0_inputs(v):
    import numpy as np
    T = np.ascontiguousarray
    gates = [v["L0_conv_W_w"].reshape(3, NDIR, CG, P, PROXY)[i] for i in range(3)]
    gates += [v[f"L0_conv_W_{n}"].reshape(NDIR, CG, P, PROXY) for n in "lud"]
    wg = np.stack(gates).transpose(4, 2, 1, 0, 3).reshape(PROXY, -1)
    col = lambda a: a.reshape(CG, P).T
    mask = np.zeros((P, 3), np.float32)
    for i, part in enumerate([0, 1, 0, 1, 0, 1, 2]):
        mask[16 * i:16 * i + 16, part] = 1.0
    return {
        "x": T(v["x"].reshape(-1, CH, PIX)),
        "w_in": T(v["L0_conv_W_in"].T), "w_dw": T(v["L0_conv_W_dw"].reshape(DIN, 9)), "b_dw": T(col(v["L0_conv_b_dw"])),
        "w_proxy": T(np.tile(v["L0_conv_W_xd"].T, (1, P // PROXY))), "w_gate": T(np.tile(wg, (P // PROXY, 1))),
        "w_mix": T(np.tile(v["L0_conv_w_m"], (P, 1))), "part_mask": mask, "w_out": T(v["L0_conv_W_out"].T),
        "vecs": T(np.stack([col(v["L0_conv_" + n]) for n in ("grn_gamma", "grn_beta", "ln_w", "ln_b")], 1)),
        "ident": np.eye(P, dtype=np.float32),
    }


def layer1(nc, B, io, mid, out):
    T = BANK
    NJ = PIX // T
    NCH = B * NJ
    TT = T // P
    NS = 16
    RANK = 12
    KCONV = 4
    NM = 2
    NG = NM * CG
    UNITS = NS * CG
    DTROW = 96
    R_DA, R_U, R_H, R_P = 6, 6, 6, 6
    R_B, R_C = 4, 4
    LEAD_A, LEAD_U = 4, 4
    Y0, ROW0, PREP0 = 0, 3, 5

    IN = (0, 0)
    Z = (4, 17)
    SILU = (16, 24)
    XPROJ = (18, 26)
    SPLIT = (24, 31)
    SOFT, APART = (24, 31), (6, 3)
    NORM = 24
    LAG_Y = 4
    GATE = 2
    OUT = 5
    POOL_P = ((5, 10, 15, 20), (3, 7, 11, 15))

    def products(s, m, k, by_pool):
        mine = lambda mm, end: sum((i in POOL_P[mm]) == by_pool for i in range(end))
        assert mine(0, UNITS) == mine(1, UNITS)
        return mine(0, UNITS) * s + (mine(m, k + 1) if k >= 0 else k + 1)

    def group_at(k, first, apart=1):
        g = (k - first) // apart
        return g if (k - first) % apart == 0 and 0 <= g < CG else None

    with ExitStack() as ctx:
        def sb(name, shape, dt=F32):
            return ctx.enter_context(nc.sbuf_tensor(name, shape, dt))

        sems = []

        def sem(name):
            sems.append(ctx.enter_context(nc.semaphore(name)))
            return sems[-1]

        wi_a = sb("wi_a", [P, NM, 2, CG, P])
        wi_b = sb("wi_b", [CH - P, NM, 2, CG, P])
        wc = sb("wc", [P, NG, KCONV])
        b_conv = sb("b_conv", [P, NG])
        wx = sb("wx", [P, NG, DTROW + RANK])
        wdt = sb("wdt", [P, NG, P])
        bdt = sb("bdt", [P, NG])
        A = sb("A", [P, NG, NS])
        Dv = sb("Dv", [P, NG])
        diag_d = sb("diag_d", [P, NG, P])
        wo = sb("wo", [P, NG, CH])
        sel = sb("sel", [P, 2 * NS, P], BF16)
        ln_gb = sb("ln_gb", [P, 2, CH])
        keep = sb("keep", [P, NCH])
        ident = sb("ident1", [P, P])
        tok = sb("tok", [P, TT, CH])
        xs = sb("xs", [P, TT, CH])
        resid = sb("resid", [P, TT, CH])
        stats = sb("stats", [P, TT, 6])
        mv = sb("mv", [P, TT, 2])
        vr = sb("vr", [P, 3, TT])
        xt_a = sb("xt_a", [P, T])
        xt_b = sb("xt_b", [CH - P, T])
        raw = sb("raw", [P, CG, T + KCONV])
        halo = sb("halo", [P, NG, KCONV])
        xc = sb("xc", [P, NG, T])
        dt = sb("dt", [P, NG, T])
        dtx = sb("dtx", [P, NG, T])
        yz = sb("yz", [P, NG, T])
        zs = sb("zs", [P, NG, T])
        S = sb("S1", [P, NM, T], BF16)
        rest = sb("rest", [P, T])
        midt = sb("midt", [P, T], BF16)
        w1 = sb("w1", [P, CG, T])
        lnw = sb("lnw", [P, CG, T])
        vmax = sb("vmax", [P, CG, T])
        minus_one = sb("minus_one", [P, 1])
        last = sb("last", [P, NM, UNITS])
        dA = sb("dA", [P, R_DA, T])
        u = sb("u", [P, R_U, T])
        h = sb("h", [P, R_H, T])
        p = sb("p", [P, R_P, T])
        bb = sb("bb", [P, R_B, T])
        cb = sb("cb", [P, R_C, T])
        o = sb("o", [P, TT, CH])

        ps = ctx.enter_context(nc.psum_tensor("ps1", [P, 8, BANK], F32))

        s_w = sem("t_w")
        s_passed = sem("t_passed")
        s_set = sem("t_set")
        s_zero = sem("t_zero")
        s_tok = sem("t_tok")
        s_ln = sem("t_ln")
        s_lr = sem("t_lr")
        s_gb = sem("t_gb")
        s_tr = sem("t_tr")
        s_xt = sem("t_xt")
        s_rs = sem("t_rs")
        s_kp = sem("t_kp")
        s_in = sem("t_in")
        s_raw = sem("t_raw")
        s_tap = sem("t_tap")
        s_conv = sem("t_conv")
        s_xc = sem("t_xc")
        s_z = sem("t_z")
        s_zs = sem("t_zs")
        s_xp = sem("t_xp")
        s_hi = sem("t_hi")
        s_res = sem("t_res")
        s_mid = sem("t_mid")
        s_lo = sem("t_lo")
        s_dtp = sem("t_dtp")
        s_abs = sem("t_abs")
        s_e = sem("t_e")
        s_w1 = sem("t_w1")
        s_l = sem("t_l")
        s_max = sem("t_max")
        s_c1 = sem("t_c1")
        s_c2 = sem("t_c2")
        s_dt = sem("t_dt")
        s_dtx = sem("t_dtx")
        s_row = [sem("t_row_b"), sem("t_row_c")]
        s_rows = [sem("t_rows_b"), sem("t_rows_c")]
        s_da = sem("t_da")
        s_u = sem("t_u")
        s_scan = sem("t_scan")
        s_last = sem("t_last")
        s_p = [sem("t_p"), sem("t_p_pool")]
        s_y = sem("t_y")
        s_yz = sem("t_yz")
        s_op = sem("t_op")
        s_o = sem("t_o")
        s_st = [sem(f"t_st{i}") for i in range(TT)]

        NLOADS = 16

        def waits_passed(eng):
            eng.sem_inc(s_passed, 1)

        def is_last(s):
            return isinstance(s, int) and s == 2 * NCH - 1

        def ahead(s, m, k, lead):
            if k + lead < UNITS:
                return s, m, k + lead
            return None if is_last(s) else (s + 1, 1 - m, k + lead - UNITS)

        def behind(s, m, k, lag):
            if k >= lag:
                return s, m, k - lag
            return (s - 1, 1 - m, k - lag + UNITS) if has_before(s) else None

        def has_before(s):
            return not (isinstance(s, int) and s == 0)

        def run(stage, norm, prepare, finish, eng, begin=lambda: None):
            for k in range(UNITS):
                norm(k, 0)
            for k in range(UNITS):
                prepare(k, 0, 0, 0)
            begin()
            stage(0, 0, 0, None)
            with eng.Fori(0, NCH - 2) as c:
                stage(2 * c + 1, 1, c, None)
                stage(2 * c + 2, 0, c + 1, c)
            stage(2 * NCH - 3, 1, NCH - 2, None)
            stage(2 * NCH - 2, 0, NCH - 1, NCH - 2)
            stage(2 * NCH - 1, 1, NCH - 1, None)
            finish()

        with nc.Block() as block:
            @block.sync
            def _(sp):
                loads = [
                    (wi_a[:, :, :, :, :].rearrange("p a b c d -> p (a b c d)"), io["wi"][0:P, :]),
                    (wi_b[:, :, :, :, :].rearrange("p a b c d -> p (a b c d)"), io["wi"][P:CH, :]),
                    (wc[:, :, :], io["wc"].rearrange("(g p) k -> p g k", p=P)),
                    (b_conv[:, :], io["bc"]), (bdt[:, :], io["bdt"]), (Dv[:, :], io["D"]),
                    (wx[:, :, :], io["wx"].rearrange("(g p) m -> p g m", p=P)),
                    (wdt[DTROW:DTROW + RANK, :, :], io["wdt"].rearrange("r (g m) -> r g m", g=NG)),
                    (A[:, :, :], io["A_log"].rearrange("(g p) n -> p g n", p=P)),
                    (wo[:, :, :], io["wo"].rearrange("(g p) m -> p g m", p=P)),
                    (ln_gb[:, 0, :], io["ln_g"]), (ln_gb[:, 1, :], io["ln_b"]),
                    (ident[:, :], io["ident"]), (keep[:, :], io["keep"][:, 0:NCH]),
                    (xc[:, 0:4, :].rearrange("p g n -> p (g n)"), io["sel"][:, 0:4 * T]),
                    (dt[:, 0:4, :].rearrange("p g n -> p (g n)"), io["sel"][:, 4 * T:8 * T]),
                ]
                assert len(loads) == NLOADS
                for dst, src in loads:
                    sp.dma_start(dst, src).then_inc(s_w, 16)
                tokens = mid.rearrange("b c n -> (b c n)").rearrange("(j i p c) -> j p i c", i=TT, p=P, c=CH)
                stored = out.rearrange("b c n -> (b c n)").rearrange("(j i p c) -> j i p c", i=TT, p=P, c=CH)

                def store(c):
                    for i in range(TT):
                        sp.wait_ge(s_o, START + TT * c + i + 1)
                        sp.dma_start(stored[c, i], o[:, i, :]).then_inc(s_st[i], 16)

                sp.dma_start(tok[:, :, :], tokens[0]).then_inc(s_tok, 16)
                sp.wait_ge(s_ln, START + 8)
                sp.dma_start(tok[:, :, :], tokens[1]).then_inc(s_tok, 16)
                with sp.Fori(0, NCH - 2) as c:
                    sp.wait_ge(s_ln, START + 8 * c + 16)
                    sp.dma_start(tok[:, :, :], tokens[c + 2]).then_inc(s_tok, 16)
                    store(c)
                store(NCH - 2)
                store(NCH - 1)
                for s in s_st:
                    sp.wait_ge(s, START + NCH * 16)

            def times_c(eng, s, m, k):
                eng.wait_ge(s_scan, START + UNITS * s + k + 1)
                eng.wait_ge(s_rows[1], START + NS * s + k // CG + 1)
                eng.wait_ge(s_y, START + UNITS * s + k + 1 - R_P)
                eng.tensor_tensor(p[:, k % R_P, :], h[:, k % R_H, :], cb[:, k // CG % R_C, :],
                                  ALU.mult).then_inc(s_p[k in POOL_P[m]], 1)

            @block.gpsimd
            def _(pool):
                for s in sems:
                    pool.sem_inc(s, START)
                pool.memset(last[:, :, :], 0.0).then_inc(s_zero, 1)
                pool.memset(halo[:, :, :], 0.0).then_inc(s_zero, 1)
                pool.memset(minus_one[:, :], -1.0).then_inc(s_zero, 1)
                pool.wait_ge(s_w, START + 16 * NLOADS)

                def norm(k, c):
                    if k in (NORM + 9, NORM + 13):
                        v = ln_gb[:, (k - NORM - 9) // 4, :]
                        over_tokens = bass.AP(tensor=v.tensor, offset=v.offset, ap=[v.ap[0], [0, TT], [1, CH]])
                        if k == NORM + 9:
                            pool.wait_ge(s_ln, START + 8 * c + 8)
                            pool.tensor_tensor(xs[:, :, :], xs[:, :, :], over_tokens, ALU.mult).then_inc(s_gb, 1)
                        else:
                            pool.wait_ge(s_gb, START + 2 * c + 1)
                            pool.tensor_tensor(xs[:, :, :], xs[:, :, :], over_tokens, ALU.add).then_inc(s_gb, 1)

                def prepare(k, r, m, c):
                    g = group_at(k, SOFT[m] + 5, APART[m])
                    if g is not None:
                        n = CG * r + g
                        pool.wait_ge(s_c1, START + n + 1)
                        pool.wait_ge(s_max, START + n + 1)
                        pool.tensor_tensor(dtx[:, m * CG + g, :], vmax[:, g, :], dtx[:, m * CG + g, :], ALU.add).then_inc(s_c2, 1)

                def times_b(s, m, k):
                    n, g = k // CG, k % CG
                    if k < CG:
                        pool.wait_ge(s_dtx, START + CG * s + k + 1)
                    pool.wait_ge(s_rows[0], START + NS * s + n + 1)
                    pool.wait_ge(s_scan, START + UNITS * s + k + 1 - R_U)
                    pool.tensor_tensor(u[:, k % R_U, :], dtx[:, m * CG + g, :], bb[:, n % R_B, :],
                                       ALU.mult).then_inc(s_u, 1)

                def stage(s, m, c, done):
                    for k in range(UNITS):
                        unit = ahead(s, m, k, LEAD_U)
                        if unit:
                            times_b(*unit)
                        if k - 1 in POOL_P[m]:
                            times_c(pool, s, m, k - 1)
                        if not is_last(s):
                            prepare(k, s + 1, 1 - m, c + m)
                        if m == 0 and not (isinstance(c, int) and c == NCH - 1):
                            norm(k, c + 1)

                def begin():
                    for k in range(LEAD_U):
                        times_b(0, 0, k)

                run(stage, norm, prepare, lambda: None, pool, begin)

            @block.tensor
            def _(pe):
                pe.wait_ge(s_w, START + 16 * NLOADS)
                pe.wait_ge(s_set, START + 4)

                def in_proj(m, part, g):
                    pe.matmul(ps[:, PREP0 + g, :], wi_a[:, m, part, g, :], xt_a[:, :], start=True, stop=False)
                    return pe.matmul(ps[:, PREP0 + g, :], wi_b[:, m, part, g, :], xt_b[:, :], start=False, stop=True)

                def norm(k, c):
                    if k == NORM + 19:
                        pe.wait_ge(s_gb, START + 2 * c + 2)
                        pe.wait_ge(s_max, START + NG * c)
                        for i in range(TT):
                            pe.transpose(ps[:, PREP0, i * P:(i + 1) * P], xs[:, i, 0:P], ident[:, :])
                            mm = pe.transpose(ps[0:CH - P, PREP0 + 1, i * P:(i + 1) * P], xs[:, i, P:CH], ident[:, :])
                        mm.then_inc(s_tr, 1)

                def prepare(k, r, m, c):
                    g = group_at(k, IN[m])
                    if g is not None:
                        if m == 0:
                            pe.wait_ge(s_xt, START + 2 * c + 2)
                        pe.wait_ge(s_max, START + CG * r)
                        in_proj(m, 0, g).then_inc(s_in, 1)
                    g = group_at(k, Z[m])
                    if g is not None:
                        if m:
                            pe.wait_ge(s_o, START + TT * c)
                        pe.wait_ge(s_raw, START + CG * r + g + 1)
                        pe.wait_ge(s_tap, START + CG * r + g + 1)
                        in_proj(m, 1, g).then_inc(s_z, 1)
                    if k == XPROJ[m]:
                        pe.wait_ge(s_xc, START + CG * r + CG)
                        pe.wait_ge(s_zs, START + CG * r + 1)
                        for g in range(CG):
                            mm = pe.matmul(ps[0:DTROW + RANK, PREP0, :], wx[:, m * CG + g, :], xc[:, m * CG + g, :],
                                           start=g == 0, stop=g == CG - 1)
                        mm.then_inc(s_xp, 1)
                    g = group_at(k, SOFT[m] - 2, 2)
                    if g is not None:
                        pe.wait_ge(s_hi, START + 2 * r + 2)
                        pe.wait_ge(s_zs, START + CG * r + CG)
                        if g == 2:
                            pe.wait_ge(s_res, START + r + 1)
                        pe.matmul(ps[:, PREP0 + (g + 1) % 3, :], wdt[DTROW:DTROW + RANK, m * CG + g, :],
                                  rest[DTROW:DTROW + RANK, :], start=True, stop=True).then_inc(s_dtp, 1)

                def row(s, m, k, is_c):
                    n = k // CG
                    if n == 0:
                        pe.wait_ge(s_lo, START + s + 1)
                        pe.wait_ge(s_mid, START + 2 * s + 2)
                    pe.wait_ge(s_rows[is_c], START + NS * s + n)
                    pe.matmul(ps[:, ROW0 + is_c, :], sel[0:DTROW, 2 * n + is_c, :], S[0:DTROW, m, :],
                              start=True, stop=True).then_inc(s_row[is_c], 1)

                def output(c, i):
                    if i == 0:
                        pe.wait_ge(s_yz, START + NG * (c + 1))
                    pe.wait_ge(s_max, START + NG * (c + 1))
                    if not (isinstance(c, int) and c == NCH - 1):
                        pe.wait_ge(s_raw, START + NG * (c + 2))
                        pe.wait_ge(s_tap, START + NG * (c + 2))
                    pe.wait_ge(s_o, START + TT * c + i - 2)
                    for g in range(NG):
                        mm = pe.matmul(ps[:, PREP0 + i % 3, 0:CH], yz[:, g, i * P:(i + 1) * P], wo[:, g, :],
                                       start=g == 0, stop=g == NG - 1)
                    mm.then_inc(s_op, 1)

                def add_y(s, m, k):
                    g = k % CG
                    by_pool = k in POOL_P[m]
                    pe.wait_ge(s_p[by_pool], START + products(s, m, k, by_pool))
                    pe.matmul(ps[:, Y0 + g, :], ident[:, :], p[:, k % R_P, :], start=False,
                              stop=k // CG == NS - 1).then_inc(s_y, 1)

                def stage(s, m, c, done):
                    for k in range(UNITS):
                        if k % CG < 2:
                            unit = ahead(s, m, k - k % CG, CG * ((R_C if k % CG else R_B) - 1))
                            if unit:
                                row(*unit, k % CG)
                        g = group_at(k, LAG_Y)
                        if g is not None:
                            if has_before(s):
                                pe.wait_ge(s_yz, START + CG * (s - 1) + g + 1)
                            pe.matmul(ps[:, Y0 + g, :], diag_d[:, m * CG + g, :], xc[:, m * CG + g, :],
                                      start=True, stop=False)
                        unit = behind(s, m, k, LAG_Y)
                        if unit:
                            add_y(*unit)
                        if not is_last(s):
                            prepare(k, s + 1, 1 - m, c + m)
                        if m == 0 and not (isinstance(c, int) and c == NCH - 1):
                            norm(k, c + 1)
                        if done is not None and k in range(OUT, OUT + 3 * TT, 3):
                            output(done, (k - OUT) // 3)
                    if is_last(s):
                        for k in range(UNITS - LAG_Y, UNITS):
                            add_y(s, m, k)

                def finish():
                    for i in range(TT):
                        output(NCH - 1, i)

                def begin():
                    for n in range(R_B - 1):
                        row(0, 0, CG * n, 0)
                        if n < R_C - 1:
                            row(0, 0, CG * n, 1)

                run(stage, norm, prepare, finish, pe, begin)

            @block.scalar
            def _(act):
                act.wait_ge(s_w, START + 16 * NLOADS)
                act.preload_act_table_set("natural_log_exp_and_others")
                act.activation(A[:, :, :], A[:, :, :], ACT.Exp).then_inc(s_set, 1)
                act.wait_ge(s_zero, START + 3)
                act.wait_ge(s_set, START + 4)

                def norm(k, c):
                    if k == NORM + 3:
                        act.wait_ge(s_ln, START + 8 * c + 3)
                        act.activation(vr[:, 1, :], vr[:, 0, :], ACT.Ln).then_inc(s_lr, 1)
                        act.wait_ge(s_lr, START + 2 * c + 1)
                        act.activation(vr[:, 1, :], vr[:, 1, :], ACT.Exp, scale=-0.5).then_inc(s_lr, 1)
                    if k == NORM + 21:
                        act.wait_ge(s_tr, START + c + 1)
                        act.wait_ge(s_z, START + NG * c)
                        act.activation(xt_a[:, :], ps[:, PREP0, :], ACT.Copy).then_inc(s_xt, 1)
                        act.activation(xt_b[:, :], ps[0:CH - P, PREP0 + 1, :], ACT.Copy).then_inc(s_xt, 1)

                def prepare(k, r, m, c):
                    g = group_at(k, IN[m] + 1)
                    if g is not None:
                        act.wait_ge(s_in, START + CG * r + g + 1)
                        act.wait_ge(s_conv, START + 5 * CG * r)
                        act.activation(raw[:, g, KCONV - 1:KCONV - 1 + T], ps[:, PREP0 + g, :],
                                       ACT.Copy).then_inc(s_raw, 1)
                        gg = m * CG + g
                        act.activation(xc[:, gg, :], ps[:, PREP0 + g, :], ACT.Identity, bias=b_conv[:, gg:gg + 1],
                                       scale=wc[:, gg, KCONV - 1:KCONV]).then_inc(s_tap, 1)
                    if k == SILU[m]:
                        for g in range(CG):
                            act.wait_ge(s_conv, START + 5 * (CG * r + g) + 4)
                            act.activation(xc[:, m * CG + g, :], xc[:, m * CG + g, :], ACT.Silu).then_inc(s_xc, 1)
                        for g in range(CG):
                            act.wait_ge(s_z, START + CG * r + g + 1)
                            act.wait_ge(s_yz, START + CG * (r - 1))
                            act.activation(zs[:, m * CG + g, :], ps[:, PREP0 + g, :], ACT.Silu).then_inc(s_zs, 1)
                        act.preload_act_table_set("natural_log_exp_and_others")
                    if k == XPROJ[m] + 1:
                        act.wait_ge(s_xp, START + r + 1)
                        act.activation(S[0:DTROW, m, :], ps[0:DTROW, PREP0, :], ACT.Copy).then_inc(s_hi, 1)
                        act.activation(rest[DTROW:DTROW + RANK, :], ps[DTROW:DTROW + RANK, PREP0, :],
                                       ACT.Copy).then_inc(s_hi, 1)
                    if k == SPLIT[m] + 1:
                        act.wait_ge(s_res, START + r + 1)
                        act.activation(midt[0:DTROW, :], rest[0:DTROW, :], ACT.Copy).then_inc(s_mid, 1)
                        act.wait_ge(s_mid, START + 2 * r + 1)
                        act.activation(S[32:64, m, :], midt[32:64, :], ACT.Copy).then_inc(s_mid, 1)
                    g = group_at(k, SOFT[m], APART[m])
                    if g is not None:
                        n, e, v = CG * r + g, dt[:, m * CG + g, :], ps[:, PREP0 + (g + 1) % 3, :]
                        b = bdt[:, m * CG + g:m * CG + g + 1]
                        act.wait_ge(s_dtp, START + n + 1)
                        act.activation(e, v, ACT.Abs, bias=b).then_inc(s_abs, 1)
                        act.wait_ge(s_c2, START + n - CG + 1)
                        act.activation(vmax[:, g, :], v, ACT.Relu, bias=b).then_inc(s_max, 1)
                        act.wait_ge(s_abs, START + n + 1)
                        act.activation(e, e, ACT.Exp, scale=-1.0).then_inc(s_e, 1)
                    g = group_at(k, SOFT[m] + 2, APART[m])
                    if g is not None:
                        n, w = CG * r + g, w1[:, g, :]
                        act.wait_ge(s_e, START + n + 1)
                        act.wait_ge(s_dt, START + n - CG + 1)
                        act.activation(w, dt[:, m * CG + g, :], ACT.Identity, bias=minus_one[:, :],
                                       scale=-1.0).then_inc(s_w1, 1)
                        act.wait_ge(s_w1, START + n + 1)
                        act.activation(lnw[:, g, :], w, ACT.Ln, scale=-1.0).then_inc(s_l, 1)

                def row_out(s, m, k, is_c):
                    n = k // CG
                    act.wait_ge(s_row[is_c], START + NS * s + n + 1)
                    if is_c:
                        end = k - CG * (R_C - 1) - 1
                        act.wait_ge(s_p[0], START + products(s, m, end, False))
                        if end > 0:
                            act.wait_ge(s_p[1], START + products(s, m, end, True))
                        act.activation(cb[:, n % R_C, :], ps[:, ROW0 + 1, :], ACT.Copy).then_inc(s_rows[1], 1)
                    else:
                        act.wait_ge(s_u, START + UNITS * s + k - CG * (R_B - 1))
                        act.activation(bb[:, n % R_B, :], ps[:, ROW0, :], ACT.Copy).then_inc(s_rows[0], 1)

                def decay(s, m, k):
                    n, g = k // CG, k % CG
                    if k < CG:
                        act.wait_ge(s_dt, START + CG * s + k + 1)
                    act.wait_ge(s_scan, START + UNITS * s + k + 1 - R_DA)
                    act.activation(dA[:, k % R_DA, :], dt[:, m * CG + g, :], ACT.Exp,
                                   scale=A[:, m * CG + g, n:n + 1]).then_inc(s_da, 1)

                def stage(s, m, c, done):
                    for k in range(UNITS):
                        unit = ahead(s, m, k, LEAD_A)
                        if unit:
                            decay(*unit)
                        if k % CG:
                            unit = ahead(s, m, k - k % CG, CG * ((R_C if k % CG == 2 else R_B) - 1))
                            if unit:
                                row_out(*unit, k % CG - 1)
                        if m == 0 and k == OUT + 11:
                            act.wait_ge(s_o, START + TT * c)
                            act.activation(resid[:, :, :], xs[:, :, :], ACT.Copy).then_inc(s_rs, 1)
                        if not is_last(s):
                            prepare(k, s + 1, 1 - m, c + m)
                        if m == 0 and not (isinstance(c, int) and c == NCH - 1):
                            norm(k, c + 1)
                def begin():
                    for n in range(R_B - 1):
                        row_out(0, 0, CG * n, 0)
                        if n < R_C - 1:
                            row_out(0, 0, CG * n, 1)
                    for k in range(LEAD_A):
                        decay(0, 0, k)

                run(stage, norm, prepare, lambda: None, act, begin)

            @block.vector
            def _(dve):
                dve.wait_ge(s_w, START + 16 * NLOADS)
                for i, src in enumerate((xc, dt)):
                    ins = dve.tensor_copy(sel[:, i * NS:(i + 1) * NS, :].rearrange("p i m -> p (i m)"),
                                          src[:, 0:4, :].rearrange("p g n -> p (g n)"))
                ins.then_inc(s_set, 1)
                for g in range(NG):
                    ins = dve.tensor_scalar(diag_d[:, g, :], ident[:, :], Dv[:, g:g + 1], None, ALU.mult)
                ins.then_inc(s_set, 1)
                dve.wait_ge(s_set, START + 3)
                dve.tensor_scalar(A[:, :, :], A[:, :, :], -1.0, None, ALU.mult).then_inc(s_set, 1)
                dve.wait_ge(s_zero, START + 2)

                def norm(k, c):
                    l = START + 8 * c
                    if k == NORM:
                        dve.wait_ge(s_tok, START + 16 * c + 16)
                        for i in range(TT):
                            ins = dve.bn_stats(stats[:, i, :], tok[:, i, :])
                        ins.then_inc(s_ln, 1)
                    if k == NORM + 1:
                        dve.wait_ge(s_ln, l + 1)
                        waits_passed(dve)
                        for i in range(TT):
                            ins = dve.bn_aggr(mv[:, i, :], stats[:, i, :])
                        ins.then_inc(s_ln, 1)
                        dve.wait_ge(s_ln, l + 2)
                        dve.tensor_scalar(vr[:, 0, :], mv[:, :, 1], LN1_EPS, None, ALU.add).then_inc(s_ln, 1)
                    if k == NORM + 7:
                        dve.wait_ge(s_lr, START + 2 * c + 2)
                        dve.tensor_tensor(vr[:, 2, :], vr[:, 0, :], vr[:, 1, :], ALU.mult).then_inc(s_ln, 1)
                        dve.wait_ge(s_ln, l + 4)
                        dve.tensor_tensor(vr[:, 2, :], vr[:, 2, :], vr[:, 1, :], ALU.mult).then_inc(s_ln, 1)
                        dve.wait_ge(s_ln, l + 5)
                        dve.tensor_scalar(vr[:, 2, :], vr[:, 2, :], -0.5, 1.5, ALU.mult, ALU.add).then_inc(s_ln, 1)
                        dve.wait_ge(s_ln, l + 6)
                        dve.tensor_tensor(vr[:, 1, :], vr[:, 2, :], vr[:, 1, :], ALU.mult).then_inc(s_ln, 1)
                    if k == NORM + 8:
                        dve.wait_ge(s_ln, l + 7)
                        dve.wait_ge(s_rs, START + c)
                        dve.wait_ge(s_tr, START + c)
                        for i in range(TT):
                            ins = dve.tensor_scalar(xs[:, i, :], tok[:, i, :], mv[:, i, 0:1], vr[:, 1, i:i + 1],
                                                    ALU.subtract, ALU.mult)
                        ins.then_inc(s_ln, 1)

                def prepare(k, r, m, c):
                    if k in (0, 5):
                        f = keep[:, c:c + 1] if isinstance(c, int) else keep[:, bass.ds(c, 1)]
                        left = halo[:, m * CG:(m + 1) * CG, :] if k == 0 else last[:, m, :]
                        if k == 5:
                            dve.wait_ge(s_last, START + NS * (r - 1))
                        dve.tensor_scalar(left, left, f, None, ALU.mult).then_inc(s_kp, 1)
                    if IN[m] + 2 <= k < IN[m] + 2 + 3 * CG:
                        g, part = (k - IN[m] - 2) // 3, (k - IN[m] - 2) % 3
                        n = START + 5 * (CG * r + g)
                        x_raw, x, gg = raw[:, g, :], xc[:, m * CG + g, :], m * CG + g

                        def tap(i):
                            dve.wait_ge(s_conv, n + i + 1)
                            dve.scalar_tensor_tensor(out=x, in0=x_raw[:, i:i + T], scalar=wc[:, gg, i:i + 1], in1=x,
                                                     op0=ALU.mult, op1=ALU.add).then_inc(s_conv, 1)

                        if part == 0:
                            dve.wait_ge(s_raw, START + CG * r + g + 1)
                            dve.wait_ge(s_kp, START + 2 * r + 1)
                            dve.tensor_copy(x_raw[:, 0:KCONV - 1], halo[:, gg, 0:KCONV - 1]).then_inc(s_conv, 1)
                            dve.wait_ge(s_tap, START + CG * r + g + 1)
                            tap(0)
                        elif part == 1:
                            tap(1)
                        else:
                            tap(2)
                            dve.tensor_copy(halo[:, gg, 0:KCONV - 1], x_raw[:, T:T + KCONV - 1]).then_inc(s_conv, 1)
                    if k == SPLIT[m]:
                        dve.wait_ge(s_hi, START + 2 * r + 2)
                        dve.tensor_tensor(rest[0:DTROW, :], ps[0:DTROW, PREP0, :], S[0:DTROW, m, :],
                                          ALU.subtract).then_inc(s_res, 1)
                    if k == SPLIT[m] + 3:
                        dve.wait_ge(s_mid, START + 2 * r + 1)
                        dve.wait_ge(s_res, START + r + 1)
                        dve.tensor_tensor(S[64:96, m, :], rest[64:96, :], midt[64:96, :],
                                          ALU.subtract).then_inc(s_lo, 1)
                    g = group_at(k, SOFT[m] + 4, APART[m])
                    if g is not None:
                        n = CG * r + g
                        dve.wait_ge(s_w1, START + n + 1)
                        dve.scalar_tensor_tensor(out=dtx[:, m * CG + g, :], in0=w1[:, g, :], scalar=1.0,
                                                 in1=dt[:, m * CG + g, :], op0=ALU.add,
                                                 op1=ALU.add).then_inc(s_c1, 1)
                    g = group_at(k, SOFT[m] + 7, APART[m])
                    if g is not None:
                        dve.wait_ge(s_dt, START + CG * r + g + 1)
                        dve.tensor_tensor(dtx[:, m * CG + g, :], dt[:, m * CG + g, :], xc[:, m * CG + g, :],
                                          ALU.mult).then_inc(s_dtx, 1)
                    g = group_at(k, SOFT[m] + 6, APART[m])
                    if g is not None:
                        n = CG * r + g
                        dve.wait_ge(s_l, START + n + 1)
                        dve.wait_ge(s_c2, START + n + 1)
                        dve.tensor_tensor(dt[:, m * CG + g, :], dtx[:, m * CG + g, :], lnw[:, g, :],
                                          ALU.add).then_inc(s_dt, 1)

                def gate(s, m, g):
                    gg = m * CG + g
                    dve.wait_ge(s_y, START + UNITS * (s + 1) - CG + g + 1)
                    dve.tensor_tensor(yz[:, gg, :], ps[:, Y0 + g, :], zs[:, gg, :], ALU.mult).then_inc(s_yz, 1)

                def output(c, i):
                    dve.wait_ge(s_op, START + TT * c + i + 1)
                    dve.wait_ge(s_rs, START + c + 1)
                    dve.wait_ge(s_st[i], START + 16 * c)
                    dve.tensor_tensor(o[:, i, :], ps[:, PREP0 + i % 3, 0:CH], resid[:, i, :],
                                      ALU.add).then_inc(s_o, 1)

                def keep_last(s, m, k):
                    dve.wait_ge(s_scan, START + UNITS * s + k + CG)
                    dve.tensor_copy(last[:, m, k:k + CG], h[:, k % R_H:k % R_H + CG, T - 1]).then_inc(s_last, 1)

                def stage(s, m, c, done):
                    um = UNITS * s

                    for k in range(UNITS):
                        n, g = k // CG, k % CG
                        if k == 0:
                            dve.wait_ge(s_kp, START + 2 * s + 2)
                        dve.wait_ge(s_da, START + um + k + 1)
                        dve.wait_ge(s_u, START + um + k + 1)
                        dve.wait_ge(s_last, START + NS * s + (k - R_H) // CG + 1)
                        if k - R_H in POOL_P[m]:
                            dve.wait_ge(s_p[1], START + products(s, m, k - R_H, True))
                        dve.tensor_tensor_scan(h[:, k % R_H, :], dA[:, k % R_DA, :], u[:, k % R_U, :],
                                               last[:, m, k:k + 1], ALU.mult, ALU.add).then_inc(s_scan, 1)
                        unit = behind(s, m, k, CG)
                        if k % CG == 0 and unit:
                            keep_last(*unit)
                        if k and k - 1 not in POOL_P[m]:
                            times_c(dve, s, m, k - 1)
                        g = group_at(k, GATE)
                        if g is not None and has_before(s):
                            gate(s - 1, 1 - m, g)
                        if done is not None and k - 1 in range(OUT, OUT + 3 * TT, 3):
                            output(done, (k - 1 - OUT) // 3)
                        if not is_last(s):
                            prepare(k, s + 1, 1 - m, c + m)
                        if m == 0 and not (isinstance(c, int) and c == NCH - 1):
                            norm(k, c + 1)
                    times_c(dve, s, m, UNITS - 1)

                def finish():
                    for g in range(CG):
                        gate(2 * NCH - 1, 1, g)
                    for i in range(TT):
                        output(NCH - 1, i)

                run(stage, norm, prepare, finish, dve)


def layer1_inputs(v):
    import numpy as np
    T = np.ascontiguousarray
    w = lambda m, n: v[f"L1_conv_m{m}_{n}"]
    wi = np.concatenate([w(1, "in_w").T, w(2, "in_w").T[::-1]], 1)
    col = lambda n: T(np.concatenate([w(1, n), w(2, n)]).reshape(2 * CG, P).T)
    xw = [np.concatenate([w(m, "x_w").T[:, 12:]] * 3 + [w(m, "x_w").T[:, :12]], 1) for m in (1, 2)]
    both = lambda n: T(np.concatenate([w(1, n), w(2, n)]))
    sel = np.zeros((P, 32, P), np.float32)
    for i in range(32):
        for part in range(3):
            sel[32 * part + 16 * (i % 2) + i // 2, i, :] = 1.0
    keep = np.ones((P, PIX // BANK * v["x"].shape[0]), np.float32)
    keep[:, ::PIX // BANK] = 0.0
    return {
        "wi": T(wi), "wc": both("conv_w"), "bc": col("conv_b"), "wx": T(np.concatenate(xw)),
        "wdt": T(np.concatenate([w(1, "dt_w").T, w(2, "dt_w").T], 1)), "bdt": col("dt_b"),
        "A_log": both("A_log"), "D": col("D"), "wo": T(np.concatenate([w(1, "out_w").T, w(2, "out_w").T])),
        "ln_g": T(np.tile(v["L1_conv_ln_g"], (P, 1))), "ln_b": T(np.tile(v["L1_conv_ln_b"], (P, 1))),
        "keep": keep, "ident": np.eye(P, dtype=np.float32), "sel": sel.reshape(P, 32 * P),
    }


def program(nc, B, io):
    mid = nc.dram_tensor("mid_dram", [B, CH, PIX], F32, kind="Internal").ap()
    layer0(nc, B, io["layer0"], mid)
    layer1(nc, B, io["layer1"], mid, io["out"])


def kernel(**inputs):
    import numpy as _np
    import concourse.bacc as _bacc
    from concourse import mybir as _mybir
    from concourse.bass_utils import run_bass_kernel_spmd as _run

    nc = _bacc.Bacc("TRN2", target_bir_lowering=False, num_devices=1)
    v = {k: _np.asarray(a) for k, a in inputs.items()}
    B = v["x"].shape[0]
    arrays, io = {}, {}
    for layer, made in (("layer0", layer0_inputs(v)), ("layer1", layer1_inputs(v))):
        io[layer] = {}
        for name, a in made.items():
            full = f"{layer}_{name}_dram"
            arrays[full] = a
            io[layer][name] = nc.dram_tensor(full, list(a.shape), _mybir.dt.from_np(a.dtype), kind="ExternalInput").ap()
    io["out"] = nc.dram_tensor("out_dram", [B, CH, PIX], F32, kind="ExternalOutput").ap()
    program(nc, B, io)
    r = _run(nc, [arrays], core_ids=[0])
    return r.results[0]["out_dram"].reshape(v["x"].shape)
```
